# Optimizing a Trainium2 kernel written in Bass

```python
import numpy as np
import jax
import jax.numpy as jnp

def _softmax(x, axis=-1):
    return jax.nn.softmax(x, axis=axis)

def _gelu(x):
    return jax.nn.gelu(x, approximate=True)

def _silu(x):
    return jax.nn.silu(x)

def _sigmoid(x):
    return jax.nn.sigmoid(x)

def _layernorm(x, axis=-1, eps=1e-05):
    m = jnp.mean(x, axis=axis, keepdims=True)
    v = jnp.var(x, axis=axis, keepdims=True)
    return (x - m) / jnp.sqrt(v + eps)

def _scatter_add(tgt, idx, src, axis=0):
    return tgt.at[idx].add(src)

def _segment_sum(src, seg, n):
    return jax.ops.segment_sum(src, seg, n)
kernel_name = 'mk_flamingo_gated_d4_seqx_r8_3a62a4'

def setup_inputs(seed: int=0):
    np.random.seed(seed)
    _w = jnp.asarray

    def _rec_inputs():
        import jax
        import jax.numpy as jnp
        _rk = jax.random.key(seed)
        x = 7.22e-05 + 1 * jax.random.normal(jax.random.fold_in(_rk, 1), (16, 128, 256), jnp.float32)
        _lenS = 128 - jax.random.randint(jax.random.fold_in(_rk, 7), (16,), 0, max(1, 128 // 4) + 1, jnp.int32)
        _lenS2 = 128 - jax.random.randint(jax.random.fold_in(_rk, 8), (16,), 0, max(1, 128 // 4) + 1, jnp.int32)
        _ctx_2048P = jax.random.normal(jax.random.fold_in(_rk, 11), (16, 16, 256), jnp.float32)
        _ctx_2048c = jax.random.dirichlet(jax.random.fold_in(_rk, 511), 0.3 * jnp.ones((16,), jnp.float32), (16, 128))
        _ctx_2048t = jnp.einsum('bsk,bkd->bsd', _ctx_2048c, _ctx_2048P)
        _ctx_2048t = _ctx_2048t * jax.lax.rsqrt(jnp.mean(jnp.square(_ctx_2048t)) + 1e-12) * 0.953939
        ctx_2048 = 4.13588e-05 + 0.999923 * (_ctx_2048t + 0.3 * jax.random.normal(jax.random.fold_in(_rk, 611), (16, 128, 256), jnp.float32))
        _validS = jnp.arange(128)[None, :] < _lenS[:, None]
        _validS2 = jnp.arange(128)[None, :] < _lenS2[:, None]
        _causal = jnp.tril(jnp.ones((128, 128), dtype=bool))
        mask_Bx1xSxS_fk0 = jnp.where(jnp.broadcast_to(_validS[:, None, None, :], (16, 1, 128, 128)), -1000000000.0, 0.0).astype(jnp.float32)
        mask_BxS2_ik0 = jnp.where(jnp.broadcast_to(_validS2[:, :], (16, 128)), 0, 1).astype(jnp.int32)
        _g = jax.random.normal(jax.random.fold_in(_rk, 9001), (2, 4), jnp.float32)
        _g = jnp.sign(_g) * jnp.maximum(jnp.abs(_g), 1.0) + (_g == 0) * 1.0
        g_xattn = _g[0]
        g_ffn = _g[1]
        return (x, ctx_2048, mask_Bx1xSxS_fk0, mask_BxS2_ik0, g_xattn, g_ffn)
    x, ctx_2048, mask_Bx1xSxS_fk0, mask_BxS2_ik0, g_xattn, g_ffn = _rec_inputs()

    def _L0_xattn_setup():
        import jax, jax.numpy as jnp
        import numpy as np
        N_HEADS = 16
        N_KV_HEADS = 4

        def _rope_cos_sin(T, d, dtype):
            inv_freq = 1.0 / 10000.0 ** (jnp.arange(0, d, 2, dtype=dtype) / d)
            t = jnp.arange(T, dtype=dtype)
            freqs = jnp.einsum('i,j->ij', t, inv_freq)
            emb = jnp.concatenate([freqs, freqs], axis=-1)
            return (jnp.cos(emb), jnp.sin(emb))

        def _rotate_half(x):
            h = x.shape[-1] // 2
            return jnp.concatenate([-x[..., h:], x[..., :h]], axis=-1)
        key = jax.random.key(seed)
        ks = jax.random.split(key, 12)
        B, C, T = (4, 128, 256)
        d = C // N_HEADS
        kv_dim = d * N_KV_HEADS
        out_ch = C

        def xavier(k, shape):
            fan_out, fan_in = shape
            lim = np.sqrt(6.0 / (fan_in + fan_out))
            return jax.random.uniform(k, shape, jnp.float32, -lim, lim)
        return {'query': jax.random.normal(ks[0], (B, C, T), jnp.float32), 'key_value': jax.random.normal(ks[1], (B, C, T), jnp.float32), 'Wq': xavier(ks[2], (C, C)), 'bq': jnp.zeros((C,), jnp.float32), 'Wk': xavier(ks[3], (kv_dim, C)), 'bk': jnp.zeros((kv_dim,), jnp.float32), 'Wv': xavier(ks[4], (kv_dim, C)), 'bv': jnp.zeros((kv_dim,), jnp.float32), 'Wo': xavier(ks[5], (out_ch, C)), 'bo': jax.random.normal(ks[6], (out_ch,), jnp.float32) * 0.02}
    _L0_xattn_all = _L0_xattn_setup()
    _L0_xattn_in = {k: v for k, v in _L0_xattn_all.items() if k in ('Wq', 'bq', 'Wk', 'bk', 'Wv', 'bv', 'Wo', 'bo')}
    del _L0_xattn_all

    def _L0_ffn_setup():
        import jax, jax.numpy as jnp
        import numpy as np
        B, T, C = (2, 128, 256)
        E, TOPK = (8, 2)
        F_MOE = 176
        F_SHARED = 704
        key = jax.random.key(seed)
        ks = jax.random.split(key, 9)
        s = 0.02
        return {'x': jax.random.normal(ks[0], (B, T, C), dtype=jnp.float32), 'gate_w': jax.random.normal(ks[1], (E, C), dtype=jnp.float32) * s, 'expert_fc1': jax.random.normal(ks[2], (E, F_MOE, C), dtype=jnp.float32) * s, 'expert_fc2': jax.random.normal(ks[3], (E, F_MOE, C), dtype=jnp.float32) * s, 'expert_proj': jax.random.normal(ks[4], (E, C, F_MOE), dtype=jnp.float32) * s, 'shared_fc1': jax.random.normal(ks[5], (F_SHARED, C), dtype=jnp.float32) * s, 'shared_fc2': jax.random.normal(ks[6], (F_SHARED, C), dtype=jnp.float32) * s, 'shared_proj': jax.random.normal(ks[7], (C, F_SHARED), dtype=jnp.float32) * s, 'shared_gate_w': jax.random.normal(ks[8], (1, C), dtype=jnp.float32) * s}
    _L0_ffn_all = _L0_ffn_setup()
    _L0_ffn_in = {k: v for k, v in _L0_ffn_all.items() if k in ('gate_w', 'expert_fc1', 'expert_fc2', 'expert_proj', 'shared_fc1', 'shared_fc2', 'shared_proj', 'shared_gate_w')}
    del _L0_ffn_all

    def _L1_xattn_setup():
        import jax, jax.numpy as jnp
        import numpy as np
        import math
        B, S, HID, H = (2, 256, 256, 32)
        D = HID // H
        AL = 10

        def _rope_tables(seq_len, dim, dtype):
            inv_freq = 1.0 / 10000.0 ** (np.arange(0, dim, 2, dtype=np.float32) / dim)
            t = np.arange(seq_len, dtype=np.float32)
            freqs = np.outer(t, inv_freq)
            emb = np.concatenate([freqs, freqs], -1)
            return (jnp.asarray(np.cos(emb), dtype), jnp.asarray(np.sin(emb), dtype))

        def _rotate_half(x):
            x1, x2 = jnp.split(x, 2, axis=-1)
            return jnp.concatenate([-x2, x1], axis=-1)
        key = jax.random.key(seed)
        ks = jax.random.split(key, 8)
        hidden_states = jax.random.normal(ks[0], (B, S, HID), dtype=jnp.float32)
        adapter = jax.random.normal(ks[1], (B, AL, HID), dtype=jnp.float32)
        causal = jnp.tril(jnp.ones((S, S), dtype=bool))
        attention_mask = jnp.broadcast_to(jnp.where(causal, 0.0, -1000000000.0).astype(jnp.float32)[None, None], (B, 1, S, S))
        scale = 0.02
        Wq = jax.random.normal(ks[2], (HID, HID), dtype=jnp.float32) * scale
        Wk = jax.random.normal(ks[3], (HID, HID), dtype=jnp.float32) * scale
        Wv = jax.random.normal(ks[4], (HID, HID), dtype=jnp.float32) * scale
        Wo = jax.random.normal(ks[5], (HID, HID), dtype=jnp.float32) * scale
        gate = jax.random.normal(ks[6], (1, H, 1, 1), dtype=jnp.float32) * 0.1
        return {'hidden_states': hidden_states, 'attention_mask': attention_mask, 'adapter': adapter, 'Wq': Wq, 'Wk': Wk, 'Wv': Wv, 'Wo': Wo, 'gate': gate}
    _L1_xattn_all = _L1_xattn_setup()
    _L1_xattn_in = {k: v for k, v in _L1_xattn_all.items() if k in ('Wq', 'Wk', 'Wv', 'Wo', 'gate')}
    del _L1_xattn_all

    def _L1_ffn_setup():
        import jax, jax.numpy as jnp
        import numpy as np
        NUM_EXPERTS = 4
        key = jax.random.key(seed)
        k1, k2, k3 = jax.random.split(key, 3)
        B, N, H = (8, 256, 256)
        E = NUM_EXPERTS
        I = H * 4 // E
        x = jax.random.normal(k1, (B, N, H), dtype=jnp.float32)
        gate_up_proj = jax.random.normal(k2, (E, H, 2 * I), dtype=jnp.float32) * 0.02
        down_proj = jax.random.normal(k3, (E, I, H), dtype=jnp.float32) * 0.02
        return {'x': x, 'gate_up_proj': gate_up_proj, 'down_proj': down_proj}
    _L1_ffn_all = _L1_ffn_setup()
    _L1_ffn_in = {k: v for k, v in _L1_ffn_all.items() if k in ('gate_up_proj', 'down_proj')}
    del _L1_ffn_all

    def _L2_xattn_setup():
        import jax, jax.numpy as jnp
        import numpy as np
        import math
        H = 256
        NH = 16
        HD = H // NH
        EPS_LN = 1e-05
        RES_SCALE_MAX = 0.3

        def _nan_clean(x, lim=10000.0):
            return jnp.nan_to_num(x, nan=0.0, posinf=lim, neginf=-lim)
        key = jax.random.key(seed)
        ks = jax.random.split(key, 12)
        B, S, T = (4, 256, 32)
        std = 1.0 / math.sqrt(H)
        return {'hidden_states': jax.random.normal(ks[0], (B, S, H), jnp.float32), 'audio_tokens': jax.random.normal(ks[1], (B, T, H), jnp.float32), 'attention_mask': jax.random.randint(ks[2], (B, T), 0, 2, jnp.int32), 'Wq': jax.random.normal(ks[3], (H, H), jnp.float32) * std, 'bq': jnp.zeros((H,), jnp.float32), 'Wk': jax.random.normal(ks[4], (H, H), jnp.float32) * std, 'bk': jnp.zeros((H,), jnp.float32), 'Wv': jax.random.normal(ks[5], (H, H), jnp.float32) * std, 'bv': jnp.zeros((H,), jnp.float32), 'Wo': jax.random.normal(ks[6], (H, H), jnp.float32) * std, 'bo': jnp.zeros((H,), jnp.float32), 'ln_gamma': jnp.ones((H,), jnp.float32), 'ln_beta': jnp.zeros((H,), jnp.float32), 'residual_scale': jnp.float32(0.05)}
    _L2_xattn_all = _L2_xattn_setup()
    _L2_xattn_in = {k: v for k, v in _L2_xattn_all.items() if k in ('Wq', 'bq', 'Wk', 'bk', 'Wv', 'bv', 'Wo', 'bo', 'ln_gamma', 'ln_beta', 'residual_scale')}
    del _L2_xattn_all

    def _L2_ffn_setup():
        import jax, jax.numpy as jnp
        import numpy as np
        EPS = 1e-05

        def weight_quant(w):
            scale = 1.0 / jnp.clip(jnp.mean(jnp.abs(w)), EPS, None)
            return jnp.clip(jnp.round(w * scale), -1.0, 1.0) / scale

        def act_quant(x):
            scale = 127.0 / jnp.clip(jnp.max(jnp.abs(x), axis=-1, keepdims=True), EPS, None)
            return jnp.clip(jnp.round(x * scale), -128.0, 127.0) / scale

        def bitlinear(x, w):
            return jnp.einsum('bsd,od->bso', act_quant(x), weight_quant(w))
        key = jax.random.key(seed)
        k1, k2, k3, k4 = jax.random.split(key, 4)
        B, S, D = (4, 256, 256)
        I = int(np.ceil(D * np.pi / 64) * 64)
        x = jax.random.normal(k1, (B, S, D), dtype=jnp.float32)
        w_gate = jax.random.normal(k2, (I, D), dtype=jnp.float32) * 0.02
        w_up = jax.random.normal(k3, (I, D), dtype=jnp.float32) * 0.02
        w_down = jax.random.normal(k4, (D, I), dtype=jnp.float32) * 0.02
        return {'x': x, 'w_gate': w_gate, 'w_up': w_up, 'w_down': w_down}
    _L2_ffn_all = _L2_ffn_setup()
    _L2_ffn_in = {k: v for k, v in _L2_ffn_all.items() if k in ('w_gate', 'w_up', 'w_down')}
    del _L2_ffn_all

    def _L3_xattn_setup():
        import jax, jax.numpy as jnp
        import numpy as np
        HIDDEN = 256
        N_HEADS = 16
        N_KV_HEADS = 4
        HEAD_DIM = 128
        EPS = 1e-06

        def rms_norm(x, w, eps=EPS):
            xf = x.astype(jnp.float32)
            var = jnp.mean(xf * xf, axis=-1, keepdims=True)
            return w * (xf * jax.lax.rsqrt(var + eps)).astype(x.dtype)
        key = jax.random.key(seed)
        ks = jax.random.split(key, 8)
        B, S, S_ENC = (4, 256, 128)
        inner = N_HEADS * HEAD_DIM
        kv_dim = N_KV_HEADS * HEAD_DIM
        s = 0.02
        return {'hidden_states': jax.random.normal(ks[0], (B, S, HIDDEN), jnp.float32), 'encoder_hidden_states': jax.random.normal(ks[1], (B, S_ENC, HIDDEN), jnp.float32), 'Wq': jax.random.normal(ks[2], (HIDDEN, inner), jnp.float32) * s, 'Wk': jax.random.normal(ks[3], (HIDDEN, kv_dim), jnp.float32) * s, 'Wv': jax.random.normal(ks[4], (HIDDEN, kv_dim), jnp.float32) * s, 'Wo': jax.random.normal(ks[5], (inner, HIDDEN), jnp.float32) * s, 'q_norm_w': jnp.ones((HEAD_DIM,), jnp.float32), 'k_norm_w': jnp.ones((HEAD_DIM,), jnp.float32)}
    _L3_xattn_all = _L3_xattn_setup()
    _L3_xattn_in = {k: v for k, v in _L3_xattn_all.items() if k in ('Wq', 'Wk', 'Wv', 'Wo', 'q_norm_w', 'k_norm_w')}
    del _L3_xattn_all

    def _L3_ffn_setup():
        import jax, jax.numpy as jnp
        import numpy as np
        E = 64
        K = 6
        CAP = 64
        SCALE = 1.0
        H = 256
        I = 96
        SI = I * 2
        B, S = (2, 128)

        def _moe(x, gate_w, gate_up_proj, down_proj, shared_gate_w, shared_up_w, shared_down_w):
            b, s, h = x.shape
            T = b * s
            xf = x.reshape(T, h)
            scores = jax.nn.softmax(xf @ gate_w.T, axis=-1)
            topk_w, topk_idx = jax.lax.top_k(scores, K)
            topk_w = topk_w * SCALE
            flat_e = topk_idx.reshape(-1)
            order = jnp.argsort(flat_e)
            sorted_e = flat_e[order]
            sorted_tok = (order // K).astype(jnp.int32)
            sorted_w = topk_w.reshape(-1)[order]
            counts = jnp.zeros((E,), jnp.int32).at[flat_e].add(1)
            offsets = jnp.cumsum(counts) - counts
            pos = jnp.arange(T * K, dtype=jnp.int32) - offsets[sorted_e]
            buf_tok = jnp.full((E, CAP), T, jnp.int32).at[sorted_e, pos].set(sorted_tok, mode='drop')
            buf_w = jnp.zeros((E, CAP), x.dtype).at[sorted_e, pos].set(sorted_w, mode='drop')
            xp = jnp.concatenate([xf, jnp.zeros((1, h), x.dtype)], axis=0)
            gx = xp[buf_tok]
            gu = jnp.einsum('ech,ehi->eci', gx, gate_up_proj)
            g, u = jnp.split(gu, 2, axis=-1)
            hid = jax.nn.silu(g) * u
            eo = jnp.einsum('eci,eih->ech', hid, down_proj) * buf_w[..., None]
            routed = jnp.zeros((T + 1, h), x.dtype).at[buf_tok.reshape(-1)].add(eo.reshape(-1, h))[:T]
            shared = jax.nn.silu(xf @ shared_gate_w.T) * (xf @ shared_up_w.T) @ shared_down_w.T
            return (routed + shared).reshape(b, s, h)
        key = jax.random.key(seed)
        ks = jax.random.split(key, 7)
        x = jax.random.normal(ks[0], (B, S, H), jnp.float32)
        gate_w = jax.random.normal(ks[1], (E, H), jnp.float32) * 0.02
        gate_up_proj = jax.random.normal(ks[2], (E, H, 2 * I), jnp.float32) * 0.02
        down_proj = jax.random.normal(ks[3], (E, I, H), jnp.float32) * 0.02
        shared_gate_w = jax.random.normal(ks[4], (SI, H), jnp.float32) * 0.02
        shared_up_w = jax.random.normal(ks[5], (SI, H), jnp.float32) * 0.02
        shared_down_w = jax.random.normal(ks[6], (H, SI), jnp.float32) * 0.02
        return dict(x=x, gate_w=gate_w, gate_up_proj=gate_up_proj, down_proj=down_proj, shared_gate_w=shared_gate_w, shared_up_w=shared_up_w, shared_down_w=shared_down_w)
    _L3_ffn_all = _L3_ffn_setup()
    _L3_ffn_in = {k: v for k, v in _L3_ffn_all.items() if k in ('gate_w', 'gate_up_proj', 'down_proj', 'shared_gate_w', 'shared_up_w', 'shared_down_w')}
    del _L3_ffn_all
    return {'x': x, 'ctx_2048': ctx_2048, 'mask_Bx1xSxS_fk0': mask_Bx1xSxS_fk0, 'mask_BxS2_ik0': mask_BxS2_ik0, 'g_xattn': g_xattn, 'g_ffn': g_ffn, 'L0_xattn_Wq': _L0_xattn_in['Wq'], 'L0_xattn_bq': _L0_xattn_in['bq'], 'L0_xattn_Wk': _L0_xattn_in['Wk'], 'L0_xattn_bk': _L0_xattn_in['bk'], 'L0_xattn_Wv': _L0_xattn_in['Wv'], 'L0_xattn_bv': _L0_xattn_in['bv'], 'L0_xattn_Wo': _L0_xattn_in['Wo'], 'L0_xattn_bo': _L0_xattn_in['bo'], 'L0_ffn_gate_w': _L0_ffn_in['gate_w'], 'L0_ffn_expert_fc1': _L0_ffn_in['expert_fc1'], 'L0_ffn_expert_fc2': _L0_ffn_in['expert_fc2'], 'L0_ffn_expert_proj': _L0_ffn_in['expert_proj'], 'L0_ffn_shared_fc1': _L0_ffn_in['shared_fc1'], 'L0_ffn_shared_fc2': _L0_ffn_in['shared_fc2'], 'L0_ffn_shared_proj': _L0_ffn_in['shared_proj'], 'L0_ffn_shared_gate_w': _L0_ffn_in['shared_gate_w'], 'L1_xattn_Wq': _L1_xattn_in['Wq'], 'L1_xattn_Wk': _L1_xattn_in['Wk'], 'L1_xattn_Wv': _L1_xattn_in['Wv'], 'L1_xattn_Wo': _L1_xattn_in['Wo'], 'L1_xattn_gate': _L1_xattn_in['gate'], 'L1_ffn_gate_up_proj': _L1_ffn_in['gate_up_proj'], 'L1_ffn_down_proj': _L1_ffn_in['down_proj'], 'L2_xattn_Wq': _L2_xattn_in['Wq'], 'L2_xattn_bq': _L2_xattn_in['bq'], 'L2_xattn_Wk': _L2_xattn_in['Wk'], 'L2_xattn_bk': _L2_xattn_in['bk'], 'L2_xattn_Wv': _L2_xattn_in['Wv'], 'L2_xattn_bv': _L2_xattn_in['bv'], 'L2_xattn_Wo': _L2_xattn_in['Wo'], 'L2_xattn_bo': _L2_xattn_in['bo'], 'L2_xattn_ln_gamma': _L2_xattn_in['ln_gamma'], 'L2_xattn_ln_beta': _L2_xattn_in['ln_beta'], 'L2_xattn_residual_scale': _L2_xattn_in['residual_scale'], 'L2_ffn_w_gate': _L2_ffn_in['w_gate'], 'L2_ffn_w_up': _L2_ffn_in['w_up'], 'L2_ffn_w_down': _L2_ffn_in['w_down'], 'L3_xattn_Wq': _L3_xattn_in['Wq'], 'L3_xattn_Wk': _L3_xattn_in['Wk'], 'L3_xattn_Wv': _L3_xattn_in['Wv'], 'L3_xattn_Wo': _L3_xattn_in['Wo'], 'L3_xattn_q_norm_w': _L3_xattn_in['q_norm_w'], 'L3_xattn_k_norm_w': _L3_xattn_in['k_norm_w'], 'L3_ffn_gate_w': _L3_ffn_in['gate_w'], 'L3_ffn_gate_up_proj': _L3_ffn_in['gate_up_proj'], 'L3_ffn_down_proj': _L3_ffn_in['down_proj'], 'L3_ffn_shared_gate_w': _L3_ffn_in['shared_gate_w'], 'L3_ffn_shared_up_w': _L3_ffn_in['shared_up_w'], 'L3_ffn_shared_down_w': _L3_ffn_in['shared_down_w']}

def reference(x, ctx_2048, mask_Bx1xSxS_fk0, mask_BxS2_ik0, g_xattn, g_ffn, L0_xattn_Wq, L0_xattn_bq, L0_xattn_Wk, L0_xattn_bk, L0_xattn_Wv, L0_xattn_bv, L0_xattn_Wo, L0_xattn_bo, L0_ffn_gate_w, L0_ffn_expert_fc1, L0_ffn_expert_fc2, L0_ffn_expert_proj, L0_ffn_shared_fc1, L0_ffn_shared_fc2, L0_ffn_shared_proj, L0_ffn_shared_gate_w, L1_xattn_Wq, L1_xattn_Wk, L1_xattn_Wv, L1_xattn_Wo, L1_xattn_gate, L1_ffn_gate_up_proj, L1_ffn_down_proj, L2_xattn_Wq, L2_xattn_bq, L2_xattn_Wk, L2_xattn_bk, L2_xattn_Wv, L2_xattn_bv, L2_xattn_Wo, L2_xattn_bo, L2_xattn_ln_gamma, L2_xattn_ln_beta, L2_xattn_residual_scale, L2_ffn_w_gate, L2_ffn_w_up, L2_ffn_w_down, L3_xattn_Wq, L3_xattn_Wk, L3_xattn_Wv, L3_xattn_Wo, L3_xattn_q_norm_w, L3_xattn_k_norm_w, L3_ffn_gate_w, L3_ffn_gate_up_proj, L3_ffn_down_proj, L3_ffn_shared_gate_w, L3_ffn_shared_up_w, L3_ffn_shared_down_w):
    import jax
    import jax.numpy as jnp

    def _L0_xattn_ref(query, key_value, Wq, bq, Wk, bk, Wv, bv, Wo, bo):
        import jax, jax.numpy as jnp
        import numpy as np
        N_HEADS = 16
        N_KV_HEADS = 4

        def _rope_cos_sin(T, d, dtype):
            inv_freq = 1.0 / 10000.0 ** (jnp.arange(0, d, 2, dtype=dtype) / d)
            t = jnp.arange(T, dtype=dtype)
            freqs = jnp.einsum('i,j->ij', t, inv_freq)
            emb = jnp.concatenate([freqs, freqs], axis=-1)
            return (jnp.cos(emb), jnp.sin(emb))

        def _rotate_half(x):
            h = x.shape[-1] // 2
            return jnp.concatenate([-x[..., h:], x[..., :h]], axis=-1)
        B, C, T = query.shape
        Hq, Hkv = (N_HEADS, N_KV_HEADS)
        d = C // Hq
        q = jnp.einsum('oc,bct->bot', Wq, query) + bq[None, :, None]
        k = jnp.einsum('oc,bct->bot', Wk, key_value) + bk[None, :, None]
        v = jnp.einsum('oc,bct->bot', Wv, key_value) + bv[None, :, None]
        q = q.reshape(B, Hq, d, T).transpose(0, 1, 3, 2)
        k = k.reshape(B, Hkv, d, T).transpose(0, 1, 3, 2)
        v = v.reshape(B, Hkv, d, T).transpose(0, 1, 3, 2)
        cos, sin = _rope_cos_sin(T, d, q.dtype)
        cos, sin = (cos[None, None], sin[None, None])
        q = q * cos + _rotate_half(q) * sin
        k = k * cos + _rotate_half(k) * sin
        rep = Hq // Hkv
        k = jnp.repeat(k, rep, axis=1)
        v = jnp.repeat(v, rep, axis=1)
        scale = 1.0 / jnp.sqrt(jnp.asarray(d, q.dtype))
        scores = jnp.einsum('bhqd,bhkd->bhqk', q, k) * scale
        attn = jax.nn.softmax(scores, axis=-1)
        out = jnp.einsum('bhqk,bhkd->bhqd', attn, v)
        out = out.transpose(0, 1, 3, 2).reshape(B, C, T)
        out = jnp.einsum('oc,bct->bot', Wo, out) + bo[None, :, None]
        return out

    def _L0_ffn_ref(x, gate_w, expert_fc1, expert_fc2, expert_proj, shared_fc1, shared_fc2, shared_proj, shared_gate_w):
        import jax, jax.numpy as jnp
        import numpy as np
        B, T, C = (2, 128, 256)
        E, TOPK = (8, 2)
        F_MOE = 176
        F_SHARED = 704
        b, t, c = x.shape
        xf = x.reshape(-1, c)
        n = xf.shape[0]
        router = xf @ gate_w.T
        probs = jax.nn.softmax(router.astype(jnp.float32), axis=1).astype(x.dtype)
        top_p, top_i = jax.lax.top_k(probs, TOPK)
        combine = jnp.zeros((n, E), dtype=x.dtype).at[jnp.arange(n)[:, None], top_i].set(top_p)
        h1 = jnp.einsum('nc,efc->enf', xf, expert_fc1)
        h2 = jnp.einsum('nc,efc->enf', xf, expert_fc2)
        h = jax.nn.silu(h1) * h2
        out_e = jnp.einsum('enf,ecf->enc', h, expert_proj)
        y = jnp.einsum('ne,enc->nc', combine, out_e)
        s1 = xf @ shared_fc1.T
        s2 = xf @ shared_fc2.T
        shared = jax.nn.silu(s1) * s2 @ shared_proj.T
        y = y + jax.nn.sigmoid(xf @ shared_gate_w.T) * shared
        return y.reshape(b, t, c)

    def _L1_xattn_ref(hidden_states, attention_mask, adapter, Wq, Wk, Wv, Wo, gate):
        import jax, jax.numpy as jnp
        import numpy as np
        import math
        B, S, HID, H = (2, 256, 256, 32)
        D = HID // H
        AL = 10

        def _rope_tables(seq_len, dim, dtype):
            inv_freq = 1.0 / 10000.0 ** (np.arange(0, dim, 2, dtype=np.float32) / dim)
            t = np.arange(seq_len, dtype=np.float32)
            freqs = np.outer(t, inv_freq)
            emb = np.concatenate([freqs, freqs], -1)
            return (jnp.asarray(np.cos(emb), dtype), jnp.asarray(np.sin(emb), dtype))

        def _rotate_half(x):
            x1, x2 = jnp.split(x, 2, axis=-1)
            return jnp.concatenate([-x2, x1], axis=-1)
        bsz, q_len, hid = hidden_states.shape
        n_heads = gate.shape[1]
        head_dim = hid // n_heads
        inv_sqrt_d = 1.0 / math.sqrt(head_dim)

        def split_heads(x, length):
            return x.reshape(bsz, length, n_heads, head_dim).transpose(0, 2, 1, 3)
        q = split_heads(hidden_states @ Wq, q_len)
        k = split_heads(hidden_states @ Wk, q_len)
        v = split_heads(hidden_states @ Wv, q_len)
        cos, sin = _rope_tables(q_len, head_dim, q.dtype)
        q = q * cos + _rotate_half(q) * sin
        k = k * cos + _rotate_half(k) * sin
        scores = jnp.einsum('bhqd,bhkd->bhqk', q, k) * inv_sqrt_d
        scores = scores + attention_mask
        scores = jnp.maximum(scores, jnp.finfo(scores.dtype).min)
        w = jax.nn.softmax(scores.astype(jnp.float32), axis=-1).astype(q.dtype)
        attn_output = jnp.einsum('bhqk,bhkd->bhqd', w, v)
        adapter_len = adapter.shape[1]
        a_k = split_heads(adapter @ Wk, adapter_len)
        a_v = split_heads(adapter @ Wv, adapter_len)
        a_scores = jnp.einsum('bhqd,bhkd->bhqk', q, a_k) * inv_sqrt_d
        a_scores = jnp.tanh(gate) * jax.nn.softmax(a_scores.astype(jnp.float32), axis=-1).astype(q.dtype)
        attn_output = attn_output + jnp.einsum('bhqk,bhkd->bhqd', a_scores, a_v)
        attn_output = attn_output.transpose(0, 2, 1, 3).reshape(bsz, q_len, hid)
        return attn_output @ Wo

    def _L1_ffn_ref(x, gate_up_proj, down_proj):
        import jax, jax.numpy as jnp
        import numpy as np
        NUM_EXPERTS = 4
        B, N, H = x.shape
        E, _, two_I = gate_up_proj.shape
        I = two_I // 2
        G = N // E
        x4 = x.reshape(B, G, E, H)
        gu = jnp.einsum('bgeh,ehd->bged', x4, gate_up_proj)
        gate, up = (gu[..., :I], gu[..., I:])
        inter = jax.nn.silu(gate) * up
        out = jnp.einsum('bgei,eih->bgeh', inter, down_proj)
        return out.reshape(B, N, H)

    def _L2_xattn_ref(hidden_states, audio_tokens, attention_mask, Wq, bq, Wk, bk, Wv, bv, Wo, bo, ln_gamma, ln_beta, residual_scale):
        import jax, jax.numpy as jnp
        import numpy as np
        import math
        H = 256
        NH = 16
        HD = H // NH
        EPS_LN = 1e-05
        RES_SCALE_MAX = 0.3

        def _nan_clean(x, lim=10000.0):
            return jnp.nan_to_num(x, nan=0.0, posinf=lim, neginf=-lim)
        B, S, _ = hidden_states.shape
        T = audio_tokens.shape[1]
        hs = _nan_clean(hidden_states).astype(jnp.float32)
        at = _nan_clean(audio_tokens).astype(jnp.float32)

        def proj(x, W, b, L):
            y = x @ W.T + b
            return y.reshape(B, L, NH, HD).transpose(0, 2, 1, 3)
        q = _nan_clean(proj(hs, Wq, bq, S))
        k = _nan_clean(proj(at, Wk, bk, T))
        v = _nan_clean(proj(at, Wv, bv, T))
        scale = max(math.sqrt(HD), 1e-08)
        scores = jnp.einsum('bhsd,bhtd->bhst', q, k) / scale
        scores = jnp.clip(scores, -50.0, 50.0)
        scores = jnp.nan_to_num(scores, nan=0.0, posinf=50.0, neginf=-50.0)
        attend = (attention_mask.astype(jnp.float32) > 0.5)[:, None, None, :]
        scores = jnp.where(attend, scores, -10000.0)
        scores = jnp.clip(scores, -50.0, 50.0)
        probs = jax.nn.softmax(scores, axis=-1)
        probs = jnp.nan_to_num(probs, nan=0.0, posinf=1.0, neginf=0.0)
        probs = probs / (probs.sum(axis=-1, keepdims=True) + 1e-08)
        ctx = jnp.einsum('bhst,bhtd->bhsd', probs, v)
        ctx = ctx.transpose(0, 2, 1, 3).reshape(B, S, H)
        delta = _nan_clean(ctx @ Wo.T + bo)
        rs = jnp.clip(residual_scale, 0.0, RES_SCALE_MAX)
        delta = rs * delta
        mu = delta.mean(axis=-1, keepdims=True)
        var = jnp.mean((delta - mu) ** 2, axis=-1, keepdims=True)
        delta = (delta - mu) / jnp.sqrt(var + EPS_LN) * ln_gamma + ln_beta
        return delta

    def _L2_ffn_ref(x, w_gate, w_up, w_down):
        import jax, jax.numpy as jnp
        import numpy as np
        EPS = 1e-05

        def weight_quant(w):
            scale = 1.0 / jnp.clip(jnp.mean(jnp.abs(w)), EPS, None)
            return jnp.clip(jnp.round(w * scale), -1.0, 1.0) / scale

        def act_quant(x):
            scale = 127.0 / jnp.clip(jnp.max(jnp.abs(x), axis=-1, keepdims=True), EPS, None)
            return jnp.clip(jnp.round(x * scale), -128.0, 127.0) / scale

        def bitlinear(x, w):
            return jnp.einsum('bsd,od->bso', act_quant(x), weight_quant(w))
        gate = jax.nn.silu(bitlinear(x, w_gate))
        up = bitlinear(x, w_up)
        return bitlinear(gate * up, w_down)

    def _L3_xattn_ref(hidden_states, encoder_hidden_states, Wq, Wk, Wv, Wo, q_norm_w, k_norm_w):
        import jax, jax.numpy as jnp
        import numpy as np
        HIDDEN = 256
        N_HEADS = 16
        N_KV_HEADS = 4
        HEAD_DIM = 128
        EPS = 1e-06

        def rms_norm(x, w, eps=EPS):
            xf = x.astype(jnp.float32)
            var = jnp.mean(xf * xf, axis=-1, keepdims=True)
            return w * (xf * jax.lax.rsqrt(var + eps)).astype(x.dtype)
        B, S, _ = hidden_states.shape
        S_enc = encoder_hidden_states.shape[1]
        groups = N_HEADS // N_KV_HEADS
        scale = 1.0 / HEAD_DIM ** 0.5
        q = (hidden_states @ Wq).reshape(B, S, N_HEADS, HEAD_DIM)
        k = (encoder_hidden_states @ Wk).reshape(B, S_enc, N_KV_HEADS, HEAD_DIM)
        v = (encoder_hidden_states @ Wv).reshape(B, S_enc, N_KV_HEADS, HEAD_DIM)
        q = rms_norm(q, q_norm_w)
        k = rms_norm(k, k_norm_w)
        k = jnp.repeat(k, groups, axis=2)
        v = jnp.repeat(v, groups, axis=2)
        scores = jnp.einsum('bqhd,bkhd->bhqk', q, k) * scale
        probs = jax.nn.softmax(scores, axis=-1)
        out = jnp.einsum('bhqk,bkhd->bqhd', probs, v)
        out = out.reshape(B, S, N_HEADS * HEAD_DIM)
        return out @ Wo

    def _L3_ffn_ref(x, gate_w, gate_up_proj, down_proj, shared_gate_w, shared_up_w, shared_down_w):
        import jax, jax.numpy as jnp
        import numpy as np
        E = 64
        K = 6
        CAP = 64
        SCALE = 1.0
        H = 256
        I = 96
        SI = I * 2
        B, S = (2, 128)

        def _moe(x, gate_w, gate_up_proj, down_proj, shared_gate_w, shared_up_w, shared_down_w):
            b, s, h = x.shape
            T = b * s
            xf = x.reshape(T, h)
            scores = jax.nn.softmax(xf @ gate_w.T, axis=-1)
            topk_w, topk_idx = jax.lax.top_k(scores, K)
            topk_w = topk_w * SCALE
            flat_e = topk_idx.reshape(-1)
            order = jnp.argsort(flat_e)
            sorted_e = flat_e[order]
            sorted_tok = (order // K).astype(jnp.int32)
            sorted_w = topk_w.reshape(-1)[order]
            counts = jnp.zeros((E,), jnp.int32).at[flat_e].add(1)
            offsets = jnp.cumsum(counts) - counts
            pos = jnp.arange(T * K, dtype=jnp.int32) - offsets[sorted_e]
            buf_tok = jnp.full((E, CAP), T, jnp.int32).at[sorted_e, pos].set(sorted_tok, mode='drop')
            buf_w = jnp.zeros((E, CAP), x.dtype).at[sorted_e, pos].set(sorted_w, mode='drop')
            xp = jnp.concatenate([xf, jnp.zeros((1, h), x.dtype)], axis=0)
            gx = xp[buf_tok]
            gu = jnp.einsum('ech,ehi->eci', gx, gate_up_proj)
            g, u = jnp.split(gu, 2, axis=-1)
            hid = jax.nn.silu(g) * u
            eo = jnp.einsum('eci,eih->ech', hid, down_proj) * buf_w[..., None]
            routed = jnp.zeros((T + 1, h), x.dtype).at[buf_tok.reshape(-1)].add(eo.reshape(-1, h))[:T]
            shared = jax.nn.silu(xf @ shared_gate_w.T) * (xf @ shared_up_w.T) @ shared_down_w.T
            return (routed + shared).reshape(b, s, h)
        return _moe(x, gate_w, gate_up_proj, down_proj, shared_gate_w, shared_up_w, shared_down_w)
    x = x + jnp.tanh(g_xattn[0]) * _L0_xattn_ref(_layernorm(x, axis=-1), ctx_2048, L0_xattn_Wq, L0_xattn_bq, L0_xattn_Wk, L0_xattn_bk, L0_xattn_Wv, L0_xattn_bv, L0_xattn_Wo, L0_xattn_bo)
    x = x + jnp.tanh(g_ffn[0]) * _L0_ffn_ref(_layernorm(x, axis=-1), L0_ffn_gate_w, L0_ffn_expert_fc1, L0_ffn_expert_fc2, L0_ffn_expert_proj, L0_ffn_shared_fc1, L0_ffn_shared_fc2, L0_ffn_shared_proj, L0_ffn_shared_gate_w)
    x = x + jnp.tanh(g_xattn[1]) * _L1_xattn_ref(_layernorm(x, axis=-1), mask_Bx1xSxS_fk0, ctx_2048, L1_xattn_Wq, L1_xattn_Wk, L1_xattn_Wv, L1_xattn_Wo, L1_xattn_gate)
    x = x + jnp.tanh(g_ffn[1]) * _L1_ffn_ref(_layernorm(x, axis=-1), L1_ffn_gate_up_proj, L1_ffn_down_proj)
    x = x + jnp.tanh(g_xattn[2]) * _L2_xattn_ref(_layernorm(x, axis=-1), ctx_2048, mask_BxS2_ik0, L2_xattn_Wq, L2_xattn_bq, L2_xattn_Wk, L2_xattn_bk, L2_xattn_Wv, L2_xattn_bv, L2_xattn_Wo, L2_xattn_bo, L2_xattn_ln_gamma, L2_xattn_ln_beta, L2_xattn_residual_scale)
    x = x + jnp.tanh(g_ffn[2]) * _L2_ffn_ref(_layernorm(x, axis=-1), L2_ffn_w_gate, L2_ffn_w_up, L2_ffn_w_down)
    x = x + jnp.tanh(g_xattn[3]) * _L3_xattn_ref(_layernorm(x, axis=-1), ctx_2048, L3_xattn_Wq, L3_xattn_Wk, L3_xattn_Wv, L3_xattn_Wo, L3_xattn_q_norm_w, L3_xattn_k_norm_w)
    x = x + jnp.tanh(g_ffn[3]) * _L3_ffn_ref(_layernorm(x, axis=-1), L3_ffn_gate_w, L3_ffn_gate_up_proj, L3_ffn_down_proj, L3_ffn_shared_gate_w, L3_ffn_shared_up_w, L3_ffn_shared_down_w)
    return x

_drawn_inputs = setup_inputs


def setup_inputs(seed=0):
    import zlib

    import numpy as np

    out = dict(_drawn_inputs(seed))
    spreads = {'L0_xattn_bq': (0.0, 0.1),
     'L0_xattn_bk': (0.0, 0.581),
     'L0_xattn_bv': (0.0, 0.8),
     'L2_xattn_bq': (0.0, 1.029),
     'L2_xattn_bk': (0.0, 2.0),
     'L2_xattn_bv': (0.0, 0.1),
     'L2_xattn_bo': (0.0, 0.1),
     'L2_xattn_ln_gamma': (1.0, 0.2),
     'L2_xattn_ln_beta': (0.0, 0.34),
     'L3_xattn_q_norm_w': (1.0, 0.6),
     'L3_xattn_k_norm_w': (1.0, 0.6)}
    factors = {'g_ffn': 8.0,
     'L0_xattn_bo': 36.816,
     'L0_ffn_gate_w': 8.0,
     'L0_ffn_expert_fc1': 8.0,
     'L0_ffn_expert_fc2': 8.0,
     'L0_ffn_expert_proj': 8.0,
     'L0_ffn_shared_fc1': 6.601,
     'L0_ffn_shared_fc2': 6.559,
     'L0_ffn_shared_proj': 6.551,
     'L0_ffn_shared_gate_w': 8.0,
     'L1_xattn_Wq': 8.0,
     'L1_xattn_Wk': 8.0,
     'L1_xattn_gate': 24.981,
     'L1_ffn_gate_up_proj': 4.585,
     'L1_ffn_down_proj': 4.582,
     'L2_ffn_w_gate': 8.0,
     'L2_ffn_w_up': 8.0,
     'L2_ffn_w_down': 8.0,
     'L3_ffn_gate_w': 8.0,
     'L3_ffn_gate_up_proj': 8.0,
     'L3_ffn_down_proj': 8.0,
     'L3_ffn_shared_gate_w': 5.921,
     'L3_ffn_shared_up_w': 5.913,
     'L3_ffn_shared_down_w': 5.916,
     'L3_xattn_Wq': 3.862,
     'L3_xattn_Wk': 3.78,
     'L3_xattn_Wo': 2.921}
    for name, (base, spread) in spreads.items():
        noise = np.random.default_rng([zlib.crc32(name.encode()), seed]).standard_normal(out[name].shape)
        drawn = base * np.exp(spread * noise) if base else spread * noise
        out[name] = jnp.asarray(drawn.astype(out[name].dtype))
    for name, factor in factors.items():
        out[name] = (out[name] * factor).astype(out[name].dtype)
    return out
```

```python
from contextlib import ExitStack

import numpy as np

import concourse.bass as bass
from concourse import mybir

F32 = mybir.dt.float32
BF16 = mybir.dt.bfloat16
U32 = mybir.dt.uint32
I32 = mybir.dt.int32
ALU = mybir.AluOpType
ACT = mybir.ActivationFunctionType
AXX = mybir.AxisListType.X

P = 128
NB = 16
S = 128
D = 256
KD = D // P
BANK = 512
BLK = 4
NBLK = NB // BLK
EPS_LN = 1e-5
LOWEST = -3.38e38
ROUND = 12582912.0
PART_Q = (0, 0, 1, 1, 0, 2)
PART_K = (0, 1, 0, 1, 2, 0)
NT = len(PART_Q)

H0, G0, HD0, T0 = 16, 4, 8, 256
E0, F0, FS0 = 8, 176, 704
HID0 = E0 * F0 + FS0
NF0 = -(-HID0 // P)
H1, HD1 = 32, 8
E1 = 4
H2, HD2 = 16, 16
F2 = 832
NF2 = -(-F2 // P)
H3, G3, HD3 = 16, 4, 128
E3, K3, CAP3, I3, SI3 = 64, 6, 64, 96, 192
NSLOT = E3 * CAP3
EPS_RMS = 1e-6


class Engine:

    def __init__(self, api, sem):
        self.api, self.sem, self.count, self.seen = api, sem, 0, {}

    def after(self, *tokens):
        for t in tokens:
            if isinstance(t, list):
                self.after(*t)
            elif t is not None:
                name, sem, value = t
                if self.seen.get(name, 0) < value:
                    self.api.wait_ge(sem, value)
                    self.seen[name] = value
        return self.api

    def done(self, instruction):
        self.count += 1
        instruction.then_inc(self.sem, 1)
        return self.last()

    def last(self):
        return (id(self), self.sem, self.count)


class Lane:

    def __init__(self, sem):
        self.sem, self.count = sem, 0

    def start(self, engine, out, in_, *waits):
        engine.after(*waits).dma_start(out, in_).then_inc(self.sem, 16)
        self.count += 16
        return self.token()

    def token(self):
        return (id(self), self.sem, self.count)


class Buf:

    def __init__(self, ap, lane=None):
        self.ap, self.lane, self.free, self.held, self.age = ap, lane, [], False, 0

    def release(self, *tokens):
        self.free, self.held = list(tokens), False


class Ring:
    def __init__(self, bufs):
        self.bufs, self.clock = bufs, 0

    def take(self):
        while all(b.held for b in self.bufs):
            yield False
        buf = min((b for b in self.bufs if not b.held), key=lambda b: b.age)
        self.clock += 1
        buf.held, buf.age = True, self.clock
        return buf


class PsumBanks:

    def __init__(self, tensor):
        self.tensor, self.free, self.held = tensor, [[] for _ in range(8)], [False] * 8
        self.age, self.clock = [0] * 8, 0

    def take(self, n):
        while True:
            starts = [i for i in range(0, 8, n) if not any(self.held[i:i + n])]
            if starts:
                break
            yield False
        i = min(starts, key=lambda k: (n == 1 and not self.held[k ^ 1], max(self.age[k:k + n]), k))
        self.clock += 1
        for k in range(i, i + n):
            self.held[k], self.age[k] = True, self.clock
        return Banks(self, i, n)


class Banks:
    def __init__(self, pool, i, n):
        self.pool, self.i, self.n = pool, i, n
        self.ap = pool.tensor[:, i * BANK:(i + n) * BANK]
        self.free = [t for k in range(i, i + n) for t in pool.free[k]]

    def release(self, *tokens):
        for k in range(self.i, self.i + self.n):
            self.pool.held[k], self.pool.free[k] = False, list(tokens)
            self.pool.clock += 1
            self.pool.age[k] = self.pool.clock


def interleave(jobs, depth):
    jobs, active = list(jobs), []
    while jobs or active:
        while jobs and len(active) < depth:
            active.append(jobs.pop(0))
        moved = False
        for job in list(active):
            try:
                moved = (next(job) is not False) or moved
            except StopIteration:
                active.remove(job)
                moved = True
        if not moved:
            yield False
        else:
            yield True


def run(job):
    stuck = 0
    for moved in job:
        stuck = stuck + 1 if moved is False else 0
        if stuck > 200:
            raise RuntimeError("the jobs wait for each other")


class Arena:

    def __init__(self, tensor, lo, hi):
        self.tensor, self.at, self.lo, self.hi = tensor, lo, lo, hi

    def f32(self, cols, rows=P):
        a = self.at
        self.at += cols
        if self.at > self.hi:
            raise RuntimeError(f"arena full: {self.at} > {self.hi}")
        return self.tensor[0:rows, a:a + cols]

    def bf16(self, cols, rows=P):
        return self.f32(-(-cols // 2), rows).bitcast(BF16)[:, 0:cols]

    def reset(self):
        self.at = self.lo


def program(nc, A, out, last_stage=8):
    ctx = ExitStack()
    with ctx:
        n_sem = [0]

        def sem(name):
            n_sem[0] += 1
            return ctx.enter_context(nc.semaphore(name))

        pe = Engine(nc.tensor, sem("pe_done"))
        dve = Engine(nc.vector, sem("dve_done"))
        act = Engine(nc.scalar, sem("act_done"))
        pool = Engine(nc.gpsimd, sem("pool_done"))
        sp = Engine(nc.sync, sem("sp_done"))
        engines = [pe, dve, act, pool, sp]
        lanes = []

        def lane(name):
            lanes.append(Lane(sem(name)))
            return lanes[-1]

        COLS = 52800
        sbuf = ctx.enter_context(nc.sbuf_tensor("sbuf", [P, COLS], F32))
        psum = PsumBanks(ctx.enter_context(nc.psum_tensor("psum", [P, 8 * BANK], F32)))

        def dram(name, shape, dtype):
            return nc.dram_tensor(name, shape, dtype, kind="Internal").ap()

        A_AT, B_AT, WORK_AT = 8800, 22900, 34300
        keep = Arena(sbuf, 0, A_AT)
        region_a = Arena(sbuf, A_AT, B_AT)
        region_b = Arena(sbuf, B_AT, WORK_AT)

        x_all = keep.f32(NB * D)
        X = [x_all[:, b * D:(b + 1) * D] for b in range(NB)]
        ctxT = keep.f32(KD * NB * S).rearrange("p (k n) -> p k n", k=KD)
        ident = keep.f32(P)
        ident_bf = keep.bf16(P)
        gates = keep.f32(8)
        half_neg = keep.f32(1)
        ln_cols = [keep.f32(16) for _ in range(6)]
        stat_ring = Ring([Buf(a) for a in ln_cols])

        const_lane = lane("const_loaded")
        x_lane = lane("x_loaded")
        for name, dst in (("ident", ident),):
            const_lane.start(sp, dst, A[name])
        for name, lo in (("g_xattn", 0), ("g_ffn", 4)):
            const_lane.start(sp, gates[:, lo:lo + 4], A[name].rearrange("(a n) -> a n", a=1).broadcast_to([P, 4]))
        x_ready = []
        for b in range(NB):
            x_lane.start(sp, X[b], A["x"][b])
            x_ready.append([])
        t_bf = dve.done(dve.after(const_lane.token()).tensor_copy(ident_bf, ident))
        t_half = dve.done(dve.api.memset(half_neg, -0.5))
        t_gate = act.done(act.after(const_lane.token()).activation(gates, gates, ACT.Tanh))
        for b in range(NB):
            x_ready[b] = [x_lane.token()]
        for e in (pe, dve, act, pool):
            e.after(t_bf, t_half, t_gate, const_lane.token())

        def barrier():
            ends = [e.last() for e in engines if e is not sp] + [l.token() for l in lanes if l.count]
            for e in engines:
                e.after([t for t in ends if t[0] != id(e)])
                if e is not sp:
                    e.after(e.last())

        def rstd(out_col, var_col, eps, scale, *waits):
            n = out_col.shape[-1]
            t = dve.done(dve.after(*waits).tensor_scalar(out_col, var_col, scale, eps, ALU.mult, ALU.add))
            return pool.done(pool.after(t).tensor_tensor(out_col, out_col,
                             half_neg.broadcast_to([P, n]) if n > 1 else half_neg, ALU.pow))

        def layer_norm(src, dst, waits, dst_free):
            st = yield from stat_ring.take()
            s = st.ap
            t = dve.done(dve.after(waits, st.free).bn_stats(s[:, 0:6], src))
            t = dve.done(dve.after(t).bn_aggr(s[:, 6:8], s[:, 0:6]))
            t = rstd(s[:, 8:9], s[:, 7:8], EPS_LN, 1.0, t)
            yield True
            t = dve.done(dve.after(t, dst_free).tensor_scalar(dst, src, s[:, 6:7], s[:, 8:9],
                                                             ALU.subtract, ALU.mult))
            st.release(t)
            return t

        def split3(src, dst, tmp, waits, dst_free):
            hi, mid, lo = (dst[:, i] for i in range(3))
            t = act.done(act.after(waits, dst_free).activation(hi, src, ACT.Copy))
            t = pool.done(pool.after(t, dst_free).tensor_tensor(tmp, src, hi, ALU.subtract))
            t = act.done(act.after(t).activation(mid, tmp, ACT.Copy))
            return pool.done(pool.after(t).tensor_tensor(lo, tmp, mid, ALU.subtract))

        def transposes(blocks, ps, ident_ap, *waits):
            api = pe.after(*waits)
            for src, dst in blocks:
                last = api.transpose(dst, src, ident_ap)
            return pe.done(last)

        def normalise(av, width, head_w, dst, t_av, t_free, ring):
            nblk = width // 32
            tb = yield from ring.take()
            T = tb.ap[:, 0:width]
            R = tb.ap[:, width:width + nblk]
            t = dve.done(dve.after(t_av, tb.free).transpose(T, av.ap[:, 0:width]))
            av.release(t)
            T3 = T.rearrange("p (n r) -> p n r", r=32)
            t = dve.done(dve.after(t).reciprocal(R, T3[:, :, head_w]))
            t = dve.done(dve.after(t).tensor_tensor(
                T3, T3, R.unsqueeze(2).broadcast_to([P, nblk, 32]), ALU.mult))
            t = dve.done(dve.after(t, t_free).transpose(dst, T))
            tb.release(t)
            return t

        def load(ln, dst, src, *waits):
            return ln.start(sp, dst, src, *waits)

        w_lane = [lane(f"weights_{i}_loaded") for i in range(8)]

        def l0_attention():
            A0 = Arena(sbuf, B_AT, COLS)
            wq = A0.f32(P)
            wqp = A0.f32(P)
            wk = A0.f32(2 * 32)
            wv = A0.f32(32)
            wo = A0.f32(4 * P).rearrange("p (j o) -> p j o", j=4)
            cosq, sinq = A0.f32(T0), A0.f32(T0)
            cosk, sink = A0.f32(T0, 32), A0.f32(T0, 32)
            bq = A0.f32(2)
            bk = A0.f32(2, 32)
            bo = A0.f32(1)
            bv = A0.f32(32)
            wl = w_lane[0]
            t_zero = dve.done(dve.api.memset(wo, 0.0))
            load(wl, wq, A["l0_wqT"])
            load(wl, wqp, A["l0_wqpT"])
            load(wl, wk[:, 0:32], A["l0_wkT"])
            load(wl, wk[:, 32:64], A["l0_wkpT"])
            load(wl, wv, A["l0_wvT"])
            load(wl, cosq, A["l0_cosq"])
            load(wl, sinq, A["l0_sinq"])
            load(wl, cosk, A["l0_cosk"])
            load(wl, sink, A["l0_sink"])
            load(wl, bq, A["l0_bq2"])
            load(wl, bk, A["l0_bk2"])
            load(wl, bo, A["l0_bo"])
            load(wl, bv, A["l0_bv"].broadcast_to([P, 32]))
            for g in range(G0):
                load(wl, wo[32 * g:32 * g + HD0], A["l0_woT"][32 * g:32 * g + 32].rearrange("(j d) o -> d j o", d=HD0), t_zero)
            w_ready = wl.token()

            ctx_ring = Ring([Buf(A0.f32(T0), lane(f"ctx_loaded_{i}")) for i in range(3)])
            xn_ring = Ring([Buf(A0.f32(T0)) for _ in range(2)])
            rope_ring = Ring([Buf(A0.f32(4 * T0)) for _ in range(2)])
            part_ring = Ring([Buf(A0.bf16(3 * T0), lane(f"q_parts_stored_{i}")) for i in range(2)])
            kpart_ring = Ring([Buf(A0.bf16(3 * T0, 32), lane(f"k_parts_stored_{i}")) for i in range(2)])
            q_ring = [Buf(A0.bf16(H0 * T0), lane(f"q_stack_loaded_{i}")) for i in range(2)]
            k_ring = [Buf(A0.bf16(G0 * T0), lane(f"k_stack_loaded_{i}")) for i in range(2)]
            v_ring = [Buf(A0.f32(2 * G0 * 32)) for i in range(2)]
            d_ring = Ring([Buf(A0.f32(4 * T0)) for _ in range(4)])
            e_ring = Ring([Buf(A0.f32(2 * 4 * P)) for _ in range(8)])
            m_ring = Ring([Buf(A0.f32(4)) for _ in range(4)])
            t_ring = Ring([Buf(A0.f32(BANK + 16)) for _ in range(2)])
            attn_ring = Ring([Buf(A0.f32(4 * T0)) for _ in range(2)])
            q_dram = dram("l0_q_parts", [NB, 3, P, T0], BF16)
            k_dram = dram("l0_k_parts", [NB, 3, 32, T0], BF16)
            for buf in q_ring + k_ring:
                buf.free = [dve.done(dve.api.memset(buf.ap[0:96], 0.0))]
            for buf in v_ring:
                v4 = buf.ap.rearrange("p (c g w) -> p c g w", c=2, g=G0)
                t = dve.done(dve.api.memset(buf.ap, 0.0))
                buf.free = [dve.done(dve.after(t).memset(v4[:, :, :, HD0:HD0 + 1], 1.0))]
            q_ring, k_ring, v_ring = Ring(q_ring), Ring(k_ring), Ring(v_ring)

            def unit(b, c, g, q_st, k_st, st_ready, E, state):
                m = yield from m_ring.take()
                d = yield from d_ring.take()
                ps = yield from psum.take(2)
                api = pe.after(st_ready, ps.free)
                q3 = q_st.ap.rearrange("p (h t) -> p h t", h=H0)
                k3 = k_st.ap.rearrange("p (g t) -> p g t", g=G0)
                for j in range(4):
                    last = api.matmul(ps.ap[:, j * T0:(j + 1) * T0], q3[0:96, 4 * g + j, c * P:(c + 1) * P],
                                      k3[0:96, g, :], start=True, stop=True)
                t_s = pe.done(last)
                state["scored"] = t_s
                yield True
                s3 = ps.ap.rearrange("p (j t) -> p j t", j=4)
                d3 = d.ap.rearrange("p (j t) -> p j t", j=4)
                t = dve.done(dve.after(t_s, m.free).tensor_reduce(m.ap, s3, AXX, ALU.max))
                t = dve.done(dve.after(t, d.free).tensor_tensor(
                    d3, s3, m.ap.unsqueeze(2).broadcast_to([P, 4, T0]), ALU.subtract))
                ps.release(t)
                m.release(t)
                yield True
                e = yield from e_ring.take()
                pt = yield from psum.take(2)
                t = transposes([(d3[:, j, kc * P:(kc + 1) * P], pt.ap[:, (kc * 4 + j) * P:(kc * 4 + j + 1) * P])
                                for kc in range(2) for j in range(4)], pt, ident, t, pt.free)
                d.release(t)
                yield True
                t = act.done(act.after(t, e.free).activation(e.ap, pt.ap, ACT.Exp))
                pt.release(t)
                E[g] = (e, t)

            def values(b, c, v, v_ready, E, at, state):
                while len(E) < G0:
                    yield False
                av = yield from psum.take(1)
                v4 = v.ap.rearrange("p (c g w) -> p c g w", c=2, g=G0)
                for kc in range(2):
                    for g in range(G0):
                        last = pe.after(v_ready, av.free, E[g][1]).matmul(
                            av.ap[32 * g:32 * g + 32, :], v4[:, kc, g, :], E[g][0].ap[:, kc * BANK:(kc + 1) * BANK],
                            start=(kc == 0), stop=(kc == 1), tile_position=(0, 32 * g))
                t = pe.done(last)
                for g in range(G0):
                    E[g][0].release(t)
                state["valued"] = t
                yield True
                dst = at.ap.rearrange("p (c n) -> p c n", c=2)[:, c]
                state[c] = yield from normalise(av, BANK, HD0, dst, t, at.free, t_ring)

            def batch(b):
                cb = yield from ctx_ring.take()
                t_ctx = load(cb.lane, cb.ap, A["ctx_2048"][b], *cb.free)
                xn = yield from xn_ring.take()
                t_xn = yield from layer_norm(X[b], xn.ap, x_ready[b], xn.free)
                yield True
                pc = yield from psum.take(1)
                t = transposes([(cb.ap[:, k * P:(k + 1) * P], pc.ap[:, k * P:(k + 1) * P]) for k in range(KD)],
                               pc, ident, t_ctx, pc.free)
                t_c = act.done(act.after(t).activation(ctxT[:, :, b * S:(b + 1) * S],
                                                       pc.ap[:, 0:D].rearrange("p (k n) -> p k n", k=KD), ACT.Copy))
                pc.release(t_c)
                pq = yield from psum.take(1)
                pk = yield from psum.take(1)
                pv = yield from psum.take(1)
                api = pe.after(t_xn, w_ready, pq.free)
                api.matmul(pq.ap[:, 0:T0], wq, xn.ap, start=True, stop=True)
                t_q = pe.done(api.matmul(pq.ap[:, T0:2 * T0], wqp, xn.ap, start=True, stop=True))
                xn.release(t_q)
                api = pe.after(t_ctx, pk.free, pv.free)
                api.matmul(pk.ap[0:32, 0:T0], wk[:, 0:32], cb.ap, start=True, stop=True)
                api.matmul(pk.ap[0:32, T0:2 * T0], wk[:, 32:64], cb.ap, start=True, stop=True)
                api.matmul(pv.ap[:, 0:32], cb.ap[:, 0:P], wv, start=True, stop=True)
                t_kv = pe.done(api.matmul(pv.ap[:, 32:64], cb.ap[:, P:2 * P], wv, start=True, stop=True))
                cb.release(t_kv, t)
                yield True
                r = yield from rope_ring.take()
                q_a, q_b, k_a, k_b = (r.ap[:, i * T0:(i + 1) * T0] for i in range(4))
                t1 = dve.done(dve.after(t_q, r.free).scalar_tensor_tensor(q_a, pq.ap[:, 0:T0], bq[:, 0:1], cosq, ALU.add, ALU.mult))
                t2 = dve.done(dve.api.scalar_tensor_tensor(q_b, pq.ap[:, T0:2 * T0], bq[:, 1:2], sinq, ALU.add, ALU.mult))
                pq.release(t2)
                t_qr = dve.done(dve.after(t1, t2).tensor_tensor(q_a, q_a, q_b, ALU.add))
                t1 = dve.done(dve.after(t_kv).scalar_tensor_tensor(k_a[0:32], pk.ap[0:32, 0:T0], bk[:, 0:1], cosk, ALU.add, ALU.mult))
                t2 = dve.done(dve.api.scalar_tensor_tensor(k_b[0:32], pk.ap[0:32, T0:2 * T0], bk[:, 1:2], sink, ALU.add, ALU.mult))
                pk.release(t2)
                t_kr = dve.done(dve.after(t1, t2).tensor_tensor(k_a[0:32], k_a[0:32], k_b[0:32], ALU.add))
                v = yield from v_ring.take()
                v4 = v.ap.rearrange("p (c g w) -> p c g w", c=2, g=G0)
                bv3 = bv.rearrange("p (g w) -> p g w", g=G0)
                for c in range(2):
                    t_v = dve.done(dve.after(v.free).tensor_tensor(
                        v4[:, c, :, 0:HD0], pv.ap[:, 32 * c:32 * c + 32].rearrange("p (g w) -> p g w", g=G0), bv3, ALU.add))
                pv.release(t_v)
                yield True
                qp = yield from part_ring.take()
                kp = yield from kpart_ring.take()
                qp3 = qp.ap.rearrange("p (i t) -> p i t", i=3)
                kp3 = kp.ap.rearrange("p (i t) -> p i t", i=3)
                t_qs = split3(q_a, qp3, q_b, t_qr, qp.free)
                t_ks = split3(k_a[0:32], kp3, k_b[0:32], t_kr, kp.free)
                r.release(t_qs, t_ks)
                t_qw = qp.lane.start(sp, q_dram[b].rearrange("i r t -> r i t"), qp3, t_qs)
                t_kw = kp.lane.start(sp, k_dram[b].rearrange("i r t -> r i t"), kp3, t_ks)
                qp.release(t_qw)
                kp.release(t_kw)
                yield True
                q_st = yield from q_ring.take()
                k_st = yield from k_ring.take()
                for i in range(NT):
                    q_st.lane.start(sp, q_st.ap[HD0 * i:HD0 * i + HD0], q_dram[b, PART_Q[i]].rearrange("(d h) t -> d (h t)", d=HD0),
                                    q_st.free, t_qw)
                    k_st.lane.start(sp, k_st.ap[HD0 * i:HD0 * i + HD0], k_dram[b, PART_K[i]].rearrange("(d g) t -> d (g t)", d=HD0),
                                    k_st.free, t_kw)
                yield True
                yield True
                st_ready = [q_st.lane.token(), k_st.lane.token()]
                at = yield from attn_ring.take()
                state, jobs = {}, []
                for c in range(2):
                    E = {}
                    jobs += [unit(b, c, g, q_st, k_st, st_ready, E, state) for g in range(G0)]
                    jobs.append(values(b, c, v, t_v, E, at, state))
                yield from interleave(jobs, 4)
                q_st.release(state["scored"])
                k_st.release(state["scored"])
                v.release(state["valued"])
                po = yield from psum.take(1)
                a4 = at.ap.rearrange("p (c j n) -> p j c n", c=2, j=4)
                for j in range(4):
                    last = pe.after(state[0], state[1], po.free).matmul(po.ap[:, 0:T0], wo[:, j, :], a4[:, j], start=(j == 0), stop=(j == 3))
                t = pe.done(last)
                at.release(t)
                yield True
                tmp = yield from rope_ring.take()
                t = dve.done(dve.after(t, tmp.free).tensor_scalar(tmp.ap[:, 0:T0], po.ap[:, 0:T0], bo, gates[:, 0:1], ALU.add, ALU.mult))
                po.release(t)
                t = dve.done(dve.after(t).tensor_tensor(X[b], X[b], tmp.ap[:, 0:T0], ALU.add))
                tmp.release(t)
                x_ready[b] = [t]

            run(interleave([batch(b) for b in range(NB)], 2))

        def chunks_of(src, k=KD):
            return src.rearrange("(k p) n -> p k n", k=k)

        def split_cols(ap, k):
            return ap.rearrange("p (k n) -> p k n", k=k)

        def norm_transpose(blk, xn_ring, xnT, xnT_free, xn_out=None):
            tiles = []
            xn = yield from xn_ring.take()
            for i in range(BLK):
                b = blk * BLK + i
                tile = xn.ap[:, i * D:(i + 1) * D]
                t = yield from layer_norm(X[b], tile, x_ready[b], xn.free)
                tiles.append((tile, t))
            yield True
            ps = yield from psum.take(2)
            p4 = ps.ap.rearrange("p (k b n) -> p k b n", k=KD, b=BLK)
            t = transposes([(xn_i[:, k * P:(k + 1) * P], p4[:, k, i]) for i, (xn_i, _) in enumerate(tiles) for k in range(KD)],
                           ps, ident, [t for _, t in tiles], ps.free)
            xn.release(t)
            yield True
            t = act.done(act.after(t, xnT_free).activation(xnT, split_cols(ps.ap, KD), ACT.Copy))
            ps.release(t)
            return t

        R0 = region_a
        w_fc1 = split_cols(R0.f32(KD * HID0), KD)
        w_fc2 = split_cols(R0.f32(KD * HID0), KD)
        w_proj = split_cols(R0.f32(NF0 * D), NF0)
        w_gate0 = split_cols(R0.f32(KD * 9), KD)
        sel = R0.bf16(NF0 * P)[0:96]
        l0f_lane = lane("l0_ffn_weights_loaded")
        load(l0f_lane, w_gate0, chunks_of(A["l0_gateT"]))
        load(l0f_lane, w_fc1, chunks_of(A["l0_fc1T"]))
        load(l0f_lane, w_fc2, chunks_of(A["l0_fc2T"]))
        whole = HID0 // P * P
        load(l0f_lane, w_proj[:, 0:HID0 // P], chunks_of(A["l0_projT"][0:whole], HID0 // P))
        load(l0f_lane, w_proj[0:HID0 - whole, NF0 - 1], A["l0_projT"][whole:])

        def l0_ffn():
            load_l1_weights()
            W = Arena(sbuf, WORK_AT, COLS)
            sel_f = W.f32(NF0 * P, 96)
            sl = lane("l0_selection_loaded")
            iota8 = W.f32(E0)
            sl.start(sp, iota8, A["iota"][:, 0:E0].broadcast_to([P, E0]))
            t_io = sl.start(sp, sel_f, A["l0_sel"])
            t_sel = act.done(act.after(t_io).activation(sel, sel_f, ACT.Copy))
            xn_ring = Ring([Buf(W.f32(BLK * D)) for _ in range(1)])
            xt_ring = Ring([Buf(W.f32(KD * BANK)) for _ in range(2)])
            r_ring = Ring([Buf(W.f32(400)) for _ in range(2)])
            cs_ring = [Buf(W.bf16(BLK * 96)) for _ in range(2)]
            for buf in cs_ring:
                buf.free = [dve.done(dve.api.memset(buf.ap, 0.0))]
            cs_ring = Ring(cs_ring)
            ct_ring = Ring([Buf(W.bf16(BANK)[0:96]) for _ in range(2)])
            th_ring = Ring([Buf(W.f32(BANK)) for _ in range(3)])
            h_ring = Ring([Buf(W.f32(BANK)) for _ in range(3)])
            acc_turn = Ring([Buf(None)])

            def router(xT, t_x, out):
                r = yield from r_ring.take()
                cuts, at = {}, 0
                for name, n in (("logit", 9), ("prob", 8), ("top", 8), ("comb", 9), ("eq", 8), ("index", 8), ("mx", 1), ("sum", 1), ("tmp", 9)):
                    cuts[name] = r.ap[:, at:at + BLK * n].rearrange("p (b n) -> p b n", b=BLK)
                    at += BLK * n
                idx_u = r.ap[:, at:at + BLK * 8].bitcast(U32).rearrange("p (b n) -> p b n", b=BLK)
                lg, pr, top, comb, eq, index, mx, sm, tmp = (cuts[n] for n in ("logit", "prob", "top", "comb", "eq", "index", "mx", "sum", "tmp"))
                bc8 = lambda a: a.broadcast_to([P, BLK, E0])
                ps = yield from psum.take(1)
                for i in range(BLK):
                    for k in range(KD):
                        last = pe.after(t_x, l0f_lane.token(), ps.free).matmul(
                            ps.ap[:, 16 * i:16 * i + 9], xT[:, k, i * P:(i + 1) * P], w_gate0[:, k, :],
                            start=(k == 0), stop=(k == KD - 1))
                t = pe.done(last)
                t = dve.done(dve.after(t, r.free).tensor_copy(lg, ps.ap[:, 0:16 * BLK].rearrange("p (b n) -> p b n", b=BLK)[:, :, 0:9]))
                ps.release(t)
                t = dve.done(dve.after(t).tensor_reduce(mx, lg[:, :, 0:8], AXX, ALU.max))
                t = dve.done(dve.after(t).tensor_tensor(pr, lg[:, :, 0:8], bc8(mx), ALU.subtract))
                t = act.done(act.after(t).activation(pr, pr, ACT.Exp))
                t_sg = act.done(act.api.activation(comb[:, :, 8:9], lg[:, :, 8:9], ACT.Tanh, scale=0.5))
                yield True
                t = dve.done(dve.after(t).tensor_reduce(sm, pr, AXX, ALU.add))
                t = dve.done(dve.after(t).reciprocal(sm, sm))
                t = dve.done(dve.after(t).tensor_tensor(pr, pr, bc8(sm), ALU.mult))
                for i in range(BLK):
                    t2 = dve.done(dve.after(t).max(top[:, i], pr[:, i]))
                    t3 = dve.done(dve.after(t2).max_index(idx_u[:, i], top[:, i], pr[:, i]))
                t = dve.done(dve.after(t3).tensor_copy(index, idx_u))
                iob = iota8.unsqueeze(1).broadcast_to([P, BLK, E0])
                for k in range(2):
                    dst = comb[:, :, 0:8] if k == 0 else tmp[:, :, 0:8]
                    t = dve.done(dve.after(t, t_io).tensor_tensor(eq, iob, bc8(index[:, :, k:k + 1]), ALU.is_equal))
                    t = dve.done(dve.after(t, t_sg).tensor_tensor(dst, eq, bc8(top[:, :, k:k + 1]), ALU.mult))
                t = dve.done(dve.after(t).tensor_tensor(comb[:, :, 0:8], comb[:, :, 0:8], tmp[:, :, 0:8], ALU.add))
                t = dve.done(dve.after(t).tensor_scalar(comb[:, :, 8:9], comb[:, :, 8:9], 0.5, 0.5, ALU.mult, ALU.add))
                t = dve.done(dve.after(t).tensor_scalar(comb, comb, 0.5, None, ALU.mult))
                cs = yield from cs_ring.take()
                c4 = cs.ap.rearrange("p (b i w) -> p b i w", b=BLK, i=3)
                t = dve.done(dve.after(t, cs.free).tensor_copy(c4[:, :, 0, 0:9], comb))
                t = dve.done(dve.after(t).tensor_tensor(tmp, comb, c4[:, :, 0, 0:9], ALU.subtract))
                t = dve.done(dve.after(t).tensor_copy(c4[:, :, 1, 0:9], tmp))
                t = dve.done(dve.after(t).tensor_tensor(c4[:, :, 2, 0:9], tmp, c4[:, :, 1, 0:9], ALU.subtract))
                r.release(t)
                yield True
                ps = yield from psum.take(1)
                pb = ps.ap.bitcast(BF16)[0:96, 0:BANK]
                t = transposes([(cs.ap[:, 96 * i:96 * i + 96], pb[:, i * P:(i + 1) * P]) for i in range(BLK)],
                               ps, ident_bf, t, ps.free)
                cs.release(t)
                ct = yield from ct_ring.take()
                t = dve.done(dve.after(t, ct.free).tensor_copy(ct.ap, pb))
                ps.release(t)
                out.append((ct, t))

            def hidden(f, xT, ct, t_ct, acc, state):
                M = min(P, HID0 - f * P)
                gp = yield from psum.take(1)
                ps = yield from psum.take(2)
                fs = slice(f * P, f * P + M)
                for n, w in enumerate((w_fc1, w_fc2)):
                    for k in range(KD):
                        last = pe.after(ps.free, gp.free).matmul(
                            ps.ap[0:M, n * BANK:(n + 1) * BANK], w[:, k, fs], xT[:, k, :], start=(k == 0), stop=(k == KD - 1))
                t_h = pe.done(last)
                t_g = pe.done(pe.after(t_ct, t_sel).matmul(gp.ap[0:M], sel[:, fs], ct, start=True, stop=True))
                yield True
                h1, h2 = ps.ap[0:M, 0:BANK], ps.ap[0:M, BANK:2 * BANK]
                th = yield from th_ring.take()
                h = yield from h_ring.take()
                t = act.done(act.after(t_h, th.free).activation(th.ap[0:M], h1, ACT.Tanh, scale=0.5))
                t = dve.done(dve.after(t, h.free).scalar_tensor_tensor(h.ap[0:M], th.ap[0:M], 1.0, h1, ALU.add, ALU.mult))
                th.release(t)
                t = dve.done(dve.after(t).tensor_tensor(h.ap[0:M], h.ap[0:M], h2, ALU.mult))
                ps.release(t)
                t = dve.done(dve.after(t, t_g).tensor_tensor(h.ap[0:M], h.ap[0:M], gp.ap[0:M], ALU.mult))
                gp.release(t)
                yield True
                for i in range(BLK):
                    last = pe.after(t, acc.free).matmul(acc.ap[:, i * D:(i + 1) * D], h.ap[0:M, i * P:(i + 1) * P], w_proj[0:M, f, :],
                                                        start=(f == 0 and i % 2 == 0), stop=(f == NF0 - 1), skip_group_check=True)
                t = pe.done(last)
                h.release(t)
                state["last"] = t

            def block(blk):
                xt = yield from xt_ring.take()
                xT = split_cols(xt.ap, KD)
                t_x = yield from norm_transpose(blk, xn_ring, xT, xt.free)
                got = []
                yield from router(xT, t_x, got)
                ct, t_ct = got[0]
                turn = yield from acc_turn.take()
                acc = yield from psum.take(2)
                state = {}
                yield from interleave([hidden(f, xT, ct.ap, t_ct, acc, state) for f in range(NF0)], 2)
                xt.release(state["last"])
                ct.release(state["last"])
                xs = x_all[:, blk * BLK * D:(blk + 1) * BLK * D]
                t = dve.done(dve.after(state["last"]).scalar_tensor_tensor(xs, acc.ap, gates[:, 4:5], xs, ALU.mult, ALU.add))
                acc.release(t)
                turn.release()
                for b in range(blk * BLK, (blk + 1) * BLK):
                    x_ready[b] = [t]

            run(interleave([block(i) for i in range(NBLK)], 2))

        R1 = region_b
        l1_wq, l1_wk, l1_wv = (split_cols(R1.f32(KD * D), KD) for _ in range(3))
        l1_wo = split_cols(R1.f32(8 * D), 8)
        l1_gu = R1.f32(E1 * KD * 2 * D).rearrange("p (e k n) -> p e k n", e=E1, k=KD)
        l1_down = R1.f32(E1 * KD * D).rearrange("p (e k n) -> p e k n", e=E1, k=KD)
        l1_cos, l1_sin, l1_cosq, l1_sinq = (R1.f32(S) for _ in range(4))
        l1_gate = R1.f32(H1)
        l1_lane = lane("l1_weights_loaded")

        def load_l1_weights():
            t_zero = dve.done(dve.api.memset(l1_wo, 0.0))
            for n, dst in (("l1_wq", l1_wq), ("l1_wk", l1_wk), ("l1_wv", l1_wv)):
                load(l1_lane, dst, chunks_of(A[n]))
            for n, dst in (("l1_cos", l1_cos), ("l1_sin", l1_sin), ("l1_cosq", l1_cosq), ("l1_sinq", l1_sinq)):
                load(l1_lane, dst, A[n])
            load(l1_lane, l1_gate, A["l1_gate"].broadcast_to([P, H1]))
            wo = A["l1_wo"].rearrange("(j q d) o -> q d j o", q=4, d=HD1)
            for q in range(4):
                load(l1_lane, l1_wo[32 * q:32 * q + HD1], wo[q], t_zero)
            for e in range(E1):
                load(l1_lane, l1_gu[:, e], chunks_of(A["l1_gu"][e]))
                load(l1_lane, l1_down[:, e], chunks_of(A["l1_down"][e]))

        def store_parts(parts, dst, blk, t):
            p5 = parts.ap.rearrange("p (i c b n) -> p i c b n", i=3, c=KD, b=BLK)
            for i in range(BLK):
                for c in range(KD):
                    tok = parts.lane.start(sp, dst[blk * BLK + i, :, c * P:(c + 1) * P, :].rearrange("i r t -> r i t"), p5[:, :, c, i, :], t)
            return tok

        def load_stack(st, src, which, hd, *waits):
            for i in range(NT):
                st.lane.start(sp, st.ap[hd * i:hd * i + hd], src[which[i]].rearrange("(d h) t -> d (h t)", d=hd), st.free, *waits)
            return st.lane.token()

        def l1_attention():
            W = Arena(sbuf, WORK_AT, COLS)
            V = Arena(sbuf, A_AT, B_AT)
            l1_gate_t = act.done(act.after(l1_lane.token()).activation(l1_gate, l1_gate, ACT.Tanh))
            xn_ring = Ring([Buf(W.f32(BLK * D)) for _ in range(1)])
            xt_ring = Ring([Buf(W.f32(KD * BANK)) for _ in range(1)])
            rope_ring = Ring([Buf(W.f32(2 * KD * BANK)) for _ in range(1)])
            part_ring = Ring([Buf(W.bf16(3 * KD * BANK), lane(f"l1_parts_stored_{i}")) for i in range(2)])
            d_ring = Ring([Buf(W.f32(8 * P)) for _ in range(4)])
            e_ring = Ring([Buf(W.f32(8 * P)) for _ in range(2)])
            m_ring = Ring([Buf(W.f32(8)) for _ in range(4)])
            t_ring = Ring([Buf(W.f32(D + 8)) for _ in range(2)])
            mask_ring = Ring([Buf(W.f32(S), lane(f"mask_loaded_{i}")) for i in range(2)])
            q_ring, k_ring, a_ring = ([Buf(V.bf16(H1 * S), lane(f"l1_{n}_stack_loaded_{i}")) for i in range(m)]
                                      for n, m in (("q", 2), ("k", 1), ("a", 1)))
            for buf in q_ring + k_ring + a_ring:
                buf.free = [dve.done(dve.api.memset(buf.ap[0:96], 0.0))]
            q_ring, k_ring, a_ring = Ring(q_ring), Ring(k_ring), Ring(a_ring)
            v_ring = [Buf(V.f32(H1 * 32)) for _ in range(4)]
            for buf in v_ring:
                t = dve.done(dve.api.memset(buf.ap, 0.0))
                buf.free = [dve.done(dve.after(t).memset(split_cols(buf.ap, H1)[:, :, HD1:HD1 + 1], 1.0))]
            v_ring = Ring(v_ring)
            at_ring = Ring([Buf(V.f32(8 * P)) for _ in range(1)] + [Buf(W.f32(8 * P)) for _ in range(3)])
            q_dram, k_dram, a_dram = (dram(f"l1_{n}_parts", [NB, 3, D, S], BF16) for n in "qka")

            def project(w, src, waits, kind, dst, blk, out):
                ps = yield from psum.take(2)
                for c in range(KD):
                    for k in range(KD):
                        last = pe.after(waits, l1_lane.token(), ps.free).matmul(
                            ps.ap[:, c * BANK:(c + 1) * BANK], w[:, k, c * P:(c + 1) * P], src[:, k, :], start=(k == 0), stop=(k == KD - 1))
                t = pe.done(last)
                yield True
                r = yield from rope_ring.take()
                val, tmp = r.ap[:, 0:2 * BANK], r.ap[:, 2 * BANK:4 * BANK]
                if kind == "a":
                    t = dve.done(dve.after(t, r.free).tensor_copy(val, ps.ap))
                else:
                    cos, sin = (l1_cosq, l1_sinq) if kind == "q" else (l1_cos, l1_sin)
                    bc = lambda a: a.unsqueeze(1).broadcast_to([P, BLK, S])
                    half = [split_cols(ps.ap[:, c * BANK:(c + 1) * BANK], BLK) for c in range(2)]
                    v2 = [split_cols(val[:, c * BANK:(c + 1) * BANK], BLK) for c in range(2)]
                    m2 = [split_cols(tmp[:, c * BANK:(c + 1) * BANK], BLK) for c in range(2)]
                    dve.after(t, r.free)
                    for c in range(2):
                        dve.done(dve.api.tensor_tensor(v2[c], half[c], bc(cos), ALU.mult))
                        t = dve.done(dve.api.tensor_tensor(m2[c], half[1 - c], bc(sin), ALU.mult))
                ps.release(t)
                if kind != "a":
                    t1 = dve.done(dve.after(t).tensor_tensor(v2[0], v2[0], m2[0], ALU.subtract))
                    t = dve.done(dve.after(t1).tensor_tensor(v2[1], v2[1], m2[1], ALU.add))
                yield True
                parts = yield from part_ring.take()
                t = split3(val, parts.ap.rearrange("p (i n) -> p i n", i=3), tmp, t, parts.free)
                r.release(t)
                t = store_parts(parts, dst, blk, t)
                parts.release(t)
                out[kind] = t

            def values_of(src, w, waits, v, kind):
                ps = yield from psum.take(1)
                for k in range(KD):
                    last = pe.after(waits, ps.free).matmul(ps.ap[:, 0:D], src[:, k, :], w[:, k, :], start=(k == 0), stop=(k == KD - 1))
                t = pe.done(last)
                dst, got = split_cols(v.ap, H1)[:, :, 0:HD1], split_cols(ps.ap[:, 0:D], H1)
                if kind == "a":
                    t2 = dve.done(dve.after(t, v.free, l1_gate_t).tensor_tensor(dst, got, l1_gate.unsqueeze(2).broadcast_to([P, H1, HD1]), ALU.mult))
                else:
                    t2 = dve.done(dve.after(t, v.free).tensor_copy(dst, got))
                ps.release(t2)
                return t, t2

            def unit(s, q_st, k_st, t_st, mask, t_mask, v, t_v, at, state, kind):
                m = yield from m_ring.take()
                d = yield from d_ring.take()
                ps = yield from psum.take(2)
                q3, k3 = split_cols(q_st.ap, H1), split_cols(k_st.ap, H1)
                s3, d3 = split_cols(ps.ap, 8), split_cols(d.ap, 8)
                for j in range(8):
                    last = pe.after(t_st, ps.free).matmul(s3[:, j], q3[0:96, 8 * s + j, :], k3[0:96, 8 * s + j, :], start=True, stop=True)
                t = pe.done(last)
                state["scored"] = t
                yield True
                mb = m.ap.unsqueeze(2).broadcast_to([P, 8, S])
                if kind == "k":
                    t = dve.done(dve.after(t, t_mask, d.free).tensor_tensor(d3, s3, mask.ap.unsqueeze(1).broadcast_to([P, 8, S]), ALU.add))
                    ps.release(t)
                    state["masked"] = t
                    t = dve.done(dve.after(t, m.free).tensor_reduce(m.ap, d3, AXX, ALU.max))
                    t = dve.done(dve.after(t).tensor_tensor(d3, d3, mb, ALU.subtract))
                else:
                    t = dve.done(dve.after(t, m.free).tensor_reduce(m.ap, s3, AXX, ALU.max))
                    t = dve.done(dve.after(t, d.free).tensor_tensor(d3, s3, mb, ALU.subtract))
                    ps.release(t)
                m.release(t)
                yield True
                e = yield from e_ring.take()
                pt = yield from psum.take(2)
                p3 = split_cols(pt.ap, 8)
                t = transposes([(d3[:, j], p3[:, j]) for j in range(8)], pt, ident, t, pt.free)
                d.release(t)
                yield True
                t = act.done(act.after(t, e.free).activation(e.ap, pt.ap, ACT.Exp))
                pt.release(t)
                yield True
                av = yield from psum.take(1)
                e3, v3 = split_cols(e.ap, 8), split_cols(v.ap, H1)
                for j in range(2):
                    for q in range(4):
                        last = pe.after(t, t_v, av.free).matmul(av.ap[32 * q:32 * q + 32, j * P:(j + 1) * P], v3[:, 8 * s + 4 * j + q, :],
                                                                e3[:, 4 * j + q, :], start=True, stop=True, tile_position=(0, 32 * q))
                t = pe.done(last)
                e.release(t)
                state["valued"] = t
                yield True
                state[s] = yield from normalise(av, D, HD1, at.ap[:, s * D:(s + 1) * D], t, at.free, t_ring)

            def tile(b, xT, t_x, i, sent):
                mk = yield from mask_ring.take()
                t_m = load(mk.lane, mk.ap, A["mask1"][b], *mk.free)
                t_m = dve.done(dve.after(t_m).tensor_scalar(mk.ap, mk.ap, LOWEST, None, ALU.max))
                vs = yield from v_ring.take()
                va = yield from v_ring.take()
                tp, t_vs = yield from values_of(xT[:, :, i * P:(i + 1) * P], l1_wv, t_x, vs, "k")
                _, t_va = yield from values_of(ctxT[:, :, b * S:(b + 1) * S], l1_wv, None, va, "a")
                sent["values"] = tp
                while "q" not in sent or "k" not in sent or "a" not in sent:
                    yield False
                q_st = yield from q_ring.take()
                k_st = yield from k_ring.take()
                a_st = yield from a_ring.take()
                t_q = load_stack(q_st, q_dram[b], PART_Q, HD1, sent["q"])
                t_k = load_stack(k_st, k_dram[b], PART_K, HD1, sent["k"])
                t_a = load_stack(a_st, a_dram[b], PART_K, HD1, sent["a"])
                yield True
                at_s = yield from at_ring.take()
                at_a = yield from at_ring.take()
                ss, sa = {}, {}
                yield from interleave([unit(s, q_st, k_st, [t_q, t_k], mk, t_m, vs, t_vs, at_s, ss, "k") for s in range(4)], 3)
                k_st.release(ss["scored"])
                mk.release(ss["masked"])
                vs.release(ss["valued"])
                yield from interleave([unit(s, q_st, a_st, [t_q, t_a], mk, t_m, va, t_va, at_a, sa, "a") for s in range(4)], 3)
                q_st.release(ss["scored"], sa["scored"])
                a_st.release(sa["scored"])
                va.release(sa["valued"])
                t = pool.done(pool.after([ss[s] for s in range(4)], [sa[s] for s in range(4)]).tensor_tensor(at_s.ap, at_s.ap, at_a.ap, ALU.add))
                at_a.release(t)
                yield True
                po = yield from psum.take(1)
                a3 = split_cols(at_s.ap, 8)
                for j in range(8):
                    last = pe.after(t, po.free).matmul(po.ap[:, 0:D], a3[:, j], l1_wo[:, j, :], start=(j == 0), stop=(j == 7))
                t = pe.done(last)
                at_s.release(t)
                yield True
                t = dve.done(dve.after(t).scalar_tensor_tensor(X[b], po.ap[:, 0:D], gates[:, 1:2], X[b], ALU.mult, ALU.add))
                po.release(t)
                x_ready[b] = [t]

            def block(blk):
                xt = yield from xt_ring.take()
                xT = split_cols(xt.ap, KD)
                t_x = yield from norm_transpose(blk, xn_ring, xT, xt.free)
                cT = ctxT[:, :, blk * BANK:(blk + 1) * BANK]
                sent = {}

                def projections():
                    yield from project(l1_wq, xT, t_x, "q", q_dram, blk, sent)
                    yield from project(l1_wk, xT, t_x, "k", k_dram, blk, sent)
                    sent["projected"] = pe.last()
                    yield from project(l1_wk, cT, t_x, "a", a_dram, blk, sent)
                yield from interleave([projections()] + [tile(blk * BLK + i, xT, t_x, i, sent) for i in range(BLK)], 3)
                xt.release(sent["projected"], sent["values"])

            run(interleave([block(i) for i in range(NBLK)], 1))

        def l1_ffn():
            load_l2_weights()
            W = Arena(sbuf, WORK_AT, COLS)
            xn_ring = Ring([Buf(W.f32(BLK * D)) for _ in range(2)])
            xT = split_cols(W.f32(KD * NB * S), KD)
            yT = split_cols(W.f32(KD * NB * S), KD)
            th_ring = Ring([Buf(W.f32(BANK)) for _ in range(3)])
            h_ring = Ring([Buf(W.f32(KD * BANK)) for _ in range(2)])
            of_expert = lambda a, k, e: a[:, k, :].rearrange("p (n e) -> p n e", e=E1)[:, :, e]
            t_x = []

            def norm(blk):
                t_x.append((yield from norm_transpose(blk, xn_ring, xT[:, :, blk * BANK:(blk + 1) * BANK], None)))
            run(interleave([norm(i) for i in range(NBLK)], 2))

            def half(e, c, h, h_free, out):
                ps = yield from psum.take(2)
                for n in range(2):
                    for k in range(KD):
                        last = pe.after(t_x, l1_lane.token(), ps.free).matmul(
                            ps.ap[:, n * BANK:(n + 1) * BANK], l1_gu[:, e, k, n * D + c * P:n * D + (c + 1) * P], of_expert(xT, k, e),
                            start=(k == 0), stop=(k == KD - 1))
                t = pe.done(last)
                yield True
                th = yield from th_ring.take()
                t = act.done(act.after(t, th.free).activation(th.ap, ps.ap[:, 0:BANK], ACT.Tanh, scale=0.5))
                t = dve.done(dve.after(t).scalar_tensor_tensor(th.ap, th.ap, 1.0, ps.ap[:, 0:BANK], ALU.add, ALU.mult))
                t = dve.done(dve.after(t, h_free).scalar_tensor_tensor(h[:, c], th.ap, 0.5, ps.ap[:, BANK:2 * BANK], ALU.mult, ALU.mult))
                ps.release(t)
                th.release(t)
                out.append(t)

            done_y = []

            def expert(e):
                h = yield from h_ring.take()
                h2, got = split_cols(h.ap, KD), []
                yield from interleave([half(e, c, h2, h.free, got) for c in range(KD)], 2)
                for c in range(KD):
                    ps = yield from psum.take(1)
                    for k in range(KD):
                        last = pe.after(got, ps.free).matmul(ps.ap, l1_down[:, e, k, c * P:(c + 1) * P], h2[:, k], start=(k == 0), stop=(k == KD - 1))
                    t_m = pe.done(last)
                    t = act.done(act.after(t_m).activation(of_expert(yT, c, e), ps.ap, ACT.Copy))
                    ps.release(t)
                    done_y.append(t)
                h.release(t_m)

            run(interleave([expert(e) for e in range(E1)], 2))

            def back(blk):
                ps = yield from psum.take(2)
                p4 = ps.ap.rearrange("p (b k n) -> p b k n", b=BLK, k=KD)
                t = transposes([(yT[:, k, (blk * BLK + i) * P:(blk * BLK + i + 1) * P], p4[:, i, k]) for i in range(BLK) for k in range(KD)],
                               ps, ident, done_y, ps.free)
                yield True
                xs = x_all[:, blk * BLK * D:(blk + 1) * BLK * D]
                t = dve.done(dve.after(t).scalar_tensor_tensor(xs, ps.ap, gates[:, 5:6], xs, ALU.mult, ALU.add))
                ps.release(t)
                for b in range(blk * BLK, (blk + 1) * BLK):
                    x_ready[b] = [t]
            run(interleave([back(i) for i in range(NBLK)], 2))

        R2 = Arena(sbuf, A_AT, B_AT)
        l2_wq, l2_wk, l2_wv = (split_cols(R2.f32(KD * D), KD) for _ in range(3))
        l2_wo = split_cols(R2.f32(4 * D), 4)
        l2_bq, l2_bk = R2.f32(KD), R2.f32(KD)
        l2_bv, l2_bo, l2_gamma, l2_beta = (R2.f32(D) for _ in range(4))
        l2_rs = R2.f32(1)
        l2_att, l2_attb = R2.f32(NB), R2.f32(NB)
        l2_mask = R2.f32(NB).bitcast(I32)
        l2_raw = [split_cols(R2.f32(KD * F2), KD) for _ in range(2)] + [split_cols(R2.f32(NF2 * D), NF2)]
        l2_q = [split_cols(R2.bf16(KD * F2), KD) for _ in range(2)] + [split_cols(R2.bf16(NF2 * D), NF2)]
        l2_lane = lane("l2_weights_loaded")

        def load_l2_weights():
            t_zero = dve.done(dve.api.memset(l2_wo, 0.0))
            for n, dst in (("l2_wqT", l2_wq), ("l2_wkT", l2_wk), ("l2_wvT", l2_wv), ("l2_wgT", l2_raw[0]), ("l2_wuT", l2_raw[1])):
                load(l2_lane, dst, chunks_of(A[n]))
            full = F2 // P
            load(l2_lane, l2_raw[2][:, 0:full], chunks_of(A["l2_wdT"][0:full * P], full))
            load(l2_lane, l2_raw[2][0:F2 - full * P, full], A["l2_wdT"][full * P:])
            load(l2_lane, l2_bq, A["l2_bq"])
            load(l2_lane, l2_bk, A["l2_bk"])
            for n, dst in enumerate((l2_bv, l2_bo, l2_gamma, l2_beta)):
                load(l2_lane, dst, A["l2_rows"][n:n + 1].broadcast_to([P, D]))
            load(l2_lane, l2_rs, A["l2_rs"].broadcast_to([P, 1]))
            load(l2_lane, l2_mask, A["mask2T"])
            wo = A["l2_woT"].rearrange("(j q d) o -> q d j o", q=4, d=HD2)
            for q in range(4):
                load(l2_lane, l2_wo[32 * q:32 * q + HD2], wo[q], t_zero)

        def l2_attention():
            load_l3_weights()
            W = Arena(sbuf, WORK_AT, COLS)
            t = dve.done(dve.after(l2_lane.token()).tensor_scalar(l2_rs, l2_rs, 0.0, 0.3, ALU.max, ALU.min))
            t = dve.done(dve.api.tensor_scalar(l2_att, l2_mask, 0.5, None, ALU.is_gt))
            t_att = dve.done(dve.after(t).tensor_scalar(l2_attb, l2_att, 1.0, 50.0, ALU.subtract, ALU.mult))
            xn_ring = Ring([Buf(W.f32(BLK * D)) for _ in range(1)])
            xt_ring = Ring([Buf(W.f32(KD * BANK)) for _ in range(1)])
            val_ring = Ring([Buf(W.f32(2 * KD * BANK)) for _ in range(1)])
            part_ring = Ring([Buf(W.bf16(3 * KD * BANK), lane(f"l2_parts_stored_{i}")) for i in range(1)])
            d_ring = Ring([Buf(W.f32(8 * P)) for _ in range(3)])
            t_ring = Ring([Buf(W.f32(D + 8)) for _ in range(2)])
            q_ring, k_ring = (Ring([Buf(W.bf16(H2 * S), lane(f"l2_{n}_stack_loaded_{i}")) for i in range(2)]) for n in "qk")
            v_ring = [Buf(W.f32(H2 * 32)) for _ in range(2)]
            for buf in v_ring:
                t = dve.done(dve.api.memset(buf.ap, 0.0))
                buf.free = [dve.done(dve.after(t).memset(split_cols(buf.ap, H2)[:, :, HD2:HD2 + 1], 1.0))]
            v_ring = Ring(v_ring)
            at_ring = Ring([Buf(W.f32(4 * P)) for _ in range(2)])
            y_ring = Ring([Buf(W.f32(D + 16)) for _ in range(2)])
            q_dram, k_dram = (dram(f"l2_{n}_parts", [NB, 3, D, S], BF16) for n in "qk")

            def project(w, bias, scale, src, waits, dst, blk, sent, name):
                ps = yield from psum.take(2)
                for c in range(KD):
                    for k in range(KD):
                        last = pe.after(waits, l2_lane.token(), ps.free).matmul(
                            ps.ap[:, c * BANK:(c + 1) * BANK], w[:, k, c * P:(c + 1) * P], src[:, k, :], start=(k == 0), stop=(k == KD - 1))
                t_m = pe.done(last)
                yield True
                r = yield from val_ring.take()
                val, tmp = r.ap[:, 0:2 * BANK], r.ap[:, 2 * BANK:4 * BANK]
                for c in range(KD):
                    t = dve.done(dve.after(t_m, r.free).tensor_scalar(val[:, c * BANK:(c + 1) * BANK], ps.ap[:, c * BANK:(c + 1) * BANK],
                                                                     bias[:, c:c + 1], scale, ALU.add, ALU.mult))
                ps.release(t)
                parts = yield from part_ring.take()
                t = split3(val, parts.ap.rearrange("p (i n) -> p i n", i=3), tmp, t, parts.free)
                r.release(t)
                t = store_parts(parts, dst, blk, t)
                parts.release(t)
                sent[name], sent["projected"] = t, t_m

            def unit(b, s, q_st, k_st, t_st, v, t_v, at, state):
                d = yield from d_ring.take()
                ps = yield from psum.take(2)
                q3, k3 = split_cols(q_st.ap, H2), split_cols(k_st.ap, H2)
                s3, d3 = split_cols(ps.ap, 8), split_cols(d.ap, 8)
                for j in range(8):
                    last = pe.after(t_st, ps.free).matmul(s3[:, j], k3[0:96, 8 * s + j, :], q3[0:96, 8 * s + j, :], start=True, stop=True)
                t = pe.done(last)
                state["scored"] = t
                yield True
                t = dve.done(dve.after(t, d.free).tensor_scalar(d.ap, ps.ap, 50.0, -50.0, ALU.min, ALU.max))
                ps.release(t)
                t = act.done(act.after(t, t_att).activation(d.ap, d.ap, ACT.Exp, bias=l2_attb[:, b:b + 1], scale=l2_att[:, b:b + 1]))
                yield True
                av = yield from psum.take(1)
                v3 = split_cols(v.ap, H2)
                for j in range(2):
                    for q in range(4):
                        last = pe.after(t, t_v, av.free).matmul(av.ap[32 * q:32 * q + 32, j * P:(j + 1) * P], v3[:, 8 * s + 4 * j + q, :],
                                                                d3[:, 4 * j + q, :], start=True, stop=True, tile_position=(0, 32 * q))
                t = pe.done(last)
                d.release(t)
                state["valued"] = t
                yield True
                state[s] = yield from normalise(av, D, HD2, at.ap[:, s * D:(s + 1) * D], t, at.free, t_ring)

            def tile(b, sent):
                v = yield from v_ring.take()
                ps = yield from psum.take(1)
                for k in range(KD):
                    last = pe.after(l2_lane.token(), ps.free).matmul(ps.ap[:, 0:D], ctxT[:, k, b * S:(b + 1) * S], l2_wv[:, k, :],
                                                                    start=(k == 0), stop=(k == KD - 1))
                t = pe.done(last)
                t_v = dve.done(dve.after(t, v.free).tensor_tensor(split_cols(v.ap, H2)[:, :, 0:HD2], split_cols(ps.ap[:, 0:D], H2),
                                                                 split_cols(l2_bv, H2), ALU.add))
                ps.release(t_v)
                while "q" not in sent or "k" not in sent:
                    yield False
                q_st = yield from q_ring.take()
                k_st = yield from k_ring.take()
                t_q = load_stack(q_st, q_dram[b], PART_Q, HD2, sent["q"])
                t_k = load_stack(k_st, k_dram[b], PART_K, HD2, sent["k"])
                yield True
                at = yield from at_ring.take()
                state = {}
                yield from interleave([unit(b, s, q_st, k_st, [t_q, t_k], v, t_v, at, state) for s in range(2)], 2)
                q_st.release(state["scored"])
                k_st.release(state["scored"])
                v.release(state["valued"])
                po = yield from psum.take(1)
                for j in range(4):
                    last = pe.after(state[0], state[1], po.free).matmul(po.ap[:, 0:D], at.ap[:, j * P:(j + 1) * P], l2_wo[:, j, :],
                                                                        start=(j == 0), stop=(j == 3))
                t = pe.done(last)
                at.release(t)
                yield True
                y = yield from y_ring.take()
                d, s = y.ap[:, 0:D], y.ap[:, D:D + 16]
                t = dve.done(dve.after(t, y.free).tensor_tensor(d, po.ap[:, 0:D], l2_bo, ALU.add))
                po.release(t)
                t = dve.done(dve.after(t).tensor_scalar(d, d, l2_rs, None, ALU.mult))
                t = dve.done(dve.after(t).bn_stats(s[:, 0:6], d))
                t = dve.done(dve.after(t).bn_aggr(s[:, 6:8], s[:, 0:6]))
                t = rstd(s[:, 8:9], s[:, 7:8], EPS_LN, 1.0, t)
                yield True
                t = dve.done(dve.after(t).tensor_scalar(d, d, s[:, 6:7], s[:, 8:9], ALU.subtract, ALU.mult))
                t = dve.done(dve.after(t).tensor_tensor(d, d, l2_gamma, ALU.mult))
                t = dve.done(dve.after(t).tensor_tensor(d, d, l2_beta, ALU.add))
                t = dve.done(dve.after(t).scalar_tensor_tensor(X[b], d, gates[:, 2:3], X[b], ALU.mult, ALU.add))
                y.release(t)
                x_ready[b] = [t]

            def block(blk):
                xt = yield from xt_ring.take()
                xT = split_cols(xt.ap, KD)
                t_x = yield from norm_transpose(blk, xn_ring, xT, xt.free)
                sent = {}

                def projections():
                    yield from project(l2_wk, l2_bk, 1.0, ctxT[:, :, blk * BANK:(blk + 1) * BANK], t_x, k_dram, blk, sent, "k")
                    yield from project(l2_wq, l2_bq, 0.25, xT, t_x, q_dram, blk, sent, "q")
                yield from interleave([projections()] + [tile(blk * BLK + i, sent) for i in range(BLK)], 3)
                xt.release(sent["projected"])

            run(interleave([block(i) for i in range(NBLK)], 2))

        def l2_ffn():
            W = Arena(sbuf, WORK_AT, COLS)
            ones = W.f32(P)
            wsum, wscale = W.f32(16), W.f32(16)
            scratch = W.f32(NF2 * D)
            t_one = dve.done(dve.api.memset(ones, 1.0))
            t0 = dve.done(dve.api.memset(wsum, 0.0))
            raws = [(l2_raw[0], slice(0, P)), (l2_raw[1], slice(0, P)), (l2_raw[2][:, 0:NF2 - 1], slice(0, P)), (l2_raw[2][:, NF2 - 1], slice(0, F2 % P))]
            t = t0
            for n, (w, rows) in enumerate(raws):
                flat = w[rows] if n == 3 else w[rows].rearrange("p k n -> p (k n)")
                t = dve.done(dve.after(t).tensor_reduce(wsum[rows, n:n + 1], flat, AXX, ALU.add, apply_absolute_value=True))
            t = dve.done(dve.after(t).tensor_tensor(wsum[:, 2:3], wsum[:, 2:3], wsum[:, 3:4], ALU.add))
            got = []

            def total():
                ps = yield from psum.take(1)
                tm = pe.done(pe.after(t, t_one, ps.free).matmul(ps.ap[:, 0:4], ones, wsum[:, 0:4], start=True, stop=True))
                tv = dve.done(dve.after(tm).tensor_scalar(wscale[:, 0:4], ps.ap[:, 0:4], 1.0 / (F2 * D), 1e-5, ALU.mult, ALU.max))
                ps.release(tv)
                got.append(dve.done(dve.after(tv).reciprocal(wscale[:, 4:8], wscale[:, 0:4])))
            run(total())
            t_sc = got[0]
            t_w = []
            for n in range(3):
                parts = [(l2_raw[n], l2_q[n])] if n < 2 else [(l2_raw[2][:, 0:NF2 - 1], l2_q[2][:, 0:NF2 - 1]), (l2_raw[2][0:F2 % P, NF2 - 1], l2_q[2][0:F2 % P, NF2 - 1])]
                for w, q in parts:
                    rows = w.shape[0]
                    t = dve.done(dve.after(t_sc).tensor_scalar(w, w, wscale[0:rows, 4 + n:5 + n], ROUND, ALU.mult, ALU.add))
                    t = dve.done(dve.after(t).tensor_scalar(w, w, ROUND, -1.0, ALU.subtract, ALU.max))
                    t = dve.done(dve.after(t).tensor_scalar(q, w, 1.0, None, ALU.min))
                    t_w.append(t)
            xn_ring = Ring([Buf(W.f32(D)) for _ in range(3)])
            xq_ring = Ring([Buf(W.bf16(2 * D)) for _ in range(2)])
            s_ring = Ring([Buf(W.f32(16)) for _ in range(3)])
            th_ring = Ring([Buf(W.f32(F2)) for _ in range(2)])
            h_ring = Ring([Buf(W.f32(F2)) for _ in range(2)])
            hq_ring = Ring([Buf(W.bf16(NF2 * P)) for _ in range(2)])
            ht_ring = Ring([Buf(W.bf16(NF2 * P)) for _ in range(2)])
            HF = F2 // 2

            def tile(b):
                xn = yield from xn_ring.take()
                s = yield from s_ring.take()
                c = lambda i: s.ap[:, i:i + 1]
                t = yield from layer_norm(X[b], xn.ap, x_ready[b], xn.free)
                yield True
                t = dve.done(dve.after(t, s.free).tensor_reduce(c(0), xn.ap, AXX, ALU.max, apply_absolute_value=True))
                t = dve.done(dve.after(t).tensor_scalar(c(0), c(0), 1e-5, None, ALU.max))
                t = dve.done(dve.after(t).reciprocal(c(1), c(0)))
                t = dve.done(dve.after(t).tensor_scalar(c(1), c(1), 127.0, None, ALU.mult))
                t = dve.done(dve.after(t).tensor_scalar(xn.ap, xn.ap, c(1), ROUND, ALU.mult, ALU.add))
                t = dve.done(dve.after(t).tensor_scalar(xn.ap, xn.ap, ROUND, 127.0, ALU.subtract, ALU.min))
                xq = yield from xq_ring.take()
                xqa, xT = xq.ap[:, 0:D], split_cols(xq.ap[:, D:2 * D], KD)
                t = dve.done(dve.after(t, xq.free).tensor_scalar(xqa, xn.ap, -128.0, None, ALU.max))
                xn.release(t)
                t_a = dve.done(dve.api.tensor_scalar(c(2), c(0), wscale[:, 0:1], 1.0 / 127.0, ALU.mult, ALU.mult))
                t_b = dve.done(dve.api.tensor_scalar(c(3), c(0), wscale[:, 1:2], 1.0 / 127.0, ALU.mult, ALU.mult))
                t_c = dve.done(dve.after(t_a).tensor_scalar(c(4), c(2), 0.5, None, ALU.mult))
                t_d = dve.done(dve.after(t_b, t_c).tensor_tensor(c(5), c(4), c(3), ALU.mult))
                yield True
                px = yield from psum.take(1)
                pb = px.ap.bitcast(BF16)[:, 0:D]
                t = transposes([(xqa[:, k * P:(k + 1) * P], pb[:, k * P:(k + 1) * P]) for k in range(KD)], px, ident_bf, t, px.free)
                t = act.done(act.after(t).activation(xT, split_cols(pb, KD), ACT.Copy))
                px.release(t)
                yield True
                pg = yield from psum.take(2)
                pu = yield from psum.take(2)
                for ps, w in ((pg, l2_q[0]), (pu, l2_q[1])):
                    for h in range(2):
                        for k in range(KD):
                            last = pe.after(t, t_w, ps.free).matmul(ps.ap[:, h * BANK:h * BANK + HF], xT[:, k], w[:, k, h * HF:(h + 1) * HF],
                                                                    start=(k == 0), stop=(k == KD - 1))
                t = pe.done(last)
                xq.release(t)
                yield True
                th = yield from th_ring.take()
                hb = yield from h_ring.take()
                g2, u2 = (split_cols(p.ap, 2)[:, :, 0:HF] for p in (pg, pu))
                th2, h2 = split_cols(th.ap, 2), split_cols(hb.ap, 2)
                t = act.done(act.after(t, t_c, th.free).activation(th2, g2, ACT.Tanh, scale=c(4)))
                t = dve.done(dve.after(t, hb.free).scalar_tensor_tensor(h2, th2, 1.0, g2, ALU.add, ALU.mult))
                th.release(t)
                pg.release(t)
                t = dve.done(dve.after(t).tensor_tensor(h2, h2, u2, ALU.mult))
                pu.release(t)
                t = dve.done(dve.after(t).tensor_reduce(c(6), hb.ap, AXX, ALU.max, apply_absolute_value=True))
                t = dve.done(dve.after(t, t_d).tensor_scalar(c(6), c(6), c(5), 1e-5, ALU.mult, ALU.max))
                t = dve.done(dve.after(t).reciprocal(c(7), c(6)))
                t = dve.done(dve.after(t).tensor_scalar(c(7), c(7), c(5), 127.0, ALU.mult, ALU.mult))
                t_o = dve.done(dve.api.tensor_scalar(c(8), c(6), wscale[:, 2:3], 1.0 / 127.0, ALU.mult, ALU.mult))
                t_o = dve.done(dve.after(t_o).tensor_scalar(c(8), c(8), gates[:, 6:7], None, ALU.mult))
                t = dve.done(dve.after(t).tensor_scalar(hb.ap, hb.ap, c(7), ROUND, ALU.mult, ALU.add))
                hq = yield from hq_ring.take()
                t = dve.done(dve.after(t).tensor_scalar(hb.ap, hb.ap, ROUND, 127.0, ALU.subtract, ALU.min))
                t = dve.done(dve.after(t, hq.free).tensor_scalar(hq.ap[:, 0:F2], hb.ap, -128.0, None, ALU.max))
                hb.release(t)
                yield True
                pt = yield from psum.take(1)
                pb = pt.ap.bitcast(BF16)
                t = transposes([(hq.ap[:, f * P:min(F2, (f + 1) * P)], pb[0:min(P, F2 - f * P), f * P:(f + 1) * P]) for f in range(NF2)],
                               pt, ident_bf, t, pt.free)
                hq.release(t)
                ht = yield from ht_ring.take()
                full = (NF2 - 1) * P
                t1 = act.done(act.after(t, ht.free).activation(ht.ap[:, 0:full], pb[:, 0:full], ACT.Copy))
                t2 = act.done(act.api.activation(ht.ap[0:F2 - full, full:], pb[0:F2 - full, full:full + P], ACT.Copy))
                pt.release(t1, t2)
                yield True
                po = yield from psum.take(1)
                for f in range(NF2):
                    M = min(P, F2 - f * P)
                    last = pe.after(t1, t2, po.free).matmul(po.ap[:, 0:D], ht.ap[0:M, f * P:(f + 1) * P], l2_q[2][0:M, f, :],
                                                            start=(f == 0), stop=(f == NF2 - 1))
                t = pe.done(last)
                ht.release(t)
                yield True
                t = dve.done(dve.after(t, t_o).scalar_tensor_tensor(X[b], po.ap[:, 0:D], c(8), X[b], ALU.mult, ALU.add))
                po.release(t)
                s.release(t)
                x_ready[b] = [t]

            run(interleave([tile(b) for b in range(NB)], 2))

        R3 = Arena(sbuf, B_AT, WORK_AT)
        l3_wq = split_cols(R3.f32(KD * H3 * HD3), KD)
        l3_wk, l3_wv = (split_cols(R3.f32(KD * G3 * HD3), KD) for _ in range(2))
        l3_wo = split_cols(R3.f32(H3 * D), H3)
        l3_w = R3.f32(4)
        l3_lane = lane("l3_weights_loaded")
        x_slots = dram("l3_slot_inputs", [NSLOT, D], F32)
        y_slots = dram("l3_slot_outputs", [NSLOT + P, D], F32)
        slot_lane = lane("l3_slots_cleared")

        def load_l3_weights():
            load(l3_lane, l3_wq, chunks_of(A["l3_wq"]))
            load(l3_lane, l3_wk, chunks_of(A["l3_wk"]))
            load(l3_lane, l3_wv, chunks_of(A["l3_wv"]))
            load(l3_lane, l3_wo, chunks_of(A["l3_wo"], H3))
            load(l3_lane, l3_w[:, 0:2], A["l3_qkw"])

        def l3_attention():
            W = Arena(sbuf, WORK_AT, COLS)
            V = Arena(sbuf, A_AT, B_AT)
            ones = W.f32(1)
            t_one = dve.done(dve.api.memset(ones, 1.0))
            t_w = dve.done(dve.after(l3_lane.token()).tensor_scalar(l3_w[:, 2:3], l3_w[:, 0:1], l3_w[:, 1:2], float(HD3) ** -0.5, ALU.mult, ALU.mult))
            xn_ring = Ring([Buf(W.f32(BLK * D)) for _ in range(1)])
            xt_ring = Ring([Buf(W.f32(KD * BANK)) for _ in range(1)])
            q_ring = Ring([Buf(V.f32(H3 * BANK)), Buf(W.f32(H3 * BANK))])
            sq_ring = Ring([Buf(W.f32(BANK)) for _ in range(2)])
            rq_ring = Ring([Buf(W.f32(BLK * H3)) for _ in range(2)])
            kn_ring = Ring([Buf(V.f32(BANK + 8)) for _ in range(1)])
            kT_ring = Ring([Buf(V.f32(BANK)) for _ in range(2)])
            v_ring = Ring([Buf(V.f32(BANK)) for _ in range(2)])
            e_ring = Ring([Buf(W.f32(BANK)) for _ in range(3)])
            eT_ring = Ring([Buf(V.f32(BANK)) for _ in range(2)])
            m_ring = Ring([Buf(W.f32(8)) for _ in range(4)])
            o_ring = Ring([Buf(W.f32(H3 * P)) for _ in range(1)] + [Buf(V.f32(H3 * P)) for _ in range(1)])

            def queries(h, xT, t_x, q, q_free, pss, out):
                sq = yield from sq_ring.take()
                ps = yield from psum.take(1)
                for k in range(KD):
                    last = pe.after(t_x, l3_lane.token(), ps.free).matmul(ps.ap, l3_wq[:, k, h * P:(h + 1) * P], xT[:, k, :],
                                                                         start=(k == 0), stop=(k == KD - 1))
                t = pe.done(last)
                out["projected"] = t
                yield True
                t_s = act.done(act.after(t, sq.free).activation(sq.ap, ps.ap, ACT.Square))
                t_q = dve.done(dve.after(t_s, q_free).tensor_copy(q[:, h], ps.ap))
                ps.release(t_q)
                yield True
                for i in range(BLK):
                    last = pe.after(t_s, t_one, pss.free).matmul(pss.ap[:, i * H3 + h:i * H3 + h + 1], sq.ap[:, i * P:(i + 1) * P], ones, start=True, stop=True)
                t = pe.done(last)
                sq.release(t)
                out["q"], out["ss"] = t_q, t

            def keys(b, out):
                kn = yield from kn_ring.take()
                ps = yield from psum.take(1)
                for k in range(KD):
                    last = pe.after(l3_lane.token(), ps.free).matmul(ps.ap, ctxT[:, k, b * S:(b + 1) * S], l3_wk[:, k, :], start=(k == 0), stop=(k == KD - 1))
                t_k = pe.done(last)
                yield True
                n, ss = kn.ap[:, 0:BANK], kn.ap[:, BANK:BANK + 4]
                t = act.done(act.after(t_k, kn.free).activation(n, ps.ap, ACT.Square))
                t = dve.done(dve.after(t).tensor_reduce(ss, split_cols(n, G3), AXX, ALU.add))
                t = rstd(ss, ss, EPS_RMS, 1.0 / HD3, t)
                yield True
                t = dve.done(dve.after(t).tensor_tensor(split_cols(n, G3), split_cols(ps.ap, G3), ss.unsqueeze(2).broadcast_to([P, G3, HD3]), ALU.mult))
                ps.release(t)
                yield True
                kT = yield from kT_ring.take()
                pt = yield from psum.take(1)
                t = transposes([(n[:, g * P:(g + 1) * P], pt.ap[:, g * P:(g + 1) * P]) for g in range(G3)], pt, ident, t, pt.free)
                kn.release(t)
                t = dve.done(dve.after(t, t_w, kT.free).tensor_scalar(kT.ap, pt.ap, l3_w[:, 2:3], None, ALU.mult))
                pt.release(t)
                v = yield from v_ring.take()
                pv = yield from psum.take(1)
                for k in range(KD):
                    last = pe.after(pv.free).matmul(pv.ap, ctxT[:, k, b * S:(b + 1) * S], l3_wv[:, k, :], start=(k == 0), stop=(k == KD - 1))
                t_m = pe.done(last)
                t_v = act.done(act.after(t_m, v.free).activation(v.ap, pv.ap, ACT.Copy))
                pv.release(t_v)
                out.append((kT, t, v, t_v))

            def unit(i, g, q, t_q, rq, t_rq, kT, t_k, v, t_v, o, o_free, state):
                m = yield from m_ring.take()
                e = yield from e_ring.take()
                ps = yield from psum.take(1)
                for j in range(4):
                    last = pe.after(t_q, t_k, ps.free).matmul(ps.ap[:, j * P:(j + 1) * P], q[:, 4 * g + j, i * P:(i + 1) * P],
                                                              kT.ap[:, g * P:(g + 1) * P], start=True, stop=True)
                t = pe.done(last)
                state["scored"] = t
                yield True
                r4 = rq[:, i * H3 + 4 * g:i * H3 + 4 * g + 4]
                bias, rs = m.ap[:, 0:4], m.ap[:, 4:8]
                t = dve.done(dve.after(t, m.free).tensor_reduce(bias, split_cols(ps.ap, 4), AXX, ALU.max))
                t = dve.done(dve.after(t, t_rq).scalar_tensor_tensor(bias, bias, -1.0, r4, ALU.mult, ALU.mult))
                for j in range(4):
                    t = act.done(act.after(t, e.free).activation(e.ap[:, j * P:(j + 1) * P], ps.ap[:, j * P:(j + 1) * P], ACT.Exp,
                                                                bias=bias[:, j:j + 1], scale=r4[:, j:j + 1], accum_out=rs[:, j:j + 1]))
                ps.release(t)
                state["exp"] = t
                yield True
                t = dve.done(dve.after(t).reciprocal(rs, rs))
                t = dve.done(dve.after(t).tensor_tensor(split_cols(e.ap, 4), split_cols(e.ap, 4), rs.unsqueeze(2).broadcast_to([P, 4, S]), ALU.mult))
                m.release(t)
                yield True
                eT = yield from eT_ring.take()
                pt = yield from psum.take(1)
                t = transposes([(e.ap[:, j * P:(j + 1) * P], pt.ap[:, j * P:(j + 1) * P]) for j in range(4)], pt, ident, t, pt.free)
                e.release(t)
                yield True
                t = act.done(act.after(t, eT.free).activation(eT.ap, pt.ap, ACT.Copy))
                pt.release(t)
                yield True
                po = yield from psum.take(1)
                t = pe.done(pe.after(t, t_v, po.free).matmul(po.ap, v.ap[:, g * P:(g + 1) * P], eT.ap, start=True, stop=True))
                eT.release(t)
                state["valued"] = t
                yield True
                t = dve.done(dve.after(t, o_free).tensor_copy(o[:, 4 * g * P:(4 * g + 4) * P], po.ap))
                po.release(t)
                state[g] = t

            def tile(b, i, q, t_q, rq, t_rq, used):
                got = []
                yield from keys(b, got)
                kT, t_k, v, t_v = got[0]
                o = yield from o_ring.take()
                state = {}
                yield from interleave([unit(i, g, q, t_q, rq, t_rq, kT, t_k, v, t_v, o.ap, o.free, state) for g in range(G3)], 3)
                kT.release(state["scored"])
                v.release(state["valued"])
                used.append((state["scored"], state["exp"]))
                po = yield from psum.take(1)
                for h in range(H3):
                    last = pe.after([state[g] for g in range(G3)], po.free).matmul(po.ap[:, 0:D], o.ap[:, h * P:(h + 1) * P], l3_wo[:, h, :],
                                                                                   start=(h == 0), stop=(h == H3 - 1))
                t = pe.done(last)
                o.release(t)
                yield True
                t = dve.done(dve.after(t).scalar_tensor_tensor(X[b], po.ap[:, 0:D], gates[:, 3:4], X[b], ALU.mult, ALU.add))
                po.release(t)
                x_ready[b] = [t]

            def block(blk):
                xt = yield from xt_ring.take()
                xT = split_cols(xt.ap, KD)
                t_x = yield from norm_transpose(blk, xn_ring, xT, xt.free)
                q = yield from q_ring.take()
                q3 = split_cols(q.ap, H3)
                pss = yield from psum.take(1)
                out = {}
                yield from interleave([queries(h, xT, t_x, q3, q.free, pss, out) for h in range(H3)], 2)
                xt.release(out["projected"])
                rq = yield from rq_ring.take()
                n = BLK * H3
                t = dve.done(dve.after(out["ss"], rq.free).tensor_scalar(rq.ap, pss.ap[:, 0:n], 1.0 / HD3, EPS_RMS, ALU.mult, ALU.add))
                pss.release(t)
                t_rq = pool.done(pool.after(t).tensor_tensor(rq.ap, rq.ap, half_neg.broadcast_to([P, n]), ALU.pow))
                yield True
                used = []
                yield from interleave([tile(blk * BLK + i, i, q3, out["q"], rq.ap, t_rq, used) for i in range(BLK)], 2)
                q.release(*[u[0] for u in used])
                rq.release(*[u[1] for u in used])

            run(interleave([block(i) for i in range(NBLK)], 2))

        def l3_ffn():
            W = Arena(sbuf, A_AT, COLS)
            gate = split_cols(W.f32(KD * E3), KD)
            sgu = split_cols(W.f32(KD * 2 * SI3), KD)
            sd = split_cols(W.f32(2 * D), 2)
            iota, base = W.f32(E3), W.f32(E3)
            before_f = W.f32(P)
            before, ones = W.bf16(P), W.bf16(P)
            zeros = W.f32(2 * BANK)
            rl = lane("l3_router_weights_loaded")
            load(rl, gate, chunks_of(A["l3_gateT"]))
            load(rl, iota, A["iota"].broadcast_to([P, E3]))
            load(rl, base, A["slot_base"].broadcast_to([P, E3]))
            load(rl, before_f, A["before"])
            load(rl, sgu, chunks_of(A["l3_sguT"]))
            load(rl, sd[:, 0], A["l3_sdT"][0:P])
            load(rl, sd[0:SI3 - P, 1], A["l3_sdT"][P:SI3])
            t_z = dve.done(dve.api.memset(zeros, 0.0))
            for i in range(NSLOT // 512):
                slot_lane.start(sp, x_slots[i * 512:(i + 1) * 512].rearrange("(p r) n -> p (r n)", p=P), zeros, t_z)
            slot_lane.start(sp, y_slots[NSLOT:NSLOT + P], zeros[:, 0:D], t_z)
            t_bf = dve.done(dve.after(rl.token()).tensor_copy(before, before_f))
            t_on = dve.done(dve.api.memset(ones, 1.0))
            NW = 8
            w_ring = Ring([Buf((split_cols(W.f32(KD * 2 * I3), KD), W.f32(D, I3)), lane(f"expert_weights_loaded_{i}")) for i in range(NW)])
            xn_ring = Ring([Buf(W.f32(D), lane(f"rows_scattered_{i}")) for i in range(4)])
            xt_ring = Ring([Buf(W.f32(D)) for _ in range(2)])
            r_ring = Ring([Buf(W.f32(1300)) for _ in range(2)])
            keep_w = [W.f32(8) for _ in range(NB)]
            keep_i = [W.f32(8).bitcast(U32) for _ in range(NB)]
            cum_f = W.f32(E3)
            sel_bf = [W.bf16(2 * E3) for _ in range(3)]
            sel_ring = Ring([Buf(a) for a in sel_bf])
            sh_ring = Ring([Buf(W.f32(2 * SI3)) for _ in range(2)])
            shT_ring = Ring([Buf(W.f32(D)) for _ in range(2)])
            t_cum = dve.done(dve.api.memset(cum_f, 0.0))
            chain = {"cum": t_cum}
            scattered, t_slot = [], [None] * NB

            def route(b, xT, t_x, xn, t_xn):
                r = yield from r_ring.take()
                at = [0]

                def cut(n):
                    a = r.ap[:, at[0]:at[0] + n]
                    at[0] += n
                    return a
                prob, pick, keep_, slot = cut(E3), cut(E3), cut(E3), cut(E3)
                one = split_cols(cut(K3 * E3), K3)
                prod = split_cols(cut(K3 * E3), K3)
                idx = cut(8)
                idx_u = cut(8).bitcast(U32)
                mx, sm, s6 = cut(1), cut(1), cut(8)
                top = keep_w[b]
                ps = yield from psum.take(1)
                for k in range(KD):
                    last = pe.after(t_x, rl.token(), ps.free).matmul(ps.ap[:, 0:E3], xT[:, k], gate[:, k, :], start=(k == 0), stop=(k == KD - 1))
                t = pe.done(last)
                yield True
                t = dve.done(dve.after(t, r.free).tensor_reduce(mx, ps.ap[:, 0:E3], AXX, ALU.max, negate=True))
                t = act.done(act.after(t).activation(prob, ps.ap[:, 0:E3], ACT.Exp, bias=mx, accum_out=sm))
                ps.release(t)
                yield True
                t = dve.done(dve.after(t).reciprocal(sm, sm))
                t = dve.done(dve.after(t).tensor_scalar(prob, prob, sm, None, ALU.mult))
                t = dve.done(dve.after(t).max(top, prob))
                t = dve.done(dve.after(t).max_index(idx_u, top, prob))
                t = dve.done(dve.after(t).tensor_copy(idx, idx_u))
                t = dve.done(dve.after(t).tensor_tensor(one, iota.unsqueeze(1).broadcast_to([P, K3, E3]),
                                                       idx[:, 0:K3].unsqueeze(2).broadcast_to([P, K3, E3]), ALU.is_equal))
                t_p = dve.done(dve.after(t).tensor_reduce(pick, one.rearrange("p k e -> p e k"), AXX, ALU.add))
                sb = yield from sel_ring.take()
                t1 = dve.done(dve.after(t_p, sb.free).tensor_copy(sb.ap[:, 0:E3], pick))
                t2 = dve.done(dve.after(chain["cum"]).tensor_copy(sb.ap[:, E3:2 * E3], cum_f))
                chain["cum"] = dve.done(dve.after(t2).tensor_tensor(cum_f, cum_f, pick, ALU.add))
                yield True
                pp = yield from psum.take(1)
                pe.after(t1, t2, t_bf, t_on, pp.free).matmul(pp.ap[:, 0:E3], before, sb.ap[:, 0:E3], start=True, stop=False)
                t = pe.done(pe.api.matmul(pp.ap[:, 0:E3], ones, sb.ap[:, E3:2 * E3], start=False, stop=True))
                sb.release(t)
                yield True
                t1 = dve.done(dve.after(t).tensor_scalar(keep_, pp.ap[:, 0:E3], float(CAP3), None, ALU.is_lt))
                t2 = dve.done(dve.api.tensor_tensor(slot, pp.ap[:, 0:E3], base, ALU.add))
                pp.release(t1, t2)
                t = dve.done(dve.after(t1, t2).tensor_tensor(slot, slot, keep_, ALU.mult))
                t = dve.done(dve.after(t).tensor_tensor(prod, one, slot.unsqueeze(1).broadcast_to([P, K3, E3]), ALU.mult))
                t = dve.done(dve.after(t).tensor_reduce(s6[:, 0:K3], prod, AXX, ALU.add))
                t = dve.done(dve.after(t).tensor_scalar(keep_i[b][:, 0:K3], s6[:, 0:K3], float(NSLOT), None, ALU.add))
                r.release(t)
                t_slot[b] = t
                for k in range(K3):
                    pool.after(t, t_xn, slot_lane.token()).indirect_dma_start(
                        out=x_slots[:, :], out_offset=bass.IndirectOffsetOnAxis(ap=keep_i[b][:, k:k + 1], axis=0),
                        in_=xn.ap, in_offset=None, bounds_check=NSLOT - 1, oob_is_err=False).then_inc(xn.lane.sem, 16)
                    xn.lane.count += 16
                xn.release(xn.lane.token())

            def shared(b, xT, t_x):
                ps = yield from psum.take(1)
                for k in range(KD):
                    last = pe.after(t_x, rl.token(), ps.free).matmul(ps.ap[:, 0:2 * SI3], xT[:, k], sgu[:, k, :], start=(k == 0), stop=(k == KD - 1))
                t_m = pe.done(last)
                yield True
                sh = yield from sh_ring.take()
                th, h = sh.ap[:, 0:SI3], sh.ap[:, SI3:2 * SI3]
                t = act.done(act.after(t_m, sh.free).activation(th, ps.ap[:, 0:SI3], ACT.Tanh, scale=0.5))
                t = dve.done(dve.after(t).scalar_tensor_tensor(th, th, 1.0, ps.ap[:, 0:SI3], ALU.add, ALU.mult))
                t = dve.done(dve.after(t).scalar_tensor_tensor(h, th, 0.5, ps.ap[:, SI3:2 * SI3], ALU.mult, ALU.mult))
                ps.release(t)
                yield True
                pt = yield from psum.take(1)
                t = transposes([(h[:, 0:P], pt.ap[:, 0:P]), (h[:, P:SI3], pt.ap[0:SI3 - P, P:2 * P])], pt, ident, t, pt.free)
                sh.release(t)
                hT = yield from shT_ring.take()
                t1 = act.done(act.after(t, hT.free).activation(hT.ap[:, 0:P], pt.ap[:, 0:P], ACT.Copy))
                t2 = act.done(act.api.activation(hT.ap[0:SI3 - P, P:2 * P], pt.ap[0:SI3 - P, P:2 * P], ACT.Copy))
                pt.release(t1, t2)
                yield True
                po = yield from psum.take(1)
                pe.after(t1, t2, po.free).matmul(po.ap[:, 0:D], hT.ap[:, 0:P], sd[:, 0], start=True, stop=False)
                t = pe.done(pe.api.matmul(po.ap[:, 0:D], hT.ap[0:SI3 - P, P:2 * P], sd[0:SI3 - P, 1], start=False, stop=True))
                hT.release(t)
                yield True
                t = dve.done(dve.after(t, x_ready[b]).scalar_tensor_tensor(X[b], po.ap[:, 0:D], gates[:, 7:8], X[b], ALU.mult, ALU.add))
                po.release(t)
                x_ready[b] = [t]
                return t_m

            def tile(b):
                xn = yield from xn_ring.take()
                t_xn = yield from layer_norm(X[b], xn.ap, x_ready[b], xn.free)
                xt = yield from xt_ring.take()
                ps = yield from psum.take(1)
                t = transposes([(xn.ap[:, k * P:(k + 1) * P], ps.ap[:, k * P:(k + 1) * P]) for k in range(KD)], ps, ident, t_xn, ps.free)
                xT = split_cols(xt.ap, KD)
                t_x = act.done(act.after(t, xt.free).activation(xt.ap, ps.ap[:, 0:D], ACT.Copy))
                ps.release(t_x)
                yield True
                yield from route(b, xT, t_x, xn, [t_xn, t])
                t = yield from shared(b, xT, t_x)
                xt.release(t)
                scattered.append(xn.lane)

            run(interleave([tile(b) for b in range(NB)], 2))
            all_in = [buf.lane.token() for buf in xn_ring.bufs]

            xe_ring = Ring([Buf(W.f32(D), lane(f"slot_rows_loaded_{i}")) for i in range(3)])
            xeT_ring = Ring([Buf(W.f32(D)) for _ in range(2)])
            he_ring = Ring([Buf(W.f32(2 * I3)) for _ in range(2)])
            heT_ring = Ring([Buf(W.f32(P, I3)) for _ in range(2)])
            ye_ring = Ring([Buf(W.f32(D), lane(f"slot_outputs_stored_{i}")) for i in range(3)])

            def pair(n):
                ws = []
                for i in range(2):
                    w = yield from w_ring.take()
                    w.lane.start(sp, w.ap[0], chunks_of(A["l3_gu"][2 * n + i]), *w.free)
                    t_w = w.lane.start(sp, w.ap[1], A["l3_down"][2 * n + i])
                    ws.append((w, t_w))
                xe = yield from xe_ring.take()
                t = xe.lane.start(sp, xe.ap, x_slots[n * P:(n + 1) * P], xe.free, all_in)
                yield True
                ps = yield from psum.take(1)
                t = transposes([(xe.ap[:, k * P:(k + 1) * P], ps.ap[:, k * P:(k + 1) * P]) for k in range(KD)], ps, ident, t, ps.free)
                xe.release(t)
                xT = yield from xeT_ring.take()
                xT3 = split_cols(xT.ap, KD)
                t = act.done(act.after(t, xT.free).activation(xT.ap, ps.ap[:, 0:D], ACT.Copy))
                ps.release(t)
                yield True
                pg = yield from psum.take(1)
                for k in range(KD):
                    for i, (w, t_w) in enumerate(ws):
                        last = pe.after(t, t_w, pg.free).matmul(pg.ap[64 * i:64 * i + 64, 0:2 * I3], xT3[:, k, 64 * i:64 * i + 64], w.ap[0][:, k, :],
                                                                start=(k == 0), stop=(k == KD - 1), tile_position=(0, 64 * i))
                t = pe.done(last)
                xT.release(t)
                yield True
                h = yield from he_ring.take()
                th, hh = h.ap[:, 0:I3], h.ap[:, I3:2 * I3]
                t = act.done(act.after(t, h.free).activation(th, pg.ap[:, 0:I3], ACT.Tanh, scale=0.5))
                t = dve.done(dve.after(t).scalar_tensor_tensor(th, th, 1.0, pg.ap[:, 0:I3], ALU.add, ALU.mult))
                t = dve.done(dve.after(t).scalar_tensor_tensor(hh, th, 0.5, pg.ap[:, I3:2 * I3], ALU.mult, ALU.mult))
                pg.release(t)
                yield True
                pt = yield from psum.take(1)
                t = transposes([(hh, pt.ap[0:I3, 0:P])], pt, ident, t, pt.free)
                h.release(t)
                hT = yield from heT_ring.take()
                t = dve.done(dve.after(t, hT.free).tensor_copy(hT.ap, pt.ap[0:I3, 0:P]))
                pt.release(t)
                yield True
                po = yield from psum.take(1)
                for i, (w, t_w) in enumerate(ws):
                    last = pe.after(t, po.free).matmul(po.ap[64 * i:64 * i + 64, 0:D], hT.ap[:, 64 * i:64 * i + 64], w.ap[1],
                                                       start=True, stop=True, tile_position=(0, 64 * i))
                t = pe.done(last)
                for w, _ in ws:
                    w.release(t)
                hT.release(t)
                yield True
                y = yield from ye_ring.take()
                t = act.done(act.after(t, y.free).activation(y.ap, po.ap[:, 0:D], ACT.Copy))
                po.release(t)
                y.release(y.lane.start(sp, y_slots[n * P:(n + 1) * P], y.ap, t))

            run(interleave([pair(n) for n in range(E3 // 2)], 4))
            all_out = [buf.lane.token() for buf in ye_ring.bufs] + [slot_lane.token()]

            g_ring = Ring([Buf(W.f32(K3 * D), lane(f"rows_gathered_{i}")) for i in range(4)])

            def combine(b):
                g = yield from g_ring.take()
                g3 = split_cols(g.ap, K3)
                for k in range(K3):
                    pool.after(g.free, all_out, t_slot[b]).indirect_dma_start(
                        out=g3[:, k], out_offset=None, in_=y_slots[:, :],
                        in_offset=bass.IndirectOffsetOnAxis(ap=keep_i[b][:, k:k + 1], axis=0)).then_inc(g.lane.sem, 16)
                    g.lane.count += 16
                yield True
                t = dve.done(dve.after(g.lane.token()).tensor_scalar(g3[:, 0], g3[:, 0], keep_w[b][:, 0:1], None, ALU.mult))
                for k in range(1, K3):
                    t = dve.done(dve.after(t).scalar_tensor_tensor(g3[:, 0], g3[:, k], keep_w[b][:, k:k + 1], g3[:, 0], ALU.mult, ALU.add))
                t = dve.done(dve.after(t, x_ready[b]).scalar_tensor_tensor(X[b], g3[:, 0], gates[:, 7:8], X[b], ALU.mult, ALU.add))
                g.release(t)
                x_ready[b] = [t]
            run(interleave([combine(b) for b in range(NB)], 3))

        stages = [l0_attention, l0_ffn, l1_attention, l1_ffn, l2_attention, l2_ffn, l3_attention, l3_ffn]
        for stage in stages[:last_stage]:
            stage()
            barrier()
        out_lane = lane("out_stored")
        for b in range(NB):
            out_lane.start(sp, out[b], X[b], x_ready[b])
        sp.after([l.token() for l in lanes if l.count])


def constants():
    c = {"ident": np.eye(P, dtype=np.float32)}
    inv = (1.0 / np.float32(10000.0) ** (np.arange(0, HD0, 2, dtype=np.float32) / np.float32(HD0))).astype(np.float32)

    def tables(n):
        f = (np.arange(n, dtype=np.float32)[None, :] * inv[:, None]).astype(np.float32)
        return np.cos(f), np.sin(f)
    cos, sin = tables(T0)
    scale = np.float32(1.0 / np.sqrt(HD0))
    cos8 = np.concatenate([cos, cos])
    sin8 = np.concatenate([-sin, sin])
    c["l0_cosq"] = (np.repeat(cos8, H0, 0) * scale).astype(np.float32)
    c["l0_sinq"] = (np.repeat(sin8, H0, 0) * scale).astype(np.float32)
    c["l0_cosk"] = np.repeat(cos8, G0, 0).astype(np.float32)
    c["l0_sink"] = np.repeat(sin8, G0, 0).astype(np.float32)
    sel = np.zeros((3, 32, NF0 * P), np.float32)
    for f in range(HID0):
        sel[:, min(f // F0, E0), f] = 1.0
    c["l0_sel"] = sel.reshape(96, NF0 * P)
    cos, sin = tables(S)
    c["l1_cos"] = np.repeat(cos, H1, 0).astype(np.float32)
    c["l1_sin"] = np.repeat(sin, H1, 0).astype(np.float32)
    c["l1_cosq"], c["l1_sinq"] = c["l1_cos"] * scale, c["l1_sin"] * scale
    c["iota"] = np.arange(E3, dtype=np.float32).reshape(1, E3)
    c["slot_base"] = (np.arange(E3, dtype=np.float32) * CAP3 - NSLOT).reshape(1, E3)
    c["before"] = np.triu(np.ones((P, P), np.float32), 1)
    return c


def layout(i):
    a = {n: i[n] for n in ("x", "ctx_2048", "g_xattn", "g_ffn")}
    half = [(d + HD0 // 2) % HD0 for d in range(HD0)]

    def head_minor(w, heads, hd):
        return w.reshape(heads, hd, -1).transpose(1, 0, 2)
    wq, bq = head_minor(i["L0_xattn_Wq"], H0, HD0), head_minor(i["L0_xattn_bq"], H0, HD0)
    wk, bk = head_minor(i["L0_xattn_Wk"], G0, HD0), head_minor(i["L0_xattn_bk"], G0, HD0)
    a["l0_wqT"], a["l0_wqpT"] = wq.reshape(P, P).T, wq[half].reshape(P, P).T
    a["l0_wkT"], a["l0_wkpT"] = wk.reshape(32, P).T, wk[half].reshape(32, P).T
    a["l0_bq2"] = np.stack([bq.reshape(P), bq[half].reshape(P)], 1)
    a["l0_bk2"] = np.stack([bk.reshape(32), bk[half].reshape(32)], 1)
    a["l0_wvT"] = i["L0_xattn_Wv"].T
    a["l0_bv"] = i["L0_xattn_bv"].reshape(1, 32)
    a["l0_bo"] = i["L0_xattn_bo"].reshape(P, 1)
    a["l0_woT"] = i["L0_xattn_Wo"].T
    e0 = E0 * F0
    a["l0_gateT"] = np.concatenate([i["L0_ffn_gate_w"], i["L0_ffn_shared_gate_w"]]).T
    a["l0_fc1T"] = np.concatenate([i["L0_ffn_expert_fc1"].reshape(e0, D), i["L0_ffn_shared_fc1"]]).T
    a["l0_fc2T"] = np.concatenate([i["L0_ffn_expert_fc2"].reshape(e0, D), i["L0_ffn_shared_fc2"]]).T
    a["l0_projT"] = np.concatenate([i["L0_ffn_expert_proj"].transpose(0, 2, 1).reshape(e0, D), i["L0_ffn_shared_proj"].T])

    def columns_head_minor(w, heads, hd):
        return w.reshape(-1, heads, hd).transpose(0, 2, 1).reshape(-1, heads * hd)
    a["mask1"] = i["mask_Bx1xSxS_fk0"].reshape(NB, S, S)
    a["l1_wq"] = columns_head_minor(i["L1_xattn_Wq"], H1, HD1)
    a["l1_wk"] = columns_head_minor(i["L1_xattn_Wk"], H1, HD1)
    a["l1_wv"], a["l1_wo"] = i["L1_xattn_Wv"], i["L1_xattn_Wo"]
    a["l1_gate"] = i["L1_xattn_gate"].reshape(1, H1)
    a["l1_gu"], a["l1_down"] = i["L1_ffn_gate_up_proj"], i["L1_ffn_down_proj"]
    a["mask2T"] = i["mask_BxS2_ik0"].T
    a["l2_wqT"] = columns_head_minor(i["L2_xattn_Wq"].T, H2, HD2)
    a["l2_wkT"] = columns_head_minor(i["L2_xattn_Wk"].T, H2, HD2)
    a["l2_wvT"], a["l2_woT"] = i["L2_xattn_Wv"].T, i["L2_xattn_Wo"].T
    for n in ("bq", "bk"):
        a["l2_" + n] = columns_head_minor(i["L2_xattn_" + n], H2, HD2).reshape(KD, P).T
    a["l2_rows"] = np.stack([i["L2_xattn_" + n] for n in ("bv", "bo", "ln_gamma", "ln_beta")])
    a["l2_rs"] = i["L2_xattn_residual_scale"].reshape(1, 1)
    a["l2_wgT"], a["l2_wuT"], a["l2_wdT"] = i["L2_ffn_w_gate"].T, i["L2_ffn_w_up"].T, i["L2_ffn_w_down"].T
    for n in ("Wq", "Wk", "Wv", "Wo"):
        a["l3_" + n.lower()] = i["L3_xattn_" + n]
    a["l3_qkw"] = np.stack([i["L3_xattn_q_norm_w"], i["L3_xattn_k_norm_w"]], 1)
    a["l3_gateT"] = i["L3_ffn_gate_w"].T
    a["l3_gu"], a["l3_down"] = i["L3_ffn_gate_up_proj"], i["L3_ffn_down_proj"]
    a["l3_sguT"] = np.concatenate([i["L3_ffn_shared_gate_w"], i["L3_ffn_shared_up_w"]]).T
    a["l3_sdT"] = i["L3_ffn_shared_down_w"].T
    return a


LAST_STAGE = 8


def kernel(**inputs):
    import concourse.bacc as _bacc
    from concourse.bass_utils import run_bass_kernel_spmd as _run

    nc = _bacc.Bacc("TRN2", target_bir_lowering=False, num_devices=1)
    arrays, aps = {}, {}
    host = {**layout({k: np.asarray(v) for k, v in inputs.items()}), **constants()}
    for name, a in host.items():
        a = np.ascontiguousarray(a)
        arrays[f"in_{name}"] = a
        aps[name] = nc.dram_tensor(f"in_{name}", a.shape, mybir.dt.from_np(a.dtype), kind="ExternalInput").ap()
    out = nc.dram_tensor("out_x", (NB, S, D), F32, kind="ExternalOutput").ap()
    program(nc, aps, out, LAST_STAGE)
    return _run(nc, [arrays], core_ids=[0]).results[0]["out_x"]
```

```python
from contextlib import ExitStack

import numpy as np

import concourse.bass as bass
from concourse import mybir

F32 = mybir.dt.float32
BF16 = mybir.dt.bfloat16
U32 = mybir.dt.uint32
I32 = mybir.dt.int32
ALU = mybir.AluOpType
ACT = mybir.ActivationFunctionType
AXX = mybir.AxisListType.X

P = 128
NB = 16
S = 128
D = 256
KD = D // P
BANK = 512
BLK = 4
NBLK = NB // BLK
EPS_LN = 1e-5
LOWEST = -3.38e38
ROUND = 12582912.0
PART_Q = (0, 0, 1, 1, 0, 2)
PART_K = (0, 1, 0, 1, 2, 0)
NT = len(PART_Q)

H0, G0, HD0, T0 = 16, 4, 8, 256
E0, F0, FS0 = 8, 176, 704
HID0 = E0 * F0 + FS0
NF0 = -(-HID0 // P)
H1, HD1 = 32, 8
E1 = 4
H2, HD2 = 16, 16
F2 = 832
NF2 = -(-F2 // P)
H3, G3, HD3 = 16, 4, 128
E3, K3, CAP3, I3, SI3 = 64, 6, 64, 96, 192
NSLOT = E3 * CAP3
EPS_RMS = 1e-6


class Engine:

    def __init__(self, api, sem):
        self.api, self.sem, self.count, self.seen = api, sem, 0, {}

    def after(self, *tokens):
        for t in tokens:
            if isinstance(t, list):
                self.after(*t)
            elif t is not None:
                name, sem, value = t
                if self.seen.get(name, 0) < value:
                    self.api.wait_ge(sem, value)
                    self.seen[name] = value
        return self.api

    def done(self, instruction):
        self.count += 1
        instruction.then_inc(self.sem, 1)
        return self.last()

    def last(self):
        return (id(self), self.sem, self.count)


class Lane:

    def __init__(self, sem):
        self.sem, self.count = sem, 0

    def start(self, engine, out, in_, *waits):
        engine.after(*waits).dma_start(out, in_).then_inc(self.sem, 16)
        self.count += 16
        return self.token()

    def token(self):
        return (id(self), self.sem, self.count)


class Buf:

    def __init__(self, ap, lane=None):
        self.ap, self.lane, self.free, self.held, self.age = ap, lane, [], False, 0

    def release(self, *tokens):
        self.free, self.held = list(tokens), False


class Ring:
    def __init__(self, bufs):
        self.bufs, self.clock = bufs, 0

    def take(self):
        while all(b.held for b in self.bufs):
            yield False
        buf = min((b for b in self.bufs if not b.held), key=lambda b: b.age)
        self.clock += 1
        buf.held, buf.age = True, self.clock
        return buf


class PsumBanks:

    def __init__(self, tensor):
        self.tensor, self.free, self.held = tensor, [[] for _ in range(8)], [False] * 8
        self.age, self.clock = [0] * 8, 0

    def take(self, n):
        while True:
            starts = [i for i in range(0, 8, n) if not any(self.held[i:i + n])]
            if starts:
                break
            yield False
        i = min(starts, key=lambda k: (n == 1 and not self.held[k ^ 1], max(self.age[k:k + n]), k))
        self.clock += 1
        for k in range(i, i + n):
            self.held[k], self.age[k] = True, self.clock
        return Banks(self, i, n)


class Banks:
    def __init__(self, pool, i, n):
        self.pool, self.i, self.n = pool, i, n
        self.ap = pool.tensor[:, i * BANK:(i + n) * BANK]
        self.free = [t for k in range(i, i + n) for t in pool.free[k]]

    def release(self, *tokens):
        for k in range(self.i, self.i + self.n):
            self.pool.held[k], self.pool.free[k] = False, list(tokens)
            self.pool.clock += 1
            self.pool.age[k] = self.pool.clock


def interleave(jobs, depth):
    jobs, active = list(jobs), []
    while jobs or active:
        while jobs and len(active) < depth:
            active.append(jobs.pop(0))
        moved = False
        for job in list(active)[::-1]:
            try:
                moved = (next(job) is not False) or moved
            except StopIteration:
                active.remove(job)
                moved = True
        if not moved:
            yield False
        else:
            yield True


def run(job):
    stuck = 0
    for moved in job:
        stuck = stuck + 1 if moved is False else 0
        if stuck > 200:
            raise RuntimeError("the jobs wait for each other")


class Arena:

    def __init__(self, tensor, lo, hi):
        self.tensor, self.at, self.lo, self.hi = tensor, lo, lo, hi

    def f32(self, cols, rows=P):
        a = self.at
        self.at += cols
        if self.at > self.hi:
            raise RuntimeError(f"arena full: {self.at} > {self.hi}")
        return self.tensor[0:rows, a:a + cols]

    def bf16(self, cols, rows=P):
        return self.f32(-(-cols // 2), rows).bitcast(BF16)[:, 0:cols]

    def reset(self):
        self.at = self.lo


def program(nc, A, out, last_stage=8):
    ctx = ExitStack()
    with ctx:
        n_sem = [0]

        def sem(name):
            n_sem[0] += 1
            return ctx.enter_context(nc.semaphore(name))

        pe = Engine(nc.tensor, sem("pe_done"))
        dve = Engine(nc.vector, sem("dve_done"))
        act = Engine(nc.scalar, sem("act_done"))
        pool = Engine(nc.gpsimd, sem("pool_done"))
        sp = Engine(nc.sync, sem("sp_done"))
        engines = [pe, dve, act, pool, sp]
        lanes = []

        def lane(name):
            lanes.append(Lane(sem(name)))
            return lanes[-1]

        COLS = 52800
        sbuf = ctx.enter_context(nc.sbuf_tensor("sbuf", [P, COLS], F32))
        psum = PsumBanks(ctx.enter_context(nc.psum_tensor("psum", [P, 8 * BANK], F32)))

        def dram(name, shape, dtype):
            return nc.dram_tensor(name, shape, dtype, kind="Internal").ap()

        A_AT, B_AT, WORK_AT = 8800, 22900, 34300
        keep = Arena(sbuf, 0, A_AT)
        region_a = Arena(sbuf, A_AT, B_AT)
        region_b = Arena(sbuf, B_AT, WORK_AT)

        x_all = keep.f32(NB * D)
        X = [x_all[:, b * D:(b + 1) * D] for b in range(NB)]
        ctxT = keep.f32(KD * NB * S).rearrange("p (k n) -> p k n", k=KD)
        ident = keep.f32(P)
        ident_bf = keep.bf16(P)
        gates = keep.f32(8)
        half_neg = keep.f32(1)
        ln_cols = [keep.f32(16) for _ in range(6)]
        stat_ring = Ring([Buf(a) for a in ln_cols])

        const_lane = lane("const_loaded")
        x_lane = lane("x_loaded")
        for name, dst in (("ident", ident),):
            const_lane.start(sp, dst, A[name])
        for name, lo in (("g_xattn", 0), ("g_ffn", 4)):
            const_lane.start(sp, gates[:, lo:lo + 4], A[name].rearrange("(a n) -> a n", a=1).broadcast_to([P, 4]))
        x_ready = []
        for b in range(NB):
            x_lane.start(sp, X[b], A["x"][b])
            x_ready.append([])
        t_bf = dve.done(dve.after(const_lane.token()).tensor_copy(ident_bf, ident))
        t_half = dve.done(dve.api.memset(half_neg, -0.5))
        t_gate = act.done(act.after(const_lane.token()).activation(gates, gates, ACT.Tanh))
        for b in range(NB):
            x_ready[b] = [x_lane.token()]
        for e in (pe, dve, act, pool):
            e.after(t_bf, t_half, t_gate, const_lane.token())

        def barrier():
            ends = [e.last() for e in engines if e is not sp] + [l.token() for l in lanes if l.count]
            for e in engines:
                e.after([t for t in ends if t[0] != id(e)])
                if e is not sp:
                    e.after(e.last())

        def rstd(out_col, var_col, eps, scale, *waits):
            n = out_col.shape[-1]
            t = dve.done(dve.after(*waits).tensor_scalar(out_col, var_col, scale, eps, ALU.mult, ALU.add))
            return pool.done(pool.after(t).tensor_tensor(out_col, out_col,
                             half_neg.broadcast_to([P, n]) if n > 1 else half_neg, ALU.pow))

        def layer_norm(src, dst, waits, dst_free):
            st = yield from stat_ring.take()
            s = st.ap
            t = dve.done(dve.after(waits, st.free).bn_stats(s[:, 0:6], src))
            t = dve.done(dve.after(t).bn_aggr(s[:, 6:8], s[:, 0:6]))
            t = rstd(s[:, 8:9], s[:, 7:8], EPS_LN, 1.0, t)
            yield True
            t = dve.done(dve.after(t, dst_free).tensor_scalar(dst, src, s[:, 6:7], s[:, 8:9],
                                                             ALU.subtract, ALU.mult))
            st.release(t)
            return t

        def split3(src, dst, tmp, waits, dst_free):
            hi, mid, lo = (dst[:, i] for i in range(3))
            t = act.done(act.after(waits, dst_free).activation(hi, src, ACT.Copy))
            t = pool.done(pool.after(t, dst_free).tensor_tensor(tmp, src, hi, ALU.subtract))
            t = act.done(act.after(t).activation(mid, tmp, ACT.Copy))
            return pool.done(pool.after(t).tensor_tensor(lo, tmp, mid, ALU.subtract))

        def add_rows(dst3, src3, col, on_act, waits, dst_free):
            if not on_act:
                return dve.done(dve.after(waits, dst_free).tensor_tensor(dst3, src3, col.unsqueeze(2).broadcast_to(list(src3.shape)), ALU.add))
            for j in range(src3.shape[1]):
                last = act.after(waits, dst_free).activation(dst3[:, j], src3[:, j], ACT.Identity, bias=col[:, j:j + 1])
            return act.done(last)

        def transposes(blocks, ps, ident_ap, *waits):
            api = pe.after(*waits)
            for src, dst in blocks:
                last = api.transpose(dst, src, ident_ap)
            return pe.done(last)

        def normalise(av, width, head_w, dst, t_av, t_free, ring):
            nblk = width // 32
            tb = yield from ring.take()
            T = tb.ap[:, 0:width]
            R = tb.ap[:, width:width + nblk]
            t = dve.done(dve.after(t_av, tb.free).transpose(T, av.ap[:, 0:width]))
            av.release(t)
            T3 = T.rearrange("p (n r) -> p n r", r=32)
            t = dve.done(dve.after(t).reciprocal(R, T3[:, :, head_w]))
            t = dve.done(dve.after(t).tensor_tensor(
                T3, T3, R.unsqueeze(2).broadcast_to([P, nblk, 32]), ALU.mult))
            t = dve.done(dve.after(t, t_free).transpose(dst, T))
            tb.release(t)
            return t

        def load(ln, dst, src, *waits):
            return ln.start(sp, dst, src, *waits)

        w_lane = [lane(f"weights_{i}_loaded") for i in range(8)]

        def l0_attention():
            A0 = Arena(sbuf, B_AT, COLS)
            wq = A0.f32(P)
            wqp = A0.f32(P)
            wk = A0.f32(2 * 32)
            wv = A0.f32(32)
            wo = A0.f32(4 * P).rearrange("p (j o) -> p j o", j=4)
            cosq, sinq = A0.f32(T0), A0.f32(T0)
            cosk, sink = A0.f32(T0, 32), A0.f32(T0, 32)
            bq = A0.f32(2)
            bk = A0.f32(2, 32)
            bo = A0.f32(1)
            bv = A0.f32(32)
            wl = w_lane[0]
            t_zero = dve.done(dve.api.memset(wo, 0.0))
            load(wl, wq, A["l0_wqT"])
            load(wl, wqp, A["l0_wqpT"])
            load(wl, wk[:, 0:32], A["l0_wkT"])
            load(wl, wk[:, 32:64], A["l0_wkpT"])
            load(wl, wv, A["l0_wvT"])
            load(wl, cosq, A["l0_cosq"])
            load(wl, sinq, A["l0_sinq"])
            load(wl, cosk, A["l0_cosk"])
            load(wl, sink, A["l0_sink"])
            load(wl, bq, A["l0_bq2"])
            load(wl, bk, A["l0_bk2"])
            load(wl, bo, A["l0_bo"])
            load(wl, bv, A["l0_bv"].broadcast_to([P, 32]))
            for g in range(G0):
                load(wl, wo[32 * g:32 * g + HD0], A["l0_woT"][32 * g:32 * g + 32].rearrange("(j d) o -> d j o", d=HD0), t_zero)
            w_ready = wl.token()

            ctx_ring = Ring([Buf(A0.f32(T0), lane(f"ctx_loaded_{i}")) for i in range(3)])
            xn_ring = Ring([Buf(A0.f32(T0)) for _ in range(2)])
            rope_ring = Ring([Buf(A0.f32(4 * T0)) for _ in range(2)])
            part_ring = Ring([Buf(A0.bf16(3 * T0), lane(f"q_parts_stored_{i}")) for i in range(2)])
            kpart_ring = Ring([Buf(A0.bf16(3 * T0, 32), lane(f"k_parts_stored_{i}")) for i in range(2)])
            q_ring = [Buf(A0.bf16(H0 * T0), lane(f"q_stack_loaded_{i}")) for i in range(2)]
            k_ring = [Buf(A0.bf16(G0 * T0), lane(f"k_stack_loaded_{i}")) for i in range(2)]
            v_ring = [Buf(A0.f32(2 * G0 * 32)) for i in range(2)]
            d_ring = Ring([Buf(A0.f32(4 * T0)) for _ in range(4)])
            e_ring = Ring([Buf(A0.f32(2 * 4 * P)) for _ in range(8)])
            m_ring = Ring([Buf(A0.f32(4)) for _ in range(4)])
            t_ring = Ring([Buf(A0.f32(BANK + 16)) for _ in range(2)])
            attn_ring = Ring([Buf(A0.f32(4 * T0)) for _ in range(2)])
            y_ring = Ring([Buf(A0.f32(T0)) for _ in range(2)])
            L0_ON_ACT = (0,)
            q_dram = dram("l0_q_parts", [NB, 3, P, T0], BF16)
            k_dram = dram("l0_k_parts", [NB, 3, 32, T0], BF16)
            for buf in q_ring + k_ring:
                buf.free = [dve.done(dve.api.memset(buf.ap[0:96], 0.0))]
            for buf in v_ring:
                v4 = buf.ap.rearrange("p (c g w) -> p c g w", c=2, g=G0)
                t = dve.done(dve.api.memset(buf.ap, 0.0))
                buf.free = [dve.done(dve.after(t).memset(v4[:, :, :, HD0:HD0 + 1], 1.0))]
            q_ring, k_ring, v_ring = Ring(q_ring), Ring(k_ring), Ring(v_ring)

            ready = {}

            def unit(b, c, g, state):
                while b not in ready:
                    yield False
                r = ready[b]
                m = yield from m_ring.take()
                d = yield from d_ring.take()
                ps = yield from psum.take(2)
                api = pe.after(r["stacks_loaded"], ps.free)
                q3 = r["q"].ap.rearrange("p (h t) -> p h t", h=H0)
                k3 = r["k"].ap.rearrange("p (g t) -> p g t", g=G0)
                for j in range(4):
                    last = api.matmul(ps.ap[:, j * T0:(j + 1) * T0], q3[0:96, 4 * g + j, c * P:(c + 1) * P],
                                      k3[0:96, g, :], start=True, stop=True)
                t_s = pe.done(last)
                state["units"] += 1
                if state["units"] == 2 * G0:
                    r["q"].release(t_s)
                    r["k"].release(t_s)
                yield True
                s3 = ps.ap.rearrange("p (j t) -> p j t", j=4)
                d3 = d.ap.rearrange("p (j t) -> p j t", j=4)
                t = dve.done(dve.after(t_s, m.free).tensor_reduce(m.ap, s3, AXX, ALU.max, negate=True))
                t = add_rows(d3, s3, m.ap, g in L0_ON_ACT, t, d.free)
                ps.release(t)
                m.release(t)
                yield True
                e = yield from e_ring.take()
                pt = yield from psum.take(2)
                t = transposes([(d3[:, j, kc * P:(kc + 1) * P], pt.ap[:, (kc * 4 + j) * P:(kc * 4 + j + 1) * P])
                                for kc in range(2) for j in range(4)], pt, ident, t, pt.free)
                d.release(t)
                yield True
                t = act.done(act.after(t, e.free).activation(e.ap, pt.ap, ACT.Exp))
                pt.release(t)
                state["E"][c, g] = (e, t)

            def values(b, c, state):
                while any((c, g) not in state["E"] for g in range(G0)):
                    yield False
                if c == 0:
                    state["attn"] = yield from attn_ring.take()
                while "attn" not in state:
                    yield False
                at, v = state["attn"], ready[b]["v"]
                E = [state["E"][c, g] for g in range(G0)]
                av = yield from psum.take(1)
                v4 = v.ap.rearrange("p (c g w) -> p c g w", c=2, g=G0)
                for kc in range(2):
                    for g in range(G0):
                        last = pe.after(ready[b]["v_ready"], av.free, E[g][1]).matmul(
                            av.ap[32 * g:32 * g + 32, :], v4[:, kc, g, :], E[g][0].ap[:, kc * BANK:(kc + 1) * BANK],
                            start=(kc == 0), stop=(kc == 1), tile_position=(0, 32 * g))
                t = pe.done(last)
                for g in range(G0):
                    E[g][0].release(t)
                if c == 1:
                    v.release(t)
                yield True
                dst = at.ap.rearrange("p (c n) -> p c n", c=2)[:, c]
                state["out"][c] = yield from normalise(av, BANK, HD0, dst, t, at.free, t_ring)

            def project_out(b, state):
                while len(state["out"]) < 2:
                    yield False
                at = state["attn"]
                po = yield from psum.take(1)
                a4 = at.ap.rearrange("p (c j n) -> p j c n", c=2, j=4)
                for j in range(4):
                    last = pe.after(state["out"][0], state["out"][1], po.free).matmul(po.ap[:, 0:T0], wo[:, j, :], a4[:, j], start=(j == 0), stop=(j == 3))
                t = pe.done(last)
                at.release(t)
                yield True
                tmp = yield from y_ring.take()
                t = dve.done(dve.after(t, tmp.free).tensor_scalar(tmp.ap, po.ap[:, 0:T0], bo, gates[:, 0:1], ALU.add, ALU.mult))
                po.release(t)
                t = pool.done(pool.after(t).tensor_tensor(X[b], X[b], tmp.ap, ALU.add))
                tmp.release(t)
                x_ready[b] = [t]

            def prologue(b):
                cb = yield from ctx_ring.take()
                t_ctx = load(cb.lane, cb.ap, A["ctx_2048"][b], *cb.free)
                xn = yield from xn_ring.take()
                t_xn = yield from layer_norm(X[b], xn.ap, x_ready[b], xn.free)
                yield True
                pc = yield from psum.take(1)
                t = transposes([(cb.ap[:, k * P:(k + 1) * P], pc.ap[:, k * P:(k + 1) * P]) for k in range(KD)],
                               pc, ident, t_ctx, pc.free)
                t_c = act.done(act.after(t).activation(ctxT[:, :, b * S:(b + 1) * S],
                                                       pc.ap[:, 0:D].rearrange("p (k n) -> p k n", k=KD), ACT.Copy))
                pc.release(t_c)
                pq = yield from psum.take(1)
                pk = yield from psum.take(1)
                pv = yield from psum.take(1)
                api = pe.after(t_xn, w_ready, pq.free)
                api.matmul(pq.ap[:, 0:T0], wq, xn.ap, start=True, stop=True)
                t_q = pe.done(api.matmul(pq.ap[:, T0:2 * T0], wqp, xn.ap, start=True, stop=True))
                xn.release(t_q)
                api = pe.after(t_ctx, pk.free, pv.free)
                api.matmul(pk.ap[0:32, 0:T0], wk[:, 0:32], cb.ap, start=True, stop=True)
                api.matmul(pk.ap[0:32, T0:2 * T0], wk[:, 32:64], cb.ap, start=True, stop=True)
                api.matmul(pv.ap[:, 0:32], cb.ap[:, 0:P], wv, start=True, stop=True)
                t_kv = pe.done(api.matmul(pv.ap[:, 32:64], cb.ap[:, P:2 * P], wv, start=True, stop=True))
                cb.release(t_kv, t)
                yield True
                r = yield from rope_ring.take()
                q_a, q_b, k_a, k_b = (r.ap[:, i * T0:(i + 1) * T0] for i in range(4))
                t1 = dve.done(dve.after(t_q, r.free).scalar_tensor_tensor(q_a, pq.ap[:, 0:T0], bq[:, 0:1], cosq, ALU.add, ALU.mult))
                t2 = dve.done(dve.api.scalar_tensor_tensor(q_b, pq.ap[:, T0:2 * T0], bq[:, 1:2], sinq, ALU.add, ALU.mult))
                pq.release(t2)
                t_qr = dve.done(dve.after(t1, t2).tensor_tensor(q_a, q_a, q_b, ALU.add))
                t1 = dve.done(dve.after(t_kv).scalar_tensor_tensor(k_a[0:32], pk.ap[0:32, 0:T0], bk[:, 0:1], cosk, ALU.add, ALU.mult))
                t2 = dve.done(dve.api.scalar_tensor_tensor(k_b[0:32], pk.ap[0:32, T0:2 * T0], bk[:, 1:2], sink, ALU.add, ALU.mult))
                pk.release(t2)
                t_kr = dve.done(dve.after(t1, t2).tensor_tensor(k_a[0:32], k_a[0:32], k_b[0:32], ALU.add))
                v = yield from v_ring.take()
                v4 = v.ap.rearrange("p (c g w) -> p c g w", c=2, g=G0)
                bv3 = bv.rearrange("p (g w) -> p g w", g=G0)
                for c in range(2):
                    t_v = dve.done(dve.after(v.free).tensor_tensor(
                        v4[:, c, :, 0:HD0], pv.ap[:, 32 * c:32 * c + 32].rearrange("p (g w) -> p g w", g=G0), bv3, ALU.add))
                pv.release(t_v)
                yield True
                qp = yield from part_ring.take()
                kp = yield from kpart_ring.take()
                qp3 = qp.ap.rearrange("p (i t) -> p i t", i=3)
                kp3 = kp.ap.rearrange("p (i t) -> p i t", i=3)
                t_qs = split3(q_a, qp3, q_b, t_qr, qp.free)
                t_ks = split3(k_a[0:32], kp3, k_b[0:32], t_kr, kp.free)
                r.release(t_qs, t_ks)
                t_qw = qp.lane.start(sp, q_dram[b].rearrange("i r t -> r i t"), qp3, t_qs)
                t_kw = kp.lane.start(sp, k_dram[b].rearrange("i r t -> r i t"), kp3, t_ks)
                qp.release(t_qw)
                kp.release(t_kw)
                yield True
                q_st = yield from q_ring.take()
                k_st = yield from k_ring.take()
                for i in range(NT):
                    q_st.lane.start(sp, q_st.ap[HD0 * i:HD0 * i + HD0], q_dram[b, PART_Q[i]].rearrange("(d h) t -> d (h t)", d=HD0),
                                    q_st.free, t_qw)
                    k_st.lane.start(sp, k_st.ap[HD0 * i:HD0 * i + HD0], k_dram[b, PART_K[i]].rearrange("(d g) t -> d (g t)", d=HD0),
                                    k_st.free, t_kw)
                ready[b] = {"q": q_st, "k": k_st, "v": v, "v_ready": t_v, "stacks_loaded": [q_st.lane.token(), k_st.lane.token()]}

            def batch_jobs(b):
                state = {"units": 0, "E": {}, "out": {}}
                for c in range(2):
                    for g in range(G0):
                        yield unit(b, c, g, state)
                    yield values(b, c, state)
                yield project_out(b, state)

            main = [job for b in range(NB) for job in batch_jobs(b)]
            run(interleave([interleave([prologue(b) for b in range(NB)], 1), interleave(main, 5)], 2))

        def chunks_of(src, k=KD):
            return src.rearrange("(k p) n -> p k n", k=k)

        def split_cols(ap, k):
            return ap.rearrange("p (k n) -> p k n", k=k)

        def norm_transpose(blk, xn_ring, xnT, xnT_free, n=BLK):
            tiles = []
            xn = yield from xn_ring.take()
            for i in range(n):
                b = blk * n + i
                tile = xn.ap[:, i * D:(i + 1) * D]
                t = yield from layer_norm(X[b], tile, x_ready[b], xn.free)
                tiles.append((tile, t))
            yield True
            banks = KD * n * P // BANK
            ps = yield from psum.take(banks)
            p4 = ps.ap.rearrange("p (k b n) -> p k b n", k=KD, b=n)
            t = transposes([(xn_i[:, k * P:(k + 1) * P], p4[:, k, i]) for i, (xn_i, _) in enumerate(tiles) for k in range(KD)],
                           ps, ident, [t for _, t in tiles], ps.free)
            xn.release(t)
            yield True
            t = act.done(act.after(t, xnT_free).activation(xnT, split_cols(ps.ap, KD), ACT.Copy))
            ps.release(t)
            return t

        R0 = region_a
        w_fc1 = split_cols(R0.f32(KD * HID0), KD)
        w_fc2 = split_cols(R0.f32(KD * HID0), KD)
        w_proj = split_cols(R0.f32(NF0 * D), NF0)
        w_gate0 = split_cols(R0.f32(KD * 9), KD)
        sel = R0.bf16(NF0 * P)[0:96]
        l0f_lane = lane("l0_ffn_weights_loaded")
        load(l0f_lane, w_gate0, chunks_of(A["l0_gateT"]))
        load(l0f_lane, w_fc1, chunks_of(A["l0_fc1T"]))
        load(l0f_lane, w_fc2, chunks_of(A["l0_fc2T"]))
        whole = HID0 // P * P
        load(l0f_lane, w_proj[:, 0:HID0 // P], chunks_of(A["l0_projT"][0:whole], HID0 // P))
        load(l0f_lane, w_proj[0:HID0 - whole, NF0 - 1], A["l0_projT"][whole:])

        def l0_ffn():
            load_l1_weights()
            W = Arena(sbuf, WORK_AT, COLS)
            sel_f = W.f32(NF0 * P, 96)
            sl = lane("l0_selection_loaded")
            iota8 = W.f32(E0)
            sl.start(sp, iota8, A["iota"][:, 0:E0].broadcast_to([P, E0]))
            t_io = sl.start(sp, sel_f, A["l0_sel"])
            t_sel = act.done(act.after(t_io).activation(sel, sel_f, ACT.Copy))
            xn_ring = Ring([Buf(W.f32(BLK * D)) for _ in range(1)])
            xt_ring = Ring([Buf(W.f32(KD * BANK)) for _ in range(2)])
            r_ring = Ring([Buf(W.f32(400)) for _ in range(2)])
            cs_ring = [Buf(W.bf16(BLK * 96)) for _ in range(2)]
            for buf in cs_ring:
                buf.free = [dve.done(dve.api.memset(buf.ap, 0.0))]
            cs_ring = Ring(cs_ring)
            ct_ring = Ring([Buf(W.bf16(BANK)[0:96]) for _ in range(2)])
            th_ring = Ring([Buf(W.f32(BANK)) for _ in range(3)])
            h_ring = Ring([Buf(W.f32(BANK)) for _ in range(3)])
            ready = {}

            def router(xT, t_x, out):
                r = yield from r_ring.take()
                cuts, at = {}, 0
                for name, n in (("logit", 9), ("prob", 8), ("top", 8), ("comb", 9), ("eq", 8), ("index", 8), ("mx", 1), ("sum", 1), ("tmp", 9)):
                    cuts[name] = r.ap[:, at:at + BLK * n].rearrange("p (b n) -> p b n", b=BLK)
                    at += BLK * n
                idx_u = r.ap[:, at:at + BLK * 8].bitcast(U32).rearrange("p (b n) -> p b n", b=BLK)
                lg, pr, top, comb, eq, index, mx, sm, tmp = (cuts[n] for n in ("logit", "prob", "top", "comb", "eq", "index", "mx", "sum", "tmp"))
                bc8 = lambda a: a.broadcast_to([P, BLK, E0])
                ps = yield from psum.take(1)
                for i in range(BLK):
                    for k in range(KD):
                        last = pe.after(t_x, l0f_lane.token(), ps.free).matmul(
                            ps.ap[:, 16 * i:16 * i + 9], xT[:, k, i * P:(i + 1) * P], w_gate0[:, k, :],
                            start=(k == 0), stop=(k == KD - 1))
                t = pe.done(last)
                t = dve.done(dve.after(t, r.free).tensor_copy(lg, ps.ap[:, 0:16 * BLK].rearrange("p (b n) -> p b n", b=BLK)[:, :, 0:9]))
                ps.release(t)
                t = dve.done(dve.after(t).tensor_reduce(mx, lg[:, :, 0:8], AXX, ALU.max))
                t = dve.done(dve.after(t).tensor_tensor(pr, lg[:, :, 0:8], bc8(mx), ALU.subtract))
                t = act.done(act.after(t).activation(pr, pr, ACT.Exp))
                t_sg = act.done(act.api.activation(comb[:, :, 8:9], lg[:, :, 8:9], ACT.Tanh, scale=0.5))
                yield True
                t = dve.done(dve.after(t).tensor_reduce(sm, pr, AXX, ALU.add))
                t = dve.done(dve.after(t).reciprocal(sm, sm))
                t = dve.done(dve.after(t).tensor_tensor(pr, pr, bc8(sm), ALU.mult))
                for i in range(BLK):
                    t2 = dve.done(dve.after(t).max(top[:, i], pr[:, i]))
                    t3 = dve.done(dve.after(t2).max_index(idx_u[:, i], top[:, i], pr[:, i]))
                t = dve.done(dve.after(t3).tensor_copy(index, idx_u))
                iob = iota8.unsqueeze(1).broadcast_to([P, BLK, E0])
                for k in range(2):
                    dst = comb[:, :, 0:8] if k == 0 else tmp[:, :, 0:8]
                    t = dve.done(dve.after(t, t_io).tensor_tensor(eq, iob, bc8(index[:, :, k:k + 1]), ALU.is_equal))
                    t = dve.done(dve.after(t, t_sg).tensor_tensor(dst, eq, bc8(top[:, :, k:k + 1]), ALU.mult))
                t = dve.done(dve.after(t).tensor_tensor(comb[:, :, 0:8], comb[:, :, 0:8], tmp[:, :, 0:8], ALU.add))
                t = dve.done(dve.after(t).tensor_scalar(comb[:, :, 8:9], comb[:, :, 8:9], 0.5, 0.5, ALU.mult, ALU.add))
                t = dve.done(dve.after(t).tensor_scalar(comb, comb, 0.5, None, ALU.mult))
                cs = yield from cs_ring.take()
                c4 = cs.ap.rearrange("p (b i w) -> p b i w", b=BLK, i=3)
                t = dve.done(dve.after(t, cs.free).tensor_copy(c4[:, :, 0, 0:9], comb))
                t = dve.done(dve.after(t).tensor_tensor(tmp, comb, c4[:, :, 0, 0:9], ALU.subtract))
                t = dve.done(dve.after(t).tensor_copy(c4[:, :, 1, 0:9], tmp))
                t = dve.done(dve.after(t).tensor_tensor(c4[:, :, 2, 0:9], tmp, c4[:, :, 1, 0:9], ALU.subtract))
                r.release(t)
                yield True
                ps = yield from psum.take(1)
                pb = ps.ap.bitcast(BF16)[0:96, 0:BANK]
                t = transposes([(cs.ap[:, 96 * i:96 * i + 96], pb[:, i * P:(i + 1) * P]) for i in range(BLK)],
                               ps, ident_bf, t, ps.free)
                cs.release(t)
                ct = yield from ct_ring.take()
                t = dve.done(dve.after(t, ct.free).tensor_copy(ct.ap, pb))
                ps.release(t)
                out.append((ct, t))

            def hidden(blk, f, state):
                while blk not in ready:
                    yield False
                xT, t_x, ct, t_ct = ready[blk]
                if f == 0:
                    state["acc"] = yield from psum.take(2)
                while "acc" not in state:
                    yield False
                acc = state["acc"]
                M = min(P, HID0 - f * P)
                ps = yield from psum.take(2)
                gp = yield from psum.take(1)
                fs = slice(f * P, f * P + M)
                for n, w in enumerate((w_fc1, w_fc2)):
                    for k in range(KD):
                        last = pe.after(t_x, l0f_lane.token(), ps.free, gp.free).matmul(
                            ps.ap[0:M, n * BANK:(n + 1) * BANK], w[:, k, fs], split_cols(xT.ap, KD)[:, k, :], start=(k == 0), stop=(k == KD - 1))
                t_h = pe.done(last)
                t_g = pe.done(pe.after(t_ct, t_sel).matmul(gp.ap[0:M], sel[:, fs], ct.ap, start=True, stop=True))
                yield True
                h1, h2 = ps.ap[0:M, 0:BANK], ps.ap[0:M, BANK:2 * BANK]
                th = yield from th_ring.take()
                h = yield from h_ring.take()
                t = act.done(act.after(t_h, th.free).activation(th.ap[0:M], h1, ACT.Tanh, scale=0.5))
                t = dve.done(dve.after(t, h.free).scalar_tensor_tensor(h.ap[0:M], th.ap[0:M], 1.0, h1, ALU.add, ALU.mult))
                th.release(t)
                t = dve.done(dve.after(t).tensor_tensor(h.ap[0:M], h.ap[0:M], h2, ALU.mult))
                ps.release(t)
                t = dve.done(dve.after(t, t_g).tensor_tensor(h.ap[0:M], h.ap[0:M], gp.ap[0:M], ALU.mult))
                gp.release(t)
                yield True
                n = state["chunks"]
                state["chunks"] += 1
                for i in range(BLK):
                    last = pe.after(t, acc.free).matmul(acc.ap[:, i * D:(i + 1) * D], h.ap[0:M, i * P:(i + 1) * P], w_proj[0:M, f, :],
                                                        start=(n == 0 and i % 2 == 0), stop=(n == NF0 - 1), skip_group_check=True)
                t = pe.done(last)
                h.release(t)
                if n == NF0 - 1:
                    xT.release(t)
                    ct.release(t)
                    xs = x_all[:, blk * BLK * D:(blk + 1) * BLK * D]
                    t = dve.done(dve.after(t).scalar_tensor_tensor(xs, acc.ap, gates[:, 4:5], xs, ALU.mult, ALU.add))
                    acc.release(t)
                    for b in range(blk * BLK, (blk + 1) * BLK):
                        x_ready[b] = [t]

            def prologue(blk):
                xt = yield from xt_ring.take()
                xT = split_cols(xt.ap, KD)
                t_x = yield from norm_transpose(blk, xn_ring, xT, xt.free)
                got = []
                yield from router(xT, t_x, got)
                ready[blk] = (xt, t_x) + got[0]

            main = []
            for blk in range(NBLK):
                state = {"chunks": 0}
                main += [hidden(blk, f, state) for f in range(NF0)]
            run(interleave([interleave([prologue(i) for i in range(NBLK)], 1), interleave(main, 3)], 2))

        R1 = region_b
        l1_wq, l1_wk, l1_wv = (split_cols(R1.f32(KD * D), KD) for _ in range(3))
        l1_wo = split_cols(R1.f32(8 * D), 8)
        l1_gu = R1.f32(E1 * KD * 2 * D).rearrange("p (e k n) -> p e k n", e=E1, k=KD)
        l1_down = R1.f32(E1 * KD * D).rearrange("p (e k n) -> p e k n", e=E1, k=KD)
        l1_cos, l1_sin, l1_cosq, l1_sinq = (R1.f32(S) for _ in range(4))
        l1_gate = R1.f32(H1)
        l1_lane = lane("l1_weights_loaded")

        def load_l1_weights():
            t_zero = dve.done(dve.api.memset(l1_wo, 0.0))
            for n, dst in (("l1_wq", l1_wq), ("l1_wk", l1_wk), ("l1_wv", l1_wv)):
                load(l1_lane, dst, chunks_of(A[n]))
            for n, dst in (("l1_cos", l1_cos), ("l1_sin", l1_sin), ("l1_cosq", l1_cosq), ("l1_sinq", l1_sinq)):
                load(l1_lane, dst, A[n])
            load(l1_lane, l1_gate, A["l1_gate"].broadcast_to([P, H1]))
            wo = A["l1_wo"].rearrange("(j q d) o -> q d j o", q=4, d=HD1)
            for q in range(4):
                load(l1_lane, l1_wo[32 * q:32 * q + HD1], wo[q], t_zero)
            for e in range(E1):
                load(l1_lane, l1_gu[:, e], chunks_of(A["l1_gu"][e]))
                load(l1_lane, l1_down[:, e], chunks_of(A["l1_down"][e]))

        def store_parts(parts, dst, blk, t, n=BLK):
            p5 = parts.ap.rearrange("p (i c b n) -> p i c b n", i=3, c=KD, b=n)
            for i in range(n):
                for c in range(KD):
                    tok = parts.lane.start(sp, dst[blk * n + i, :, c * P:(c + 1) * P, :].rearrange("i r t -> r i t"), p5[:, :, c, i, :], t)
            return tok

        def load_stack(st, src, which, hd, *waits):
            for i in range(NT):
                st.lane.start(sp, st.ap[hd * i:hd * i + hd], src[which[i]].rearrange("(d h) t -> d (h t)", d=hd), st.free, *waits)
            return st.lane.token()

        def l1_attention():
            W = Arena(sbuf, WORK_AT, COLS)
            V = Arena(sbuf, A_AT, B_AT)
            L1_ON_ACT = (0, 2)
            PAIR = 2
            N = PAIR * S
            l1_gate_t = act.done(act.after(l1_lane.token()).activation(l1_gate, l1_gate, ACT.Tanh))
            xn_ring = Ring([Buf(W.f32(PAIR * D)) for _ in range(1)])
            xt_ring = Ring([Buf(W.f32(KD * N)) for _ in range(2)])
            rope_ring = Ring([Buf(W.f32(2 * KD * N)) for _ in range(1)])
            part_ring = Ring([Buf(W.bf16(3 * KD * N), lane(f"l1_parts_stored_{i}")) for i in range(2)])
            d_ring = Ring([Buf(W.f32(8 * P)) for _ in range(4)])
            e_ring = Ring([Buf(W.f32(8 * P)) for _ in range(4)])
            m_ring = Ring([Buf(W.f32(8)) for _ in range(4)])
            t_ring = Ring([Buf(W.f32(BANK + 16)) for _ in range(2)])
            mask_ring = Ring([Buf(W.f32(S), lane(f"mask_loaded_{i}")) for i in range(2)])
            q_ring, k_ring, a_ring = ([Buf(V.bf16(H1 * S), lane(f"l1_{n}_stack_loaded_{i}")) for i in range(2)] for n in "qka")
            for buf in q_ring + k_ring + a_ring:
                buf.free = [dve.done(dve.api.memset(buf.ap[0:96], 0.0))]
            q_ring, k_ring, a_ring = Ring(q_ring), Ring(k_ring), Ring(a_ring)
            v_ring = [Buf(V.f32(H1 * 32))] + [Buf(W.f32(H1 * 32)) for _ in range(3)]
            for buf in v_ring:
                t = dve.done(dve.api.memset(buf.ap, 0.0))
                buf.free = [dve.done(dve.after(t).memset(split_cols(buf.ap, H1)[:, :, HD1:HD1 + 1], 1.0))]
            v_ring = Ring(v_ring)
            at_ring = Ring([Buf(W.f32(8 * P)) for _ in range(1)])
            q_dram, k_dram, a_dram = (dram(f"l1_{n}_parts", [NB, 3, D, S], BF16) for n in "qka")
            sent, ready = {}, {}

            def project(w, src, waits, kind, dst, pair):
                ps = yield from psum.take(1)
                for c in range(KD):
                    for k in range(KD):
                        last = pe.after(waits, l1_lane.token(), ps.free).matmul(
                            ps.ap[:, c * N:(c + 1) * N], w[:, k, c * P:(c + 1) * P], src[:, k, :], start=(k == 0), stop=(k == KD - 1))
                t_m = t = pe.done(last)
                yield True
                r = yield from rope_ring.take()
                val, tmp = r.ap[:, 0:KD * N], r.ap[:, KD * N:2 * KD * N]
                if kind == "a":
                    t = act.done(act.after(t, r.free).activation(val, ps.ap, ACT.Copy))
                else:
                    cos, sin = (l1_cosq, l1_sinq) if kind == "q" else (l1_cos, l1_sin)
                    both = lambda a, n: a.unsqueeze(1).broadcast_to([P, n, S])
                    half = [split_cols(ps.ap[:, c * N:(c + 1) * N], PAIR) for c in range(2)]
                    v2 = [val[:, c * N:(c + 1) * N] for c in range(2)]
                    m2 = [tmp[:, c * N:(c + 1) * N] for c in range(2)]
                    dve.done(dve.after(t, r.free).tensor_tensor(split_cols(val, KD * PAIR), split_cols(ps.ap, KD * PAIR), both(cos, KD * PAIR), ALU.mult))
                    for c in range(2):
                        t = dve.done(dve.api.tensor_tensor(split_cols(m2[c], PAIR), half[1 - c], both(sin, PAIR), ALU.mult))
                ps.release(t)
                if kind != "a":
                    t1 = dve.done(dve.after(t).tensor_tensor(v2[0], v2[0], m2[0], ALU.subtract))
                    t = dve.done(dve.after(t1).tensor_tensor(v2[1], v2[1], m2[1], ALU.add))
                yield True
                parts = yield from part_ring.take()
                t = split3(val, parts.ap.rearrange("p (i n) -> p i n", i=3), tmp, t, parts.free)
                r.release(t)
                t = store_parts(parts, dst, pair, t, PAIR)
                parts.release(t)
                yield True
                return t_m, t

            def values_of(src, w, waits, v, kind):
                ps = yield from psum.take(1)
                for k in range(KD):
                    last = pe.after(waits, ps.free).matmul(ps.ap[:, 0:D], src[:, k, :], w[:, k, :], start=(k == 0), stop=(k == KD - 1))
                t = pe.done(last)
                yield True
                dst, got = split_cols(v.ap, H1)[:, :, 0:HD1], split_cols(ps.ap[:, 0:D], H1)
                if kind == "a":
                    t2 = dve.done(dve.after(t, v.free, l1_gate_t).tensor_tensor(dst, got, l1_gate.unsqueeze(2).broadcast_to([P, H1, HD1]), ALU.mult))
                else:
                    t2 = act.done(act.after(t, v.free).activation(dst, got, ACT.Copy))
                ps.release(t2)
                return t, t2

            def pair_prologue(pair):
                cT = ctxT[:, :, pair * N:(pair + 1) * N]
                _, t_a = yield from project(l1_wk, cT, None, "a", a_dram, pair)
                xt = yield from xt_ring.take()
                xT = split_cols(xt.ap, KD)
                t_x = yield from norm_transpose(pair, xn_ring, xT, xt.free, PAIR)
                t_mq, t_q = yield from project(l1_wq, xT, t_x, "q", q_dram, pair)
                t_mk, t_k = yield from project(l1_wk, xT, t_x, "k", k_dram, pair)
                sent[pair] = {"xt": xt, "x": t_x, "projected": [t_mq, t_mk], "q": t_q, "k": t_k, "a": t_a}

            def tile_prologue(b):
                pair, i = divmod(b, PAIR)
                q_st = yield from q_ring.take()
                k_st = yield from k_ring.take()
                a_st = yield from a_ring.take()
                while pair not in sent:
                    yield False
                p = sent[pair]
                t_a = load_stack(a_st, a_dram[b], PART_K, HD1, p["a"])
                t_q = load_stack(q_st, q_dram[b], PART_Q, HD1, p["q"])
                t_k = load_stack(k_st, k_dram[b], PART_K, HD1, p["k"])
                vs = yield from v_ring.take()
                va = yield from v_ring.take()
                mk = yield from mask_ring.take()
                t_m = load(mk.lane, mk.ap, A["mask1"][b], *mk.free)
                xT = split_cols(p["xt"].ap, KD)
                tp, t_vs = yield from values_of(xT[:, :, i * P:(i + 1) * P], l1_wv, p["x"], vs, "k")
                if i == PAIR - 1:
                    p["xt"].release(p["projected"], tp)
                _, t_va = yield from values_of(ctxT[:, :, b * S:(b + 1) * S], l1_wv, None, va, "a")
                yield True
                t_m = dve.done(dve.after(t_m).tensor_scalar(mk.ap, mk.ap, LOWEST, None, ALU.max))
                ready[b] = {"q": q_st, "k": k_st, "a": a_st, "vk": (vs, t_vs), "va": (va, t_va), "mask": mk,
                            "loaded": [t_q, t_k, t_a], "mask_ready": t_m}

            def unit(b, s, kind, state):
                while b not in ready:
                    yield False
                r = ready[b]
                m = yield from m_ring.take()
                d = yield from d_ring.take()
                ps = yield from psum.take(2)
                q3, k3 = split_cols(r["q"].ap, H1), split_cols(r[kind].ap, H1)
                s3, d3 = split_cols(ps.ap, 8), split_cols(d.ap, 8)
                for j in range(8):
                    last = pe.after(r["loaded"], ps.free).matmul(s3[:, j], q3[0:96, 8 * s + j, :], k3[0:96, 8 * s + j, :], start=True, stop=True)
                t = pe.done(last)
                state[kind] = state.get(kind, 0) + 1
                if state[kind] == 4:
                    r[kind].release(t)
                if state.get("k", 0) == 4 and state.get("a", 0) == 4:
                    r["q"].release(t)
                yield True
                if kind == "k":
                    t = dve.done(dve.after(t, r["mask_ready"], d.free).tensor_tensor(d3, s3, r["mask"].ap.unsqueeze(1).broadcast_to([P, 8, S]), ALU.add))
                    ps.release(t)
                    state["masked"] = state.get("masked", 0) + 1
                    if state["masked"] == 4:
                        r["mask"].release(t)
                    t = dve.done(dve.after(t, m.free).tensor_reduce(m.ap, d3, AXX, ALU.max, negate=True))
                    t = add_rows(d3, d3, m.ap, False, t, None)
                else:
                    t = dve.done(dve.after(t, m.free).tensor_reduce(m.ap, s3, AXX, ALU.max, negate=True))
                    t = add_rows(d3, s3, m.ap, s in L1_ON_ACT, t, d.free)
                    ps.release(t)
                m.release(t)
                yield True
                e = yield from e_ring.take()
                pt = yield from psum.take(2)
                p3 = split_cols(pt.ap, 8)
                t = transposes([(d3[:, j], p3[:, j]) for j in range(8)], pt, ident, t, pt.free)
                d.release(t)
                yield True
                t = act.done(act.after(t, e.free).activation(e.ap, pt.ap, ACT.Exp))
                pt.release(t)
                state["e", kind, s] = (e, t)

            def values(b, s, state):
                while ("e", "k", s) not in state or ("e", "a", s) not in state:
                    yield False
                av = yield from psum.take(1)
                for n, kind in enumerate("ka"):
                    e, t_e = state["e", kind, s]
                    v, t_v = ready[b]["v" + kind]
                    e3, v3 = split_cols(e.ap, 8), split_cols(v.ap, H1)
                    for j in range(2):
                        for q in range(4):
                            last = pe.after(t_e, t_v, av.free).matmul(av.ap[32 * q:32 * q + 32, (2 * n + j) * P:(2 * n + j + 1) * P], v3[:, 8 * s + 4 * j + q, :],
                                                                      e3[:, 4 * j + q, :], start=True, stop=True, tile_position=(0, 32 * q))
                t = pe.done(last)
                state["valued"] = state.get("valued", 0) + 1
                for kind in "ka":
                    state["e", kind, s][0].release(t)
                    if state["valued"] == 4:
                        ready[b]["v" + kind][0].release(t)
                yield True
                if state["valued"] and "attn" not in state and not state.get("taking"):
                    state["taking"] = True
                    state["attn"] = yield from at_ring.take()
                while "attn" not in state:
                    yield False
                at = state["attn"]
                tb = yield from t_ring.take()
                T, R = tb.ap[:, 0:BANK], tb.ap[:, BANK:BANK + 16]
                t = dve.done(dve.after(t, tb.free).transpose(T, av.ap))
                av.release(t)
                T3 = T.rearrange("p (n r) -> p n r", r=32)
                t = dve.done(dve.after(t).reciprocal(R, T3[:, :, HD1]))
                t = dve.done(dve.after(t).tensor_tensor(T3, T3, R.unsqueeze(2).broadcast_to([P, 16, 32]), ALU.mult))
                t = pool.done(pool.after(t).tensor_tensor(T[:, 0:D], T[:, 0:D], T[:, D:2 * D], ALU.add))
                yield True
                t = dve.done(dve.after(t, at.free).transpose(at.ap[:, s * D:(s + 1) * D], T[:, 0:D]))
                tb.release(t)
                state["out", s] = t

            def project_out(b, state):
                while any(("out", s) not in state for s in range(4)):
                    yield False
                at = state["attn"]
                po = yield from psum.take(1)
                a3 = split_cols(at.ap, 8)
                for j in range(8):
                    last = pe.after([state["out", s] for s in range(4)], po.free).matmul(po.ap[:, 0:D], a3[:, j], l1_wo[:, j, :], start=(j == 0), stop=(j == 7))
                t = pe.done(last)
                at.release(t)
                yield True
                t = dve.done(dve.after(t).scalar_tensor_tensor(X[b], po.ap[:, 0:D], gates[:, 1:2], X[b], ALU.mult, ALU.add))
                po.release(t)
                x_ready[b] = [t]

            main = []
            for b in range(NB):
                state = {}
                for s in range(4):
                    main += [unit(b, s, "k", state), unit(b, s, "a", state), values(b, s, state)]
                main.append(project_out(b, state))
            run(interleave([interleave([pair_prologue(i) for i in range(NB // PAIR)], 1),
                            interleave([tile_prologue(b) for b in range(NB)], 1), interleave(main, 6)], 3))

        def l1_ffn():
            load_l2_weights()
            W = Arena(sbuf, WORK_AT, COLS)
            xn_ring = Ring([Buf(W.f32(BLK * D)) for _ in range(2)])
            xT = split_cols(W.f32(KD * NB * S), KD)
            yT = split_cols(W.f32(KD * NB * S), KD)
            th_ring = Ring([Buf(W.f32(BANK)) for _ in range(3)])
            h_ring = Ring([Buf(W.f32(KD * BANK)) for _ in range(2)])
            of_expert = lambda a, k, e: a[:, k, :].rearrange("p (n e) -> p n e", e=E1)[:, :, e]
            t_x = []

            def norm(blk):
                t_x.append((yield from norm_transpose(blk, xn_ring, xT[:, :, blk * BANK:(blk + 1) * BANK], None)))
            run(interleave([norm(i) for i in range(NBLK)], 2))

            def half(e, c, h, h_free, out):
                ps = yield from psum.take(2)
                for n in range(2):
                    for k in range(KD):
                        last = pe.after(t_x, l1_lane.token(), ps.free).matmul(
                            ps.ap[:, n * BANK:(n + 1) * BANK], l1_gu[:, e, k, n * D + c * P:n * D + (c + 1) * P], of_expert(xT, k, e),
                            start=(k == 0), stop=(k == KD - 1))
                t = pe.done(last)
                yield True
                th = yield from th_ring.take()
                t = act.done(act.after(t, th.free).activation(th.ap, ps.ap[:, 0:BANK], ACT.Tanh, scale=0.5))
                t = dve.done(dve.after(t).scalar_tensor_tensor(th.ap, th.ap, 1.0, ps.ap[:, 0:BANK], ALU.add, ALU.mult))
                t = dve.done(dve.after(t, h_free).scalar_tensor_tensor(h[:, c], th.ap, 0.5, ps.ap[:, BANK:2 * BANK], ALU.mult, ALU.mult))
                ps.release(t)
                th.release(t)
                out.append(t)

            done_y = []

            def expert(e):
                h = yield from h_ring.take()
                h2, got = split_cols(h.ap, KD), []
                yield from interleave([half(e, c, h2, h.free, got) for c in range(KD)], 2)
                for c in range(KD):
                    ps = yield from psum.take(1)
                    for k in range(KD):
                        last = pe.after(got, ps.free).matmul(ps.ap, l1_down[:, e, k, c * P:(c + 1) * P], h2[:, k], start=(k == 0), stop=(k == KD - 1))
                    t_m = pe.done(last)
                    t = act.done(act.after(t_m).activation(of_expert(yT, c, e), ps.ap, ACT.Copy))
                    ps.release(t)
                    done_y.append(t)
                h.release(t_m)

            run(interleave([expert(e) for e in range(E1)], 2))

            def back(blk):
                ps = yield from psum.take(2)
                p4 = ps.ap.rearrange("p (b k n) -> p b k n", b=BLK, k=KD)
                t = transposes([(yT[:, k, (blk * BLK + i) * P:(blk * BLK + i + 1) * P], p4[:, i, k]) for i in range(BLK) for k in range(KD)],
                               ps, ident, done_y, ps.free)
                yield True
                xs = x_all[:, blk * BLK * D:(blk + 1) * BLK * D]
                t = dve.done(dve.after(t).scalar_tensor_tensor(xs, ps.ap, gates[:, 5:6], xs, ALU.mult, ALU.add))
                ps.release(t)
                for b in range(blk * BLK, (blk + 1) * BLK):
                    x_ready[b] = [t]
            run(interleave([back(i) for i in range(NBLK)], 2))

        R2 = Arena(sbuf, A_AT, B_AT)
        l2_wq, l2_wk, l2_wv = (split_cols(R2.f32(KD * D), KD) for _ in range(3))
        l2_wo = split_cols(R2.f32(4 * D), 4)
        l2_bq, l2_bk = R2.f32(KD), R2.f32(KD)
        l2_bv, l2_bo, l2_gamma, l2_beta = (R2.f32(D) for _ in range(4))
        l2_rs = R2.f32(1)
        l2_att, l2_attb = R2.f32(NB), R2.f32(NB)
        l2_mask = R2.f32(NB).bitcast(I32)
        l2_raw = [split_cols(R2.f32(KD * F2), KD) for _ in range(2)] + [split_cols(R2.f32(NF2 * D), NF2)]
        l2_q = [split_cols(R2.bf16(KD * F2), KD) for _ in range(2)] + [split_cols(R2.bf16(NF2 * D), NF2)]
        l2_lane = lane("l2_weights_loaded")

        def load_l2_weights():
            t_zero = dve.done(dve.api.memset(l2_wo, 0.0))
            for n, dst in (("l2_wqT", l2_wq), ("l2_wkT", l2_wk), ("l2_wvT", l2_wv), ("l2_wgT", l2_raw[0]), ("l2_wuT", l2_raw[1])):
                load(l2_lane, dst, chunks_of(A[n]))
            full = F2 // P
            load(l2_lane, l2_raw[2][:, 0:full], chunks_of(A["l2_wdT"][0:full * P], full))
            load(l2_lane, l2_raw[2][0:F2 - full * P, full], A["l2_wdT"][full * P:])
            load(l2_lane, l2_bq, A["l2_bq"])
            load(l2_lane, l2_bk, A["l2_bk"])
            for n, dst in enumerate((l2_bv, l2_bo, l2_gamma, l2_beta)):
                load(l2_lane, dst, A["l2_rows"][n:n + 1].broadcast_to([P, D]))
            load(l2_lane, l2_rs, A["l2_rs"].broadcast_to([P, 1]))
            load(l2_lane, l2_mask, A["mask2T"])
            wo = A["l2_woT"].rearrange("(j q d) o -> q d j o", q=4, d=HD2)
            for q in range(4):
                load(l2_lane, l2_wo[32 * q:32 * q + HD2], wo[q], t_zero)

        def l2_attention():
            load_l3_weights()
            W = Arena(sbuf, WORK_AT, COLS)
            t = dve.done(dve.after(l2_lane.token()).tensor_scalar(l2_rs, l2_rs, 0.0, 0.3, ALU.max, ALU.min))
            t = dve.done(dve.api.tensor_scalar(l2_att, l2_mask, 0.5, None, ALU.is_gt))
            t_att = dve.done(dve.after(t).tensor_scalar(l2_attb, l2_att, 1.0, 50.0, ALU.subtract, ALU.mult))
            PAIR = 2
            N = PAIR * S
            xn_ring = Ring([Buf(W.f32(PAIR * D)) for _ in range(1)])
            xt_ring = Ring([Buf(W.f32(KD * N)) for _ in range(2)])
            val_ring = Ring([Buf(W.f32(2 * KD * N)) for _ in range(2)])
            part_ring = Ring([Buf(W.bf16(3 * KD * N), lane(f"l2_parts_stored_{i}")) for i in range(2)])
            d_ring = Ring([Buf(W.f32(8 * P)) for _ in range(4)])
            t_ring = Ring([Buf(W.f32(D + 8)) for _ in range(2)])
            q_ring, k_ring = (Ring([Buf(W.bf16(H2 * S), lane(f"l2_{n}_stack_loaded_{i}")) for i in range(2)]) for n in "qk")
            v_ring = [Buf(W.f32(H2 * 32)) for _ in range(3)]
            for buf in v_ring:
                t = dve.done(dve.api.memset(buf.ap, 0.0))
                buf.free = [dve.done(dve.after(t).memset(split_cols(buf.ap, H2)[:, :, HD2:HD2 + 1], 1.0))]
            v_ring = Ring(v_ring)
            at_ring = Ring([Buf(W.f32(4 * P)) for _ in range(2)])
            y_ring = Ring([Buf(W.f32(D + 16)) for _ in range(2)])
            q_dram, k_dram = (dram(f"l2_{n}_parts", [NB, 3, D, S], BF16) for n in "qk")
            sent, ready = {}, {}

            def project(w, bias, scale, src, waits, dst, pair):
                ps = yield from psum.take(1)
                for c in range(KD):
                    for k in range(KD):
                        last = pe.after(waits, l2_lane.token(), ps.free).matmul(
                            ps.ap[:, c * N:(c + 1) * N], w[:, k, c * P:(c + 1) * P], src[:, k, :], start=(k == 0), stop=(k == KD - 1))
                t_m = pe.done(last)
                yield True
                r = yield from val_ring.take()
                val, tmp = r.ap[:, 0:KD * N], r.ap[:, KD * N:2 * KD * N]
                for c in range(KD):
                    t = dve.done(dve.after(t_m, r.free).tensor_scalar(val[:, c * N:(c + 1) * N], ps.ap[:, c * N:(c + 1) * N],
                                                                     bias[:, c:c + 1], scale, ALU.add, ALU.mult))
                ps.release(t)
                yield True
                parts = yield from part_ring.take()
                t = split3(val, parts.ap.rearrange("p (i n) -> p i n", i=3), tmp, t, parts.free)
                r.release(t)
                t = store_parts(parts, dst, pair, t, PAIR)
                parts.release(t)
                yield True
                return t_m, t

            def pair_prologue(pair):
                _, t_k = yield from project(l2_wk, l2_bk, 1.0, ctxT[:, :, pair * N:(pair + 1) * N], None, k_dram, pair)
                xt = yield from xt_ring.take()
                xT = split_cols(xt.ap, KD)
                t_x = yield from norm_transpose(pair, xn_ring, xT, xt.free, PAIR)
                t_m, t_q = yield from project(l2_wq, l2_bq, 0.25, xT, t_x, q_dram, pair)
                xt.release(t_m)
                sent[pair] = (t_q, t_k)

            def tile_prologue(b):
                v = yield from v_ring.take()
                ps = yield from psum.take(1)
                for k in range(KD):
                    last = pe.after(l2_lane.token(), ps.free).matmul(ps.ap[:, 0:D], ctxT[:, k, b * S:(b + 1) * S], l2_wv[:, k, :],
                                                                    start=(k == 0), stop=(k == KD - 1))
                t = pe.done(last)
                yield True
                t_v = dve.done(dve.after(t, v.free).tensor_tensor(split_cols(v.ap, H2)[:, :, 0:HD2], split_cols(ps.ap[:, 0:D], H2),
                                                                 split_cols(l2_bv, H2), ALU.add))
                ps.release(t_v)
                q_st = yield from q_ring.take()
                k_st = yield from k_ring.take()
                while b // PAIR not in sent:
                    yield False
                t_q, t_k = sent[b // PAIR]
                t_k = load_stack(k_st, k_dram[b], PART_K, HD2, t_k)
                t_q = load_stack(q_st, q_dram[b], PART_Q, HD2, t_q)
                yield True
                ready[b] = {"q": q_st, "k": k_st, "loaded": [t_q, t_k], "v": v, "v_ready": t_v}

            def unit(b, s, state):
                while b not in ready:
                    yield False
                r = ready[b]
                d = yield from d_ring.take()
                ps = yield from psum.take(2)
                q3, k3 = split_cols(r["q"].ap, H2), split_cols(r["k"].ap, H2)
                s3, d3 = split_cols(ps.ap, 8), split_cols(d.ap, 8)
                for j in range(8):
                    last = pe.after(r["loaded"], ps.free).matmul(s3[:, j], k3[0:96, 8 * s + j, :], q3[0:96, 8 * s + j, :], start=True, stop=True)
                t = pe.done(last)
                state["scored"] = state.get("scored", 0) + 1
                if state["scored"] == 2:
                    r["q"].release(t)
                    r["k"].release(t)
                yield True
                t = dve.done(dve.after(t, d.free).tensor_scalar(d.ap, ps.ap, 50.0, -50.0, ALU.min, ALU.max))
                ps.release(t)
                t = act.done(act.after(t, t_att).activation(d.ap, d.ap, ACT.Exp, bias=l2_attb[:, b:b + 1], scale=l2_att[:, b:b + 1]))
                yield True
                av = yield from psum.take(1)
                v3 = split_cols(r["v"].ap, H2)
                for j in range(2):
                    for q in range(4):
                        last = pe.after(t, r["v_ready"], av.free).matmul(av.ap[32 * q:32 * q + 32, j * P:(j + 1) * P], v3[:, 8 * s + 4 * j + q, :],
                                                                d3[:, 4 * j + q, :], start=True, stop=True, tile_position=(0, 32 * q))
                t = pe.done(last)
                d.release(t)
                state["valued"] = state.get("valued", 0) + 1
                if state["valued"] == 2:
                    r["v"].release(t)
                if state["valued"] == 1:
                    state["attn"] = yield from at_ring.take()
                yield True
                while "attn" not in state:
                    yield False
                at = state["attn"]
                state["out", s] = yield from normalise(av, D, HD2, at.ap[:, s * D:(s + 1) * D], t, at.free, t_ring)

            def project_out(b, state):
                while ("out", 0) not in state or ("out", 1) not in state:
                    yield False
                at = state["attn"]
                po = yield from psum.take(1)
                for j in range(4):
                    last = pe.after(state["out", 0], state["out", 1], po.free).matmul(po.ap[:, 0:D], at.ap[:, j * P:(j + 1) * P], l2_wo[:, j, :],
                                                                                      start=(j == 0), stop=(j == 3))
                t = pe.done(last)
                at.release(t)
                yield True
                y = yield from y_ring.take()
                d, s = y.ap[:, 0:D], y.ap[:, D:D + 16]
                t = dve.done(dve.after(t, y.free).tensor_tensor(d, po.ap[:, 0:D], l2_bo, ALU.add))
                po.release(t)
                t = dve.done(dve.after(t).tensor_scalar(d, d, l2_rs, None, ALU.mult))
                t = dve.done(dve.after(t).bn_stats(s[:, 0:6], d))
                t = dve.done(dve.after(t).bn_aggr(s[:, 6:8], s[:, 0:6]))
                t = rstd(s[:, 8:9], s[:, 7:8], EPS_LN, 1.0, t)
                yield True
                t = dve.done(dve.after(t).tensor_scalar(d, d, s[:, 6:7], s[:, 8:9], ALU.subtract, ALU.mult))
                t = pool.done(pool.after(t).tensor_tensor(d, d, l2_gamma, ALU.mult))
                t = pool.done(pool.after(t).tensor_tensor(d, d, l2_beta, ALU.add))
                yield True
                t = dve.done(dve.after(t).scalar_tensor_tensor(X[b], d, gates[:, 2:3], X[b], ALU.mult, ALU.add))
                y.release(t)
                x_ready[b] = [t]

            main = []
            for b in range(NB):
                state = {}
                main += [unit(b, s, state) for s in range(2)] + [project_out(b, state)]
            run(interleave([interleave([pair_prologue(i) for i in range(NB // PAIR)], 1),
                            interleave([tile_prologue(b) for b in range(NB)], 1), interleave(main, 5)], 3))

        def l2_ffn():
            W = Arena(sbuf, WORK_AT, COLS)
            ones = W.f32(P)
            wsum, wscale = W.f32(16), W.f32(16)
            scratch = W.f32(NF2 * D)
            t_one = dve.done(dve.api.memset(ones, 1.0))
            t0 = dve.done(dve.api.memset(wsum, 0.0))
            raws = [(l2_raw[0], slice(0, P)), (l2_raw[1], slice(0, P)), (l2_raw[2][:, 0:NF2 - 1], slice(0, P)), (l2_raw[2][:, NF2 - 1], slice(0, F2 % P))]
            t = t0
            for n, (w, rows) in enumerate(raws):
                flat = w[rows] if n == 3 else w[rows].rearrange("p k n -> p (k n)")
                t = dve.done(dve.after(t).tensor_reduce(wsum[rows, n:n + 1], flat, AXX, ALU.add, apply_absolute_value=True))
            t = dve.done(dve.after(t).tensor_tensor(wsum[:, 2:3], wsum[:, 2:3], wsum[:, 3:4], ALU.add))
            got = []

            def total():
                ps = yield from psum.take(1)
                tm = pe.done(pe.after(t, t_one, ps.free).matmul(ps.ap[:, 0:4], ones, wsum[:, 0:4], start=True, stop=True))
                tv = dve.done(dve.after(tm).tensor_scalar(wscale[:, 0:4], ps.ap[:, 0:4], 1.0 / (F2 * D), 1e-5, ALU.mult, ALU.max))
                ps.release(tv)
                got.append(dve.done(dve.after(tv).reciprocal(wscale[:, 4:8], wscale[:, 0:4])))
            run(total())
            t_sc = got[0]
            t_w = []
            for n in range(3):
                parts = [(l2_raw[n], l2_q[n])] if n < 2 else [(l2_raw[2][:, 0:NF2 - 1], l2_q[2][:, 0:NF2 - 1]), (l2_raw[2][0:F2 % P, NF2 - 1], l2_q[2][0:F2 % P, NF2 - 1])]
                for w, q in parts:
                    rows = w.shape[0]
                    t = dve.done(dve.after(t_sc).tensor_scalar(w, w, wscale[0:rows, 4 + n:5 + n], ROUND, ALU.mult, ALU.add))
                    t = dve.done(dve.after(t).tensor_scalar(w, w, ROUND, -1.0, ALU.subtract, ALU.max))
                    t = dve.done(dve.after(t).tensor_scalar(q, w, 1.0, None, ALU.min))
                    t_w.append(t)
            xn_ring = Ring([Buf(W.f32(D)) for _ in range(3)])
            xq_ring = Ring([Buf(W.bf16(2 * D)) for _ in range(2)])
            s_ring = Ring([Buf(W.f32(16)) for _ in range(3)])
            th_ring = Ring([Buf(W.f32(F2)) for _ in range(2)])
            h_ring = Ring([Buf(W.f32(F2)) for _ in range(2)])
            hq_ring = Ring([Buf(W.bf16(NF2 * P)) for _ in range(2)])
            ht_ring = Ring([Buf(W.bf16(NF2 * P)) for _ in range(2)])
            HF = F2 // 2

            def tile(b):
                xn = yield from xn_ring.take()
                s = yield from s_ring.take()
                c = lambda i: s.ap[:, i:i + 1]
                t = yield from layer_norm(X[b], xn.ap, x_ready[b], xn.free)
                yield True
                t = dve.done(dve.after(t, s.free).tensor_reduce(c(0), xn.ap, AXX, ALU.max, apply_absolute_value=True))
                t = dve.done(dve.after(t).tensor_scalar(c(0), c(0), 1e-5, None, ALU.max))
                t = dve.done(dve.after(t).reciprocal(c(1), c(0)))
                t = dve.done(dve.after(t).tensor_scalar(c(1), c(1), 127.0, None, ALU.mult))
                t = dve.done(dve.after(t).tensor_scalar(xn.ap, xn.ap, c(1), ROUND, ALU.mult, ALU.add))
                t = dve.done(dve.after(t).tensor_scalar(xn.ap, xn.ap, ROUND, 127.0, ALU.subtract, ALU.min))
                xq = yield from xq_ring.take()
                xqa, xT = xq.ap[:, 0:D], split_cols(xq.ap[:, D:2 * D], KD)
                t = dve.done(dve.after(t, xq.free).tensor_scalar(xqa, xn.ap, -128.0, None, ALU.max))
                xn.release(t)
                t_a = dve.done(dve.api.tensor_scalar(c(2), c(0), wscale[:, 0:1], 1.0 / 127.0, ALU.mult, ALU.mult))
                t_b = dve.done(dve.api.tensor_scalar(c(3), c(0), wscale[:, 1:2], 1.0 / 127.0, ALU.mult, ALU.mult))
                t_c = dve.done(dve.after(t_a).tensor_scalar(c(4), c(2), 0.5, None, ALU.mult))
                t_d = dve.done(dve.after(t_b, t_c).tensor_tensor(c(5), c(4), c(3), ALU.mult))
                yield True
                px = yield from psum.take(1)
                pb = px.ap.bitcast(BF16)[:, 0:D]
                t = transposes([(xqa[:, k * P:(k + 1) * P], pb[:, k * P:(k + 1) * P]) for k in range(KD)], px, ident_bf, t, px.free)
                t = act.done(act.after(t).activation(xT, split_cols(pb, KD), ACT.Copy))
                px.release(t)
                yield True
                pg = yield from psum.take(2)
                pu = yield from psum.take(2)
                for ps, w in ((pg, l2_q[0]), (pu, l2_q[1])):
                    for h in range(2):
                        for k in range(KD):
                            last = pe.after(t, t_w, ps.free).matmul(ps.ap[:, h * BANK:h * BANK + HF], xT[:, k], w[:, k, h * HF:(h + 1) * HF],
                                                                    start=(k == 0), stop=(k == KD - 1))
                t = pe.done(last)
                xq.release(t)
                yield True
                th = yield from th_ring.take()
                hb = yield from h_ring.take()
                g2, u2 = (split_cols(p.ap, 2)[:, :, 0:HF] for p in (pg, pu))
                th2, h2 = split_cols(th.ap, 2), split_cols(hb.ap, 2)
                t = act.done(act.after(t, t_c, th.free).activation(th2, g2, ACT.Tanh, scale=c(4)))
                t = dve.done(dve.after(t, hb.free).scalar_tensor_tensor(h2, th2, 1.0, g2, ALU.add, ALU.mult))
                th.release(t)
                pg.release(t)
                t = dve.done(dve.after(t).tensor_tensor(h2, h2, u2, ALU.mult))
                pu.release(t)
                t = dve.done(dve.after(t).tensor_reduce(c(6), hb.ap, AXX, ALU.max, apply_absolute_value=True))
                t = dve.done(dve.after(t, t_d).tensor_scalar(c(6), c(6), c(5), 1e-5, ALU.mult, ALU.max))
                t = dve.done(dve.after(t).reciprocal(c(7), c(6)))
                t = dve.done(dve.after(t).tensor_scalar(c(7), c(7), c(5), 127.0, ALU.mult, ALU.mult))
                t_o = dve.done(dve.api.tensor_scalar(c(8), c(6), wscale[:, 2:3], 1.0 / 127.0, ALU.mult, ALU.mult))
                t_o = dve.done(dve.after(t_o).tensor_scalar(c(8), c(8), gates[:, 6:7], None, ALU.mult))
                t = dve.done(dve.after(t).tensor_scalar(hb.ap, hb.ap, c(7), ROUND, ALU.mult, ALU.add))
                hq = yield from hq_ring.take()
                t = dve.done(dve.after(t).tensor_scalar(hb.ap, hb.ap, ROUND, 127.0, ALU.subtract, ALU.min))
                t = dve.done(dve.after(t, hq.free).tensor_scalar(hq.ap[:, 0:F2], hb.ap, -128.0, None, ALU.max))
                hb.release(t)
                yield True
                pt = yield from psum.take(1)
                pb = pt.ap.bitcast(BF16)
                t = transposes([(hq.ap[:, f * P:min(F2, (f + 1) * P)], pb[0:min(P, F2 - f * P), f * P:(f + 1) * P]) for f in range(NF2)],
                               pt, ident_bf, t, pt.free)
                hq.release(t)
                ht = yield from ht_ring.take()
                full = (NF2 - 1) * P
                t1 = act.done(act.after(t, ht.free).activation(ht.ap[:, 0:full], pb[:, 0:full], ACT.Copy))
                t2 = act.done(act.api.activation(ht.ap[0:F2 - full, full:], pb[0:F2 - full, full:full + P], ACT.Copy))
                pt.release(t1, t2)
                yield True
                po = yield from psum.take(1)
                for f in range(NF2):
                    M = min(P, F2 - f * P)
                    last = pe.after(t1, t2, po.free).matmul(po.ap[:, 0:D], ht.ap[0:M, f * P:(f + 1) * P], l2_q[2][0:M, f, :],
                                                            start=(f == 0), stop=(f == NF2 - 1))
                t = pe.done(last)
                ht.release(t)
                yield True
                t = dve.done(dve.after(t, t_o).scalar_tensor_tensor(X[b], po.ap[:, 0:D], c(8), X[b], ALU.mult, ALU.add))
                po.release(t)
                s.release(t)
                x_ready[b] = [t]

            run(interleave([tile(b) for b in range(NB)], 3))

        R3 = Arena(sbuf, B_AT, WORK_AT)
        l3_wq = split_cols(R3.f32(KD * H3 * HD3), KD)
        l3_wk, l3_wv = (split_cols(R3.f32(KD * G3 * HD3), KD) for _ in range(2))
        l3_wo = split_cols(R3.f32(H3 * D), H3)
        l3_w = R3.f32(4)
        l3_lane = lane("l3_weights_loaded")
        x_slots = dram("l3_slot_inputs", [NSLOT, D], F32)
        y_slots = dram("l3_slot_outputs", [NSLOT + P, D], F32)
        slot_lane = lane("l3_slots_cleared")

        def load_l3_weights():
            load(l3_lane, l3_wq, chunks_of(A["l3_wq"]))
            load(l3_lane, l3_wk, chunks_of(A["l3_wk"]))
            load(l3_lane, l3_wv, chunks_of(A["l3_wv"]))
            load(l3_lane, l3_wo, chunks_of(A["l3_wo"], H3))
            load(l3_lane, l3_w[:, 0:2], A["l3_qkw"])

        def l3_attention():
            W = Arena(sbuf, WORK_AT, COLS)
            V = Arena(sbuf, A_AT, B_AT)
            ones = W.f32(1)
            t_one = dve.done(dve.api.memset(ones, 1.0))
            t_w = dve.done(dve.after(l3_lane.token()).tensor_scalar(l3_w[:, 2:3], l3_w[:, 0:1], l3_w[:, 1:2], float(HD3) ** -0.5, ALU.mult, ALU.mult))
            PAIR = 2
            N = PAIR * S
            xn_ring = Ring([Buf(W.f32(PAIR * D)) for _ in range(1)])
            xt_ring = Ring([Buf(W.f32(KD * N)) for _ in range(2)])
            q_ring = Ring([Buf(V.f32(H3 * N)) for _ in range(2)] + [Buf(W.f32(H3 * N))])
            sq_ring = Ring([Buf(W.f32(BANK)) for _ in range(2)])
            rq_ring = Ring([Buf(W.f32(PAIR * H3)) for _ in range(3)])
            kn_ring = Ring([Buf(V.f32(BANK + 8)) for _ in range(2)])
            kT_ring = Ring([Buf(V.f32(BANK)) for _ in range(3)])
            v_ring = Ring([Buf(V.f32(BANK)) for _ in range(3)])
            e_ring = Ring([Buf(W.f32(BANK)) for _ in range(4)])
            eT_ring = Ring([Buf(W.f32(BANK)) for _ in range(3)])
            m_ring = Ring([Buf(W.f32(8)) for _ in range(5)])
            o_ring = Ring([Buf(W.f32(H3 * P)) for _ in range(2)])
            sent, ready = {}, {}

            def queries(h2, xT, t_x, q, q_free, pss, out):
                sq = yield from sq_ring.take()
                ps = yield from psum.take(1)
                for j in range(2):
                    for k in range(KD):
                        last = pe.after(t_x, l3_lane.token(), ps.free).matmul(ps.ap[:, j * N:(j + 1) * N], l3_wq[:, k, (h2 + j) * P:(h2 + j + 1) * P], xT[:, k, :],
                                                                             start=(k == 0), stop=(k == KD - 1))
                t = pe.done(last)
                yield True
                t_s = act.done(act.after(t, sq.free).activation(sq.ap, ps.ap, ACT.Square))
                t_q = dve.done(dve.after(t_s, q_free).tensor_copy(q[:, h2 * N:(h2 + 2) * N], ps.ap))
                ps.release(t_q)
                yield True
                for j in range(2):
                    for i in range(PAIR):
                        col = i * H3 + h2 + j
                        last = pe.after(t_s, t_one, pss.free).matmul(pss.ap[:, col:col + 1], sq.ap[:, j * N + i * P:j * N + (i + 1) * P], ones, start=True, stop=True)
                t_ss = pe.done(last)
                sq.release(t_ss)
                out.append((t, t_q, t_ss))

            def pair_prologue(pair):
                xt = yield from xt_ring.take()
                xT = split_cols(xt.ap, KD)
                t_x = yield from norm_transpose(pair, xn_ring, xT, xt.free, PAIR)
                q = yield from q_ring.take()
                rq = yield from rq_ring.take()
                pss = yield from psum.take(1)
                out = []
                yield from interleave([queries(h, xT, t_x, q.ap, q.free, pss, out) for h in range(0, H3, 2)], 2)
                xt.release([o[0] for o in out])
                t = dve.done(dve.after([o[2] for o in out], rq.free).tensor_scalar(rq.ap, pss.ap[:, 0:PAIR * H3], 1.0 / HD3, EPS_RMS, ALU.mult, ALU.add))
                pss.release(t)
                t = pool.done(pool.after(t).tensor_tensor(rq.ap, rq.ap, half_neg.broadcast_to([P, PAIR * H3]), ALU.pow))
                sent[pair] = {"q": q, "rq": rq, "q_ready": [o[1] for o in out], "rq_ready": t, "units": 0, "exps": 0}
                yield True

            def tile_prologue(b):
                kn = yield from kn_ring.take()
                ps = yield from psum.take(1)
                for k in range(KD):
                    last = pe.after(l3_lane.token(), ps.free).matmul(ps.ap, ctxT[:, k, b * S:(b + 1) * S], l3_wk[:, k, :], start=(k == 0), stop=(k == KD - 1))
                t_k = pe.done(last)
                yield True
                n, ss = kn.ap[:, 0:BANK], kn.ap[:, BANK:BANK + 4]
                t = act.done(act.after(t_k, kn.free).activation(n, ps.ap, ACT.Square))
                t = dve.done(dve.after(t).tensor_reduce(ss, split_cols(n, G3), AXX, ALU.add))
                t = rstd(ss, ss, EPS_RMS, 1.0 / HD3, t)
                yield True
                t = dve.done(dve.after(t).tensor_tensor(split_cols(n, G3), split_cols(ps.ap, G3), ss.unsqueeze(2).broadcast_to([P, G3, HD3]), ALU.mult))
                ps.release(t)
                yield True
                kT = yield from kT_ring.take()
                pt = yield from psum.take(1)
                t = transposes([(n[:, g * P:(g + 1) * P], pt.ap[:, g * P:(g + 1) * P]) for g in range(G3)], pt, ident, t, pt.free)
                kn.release(t)
                yield True
                t = dve.done(dve.after(t, t_w, kT.free).tensor_scalar(kT.ap, pt.ap, l3_w[:, 2:3], None, ALU.mult))
                pt.release(t)
                v = yield from v_ring.take()
                pv = yield from psum.take(1)
                for k in range(KD):
                    last = pe.after(pv.free).matmul(pv.ap, ctxT[:, k, b * S:(b + 1) * S], l3_wv[:, k, :], start=(k == 0), stop=(k == KD - 1))
                t_m = pe.done(last)
                yield True
                t_v = act.done(act.after(t_m, v.free).activation(v.ap, pv.ap, ACT.Copy))
                pv.release(t_v)
                ready[b] = {"kT": kT, "kT_ready": t, "v": v, "v_ready": t_v}

            def unit(b, g, state):
                pair, i = divmod(b, PAIR)
                while b not in ready or pair not in sent:
                    yield False
                r, p = ready[b], sent[pair]
                q = split_cols(p["q"].ap, H3)
                m = yield from m_ring.take()
                e = yield from e_ring.take()
                ps = yield from psum.take(1)
                for j in range(4):
                    last = pe.after(p["q_ready"], r["kT_ready"], ps.free).matmul(
                        ps.ap[:, j * P:(j + 1) * P], q[:, 4 * g + j, i * P:(i + 1) * P], r["kT"].ap[:, g * P:(g + 1) * P], start=True, stop=True)
                t = pe.done(last)
                p["units"] += 1
                if p["units"] == PAIR * G3:
                    p["q"].release(t)
                state["scored"] = state.get("scored", 0) + 1
                if state["scored"] == G3:
                    r["kT"].release(t)
                yield True
                r4 = p["rq"].ap[:, i * H3 + 4 * g:i * H3 + 4 * g + 4]
                bias, rs = m.ap[:, 0:4], m.ap[:, 4:8]
                t = dve.done(dve.after(t, m.free).tensor_reduce(bias, split_cols(ps.ap, 4), AXX, ALU.max))
                t = dve.done(dve.after(t, p["rq_ready"]).scalar_tensor_tensor(bias, bias, -1.0, r4, ALU.mult, ALU.mult))
                for j in range(4):
                    t = act.done(act.after(t, e.free).activation(e.ap[:, j * P:(j + 1) * P], ps.ap[:, j * P:(j + 1) * P], ACT.Exp,
                                                                bias=bias[:, j:j + 1], scale=r4[:, j:j + 1], accum_out=rs[:, j:j + 1]))
                ps.release(t)
                p["exps"] += 1
                if p["exps"] == PAIR * G3:
                    p["rq"].release(t)
                yield True
                t = dve.done(dve.after(t).reciprocal(rs, rs))
                t = dve.done(dve.after(t).tensor_tensor(split_cols(e.ap, 4), split_cols(e.ap, 4), rs.unsqueeze(2).broadcast_to([P, 4, S]), ALU.mult))
                m.release(t)
                yield True
                eT = yield from eT_ring.take()
                pt = yield from psum.take(1)
                t = transposes([(e.ap[:, j * P:(j + 1) * P], pt.ap[:, j * P:(j + 1) * P]) for j in range(4)], pt, ident, t, pt.free)
                e.release(t)
                yield True
                t = act.done(act.after(t, eT.free).activation(eT.ap, pt.ap, ACT.Copy))
                pt.release(t)
                yield True
                po = yield from psum.take(1)
                t = pe.done(pe.after(t, r["v_ready"], po.free).matmul(po.ap, r["v"].ap[:, g * P:(g + 1) * P], eT.ap, start=True, stop=True))
                eT.release(t)
                state["valued"] = state.get("valued", 0) + 1
                if state["valued"] == G3:
                    r["v"].release(t)
                if state["valued"] == 1:
                    state["o"] = yield from o_ring.take()
                yield True
                while "o" not in state:
                    yield False
                o = state["o"]
                t = dve.done(dve.after(t, o.free).tensor_copy(o.ap[:, 4 * g * P:(4 * g + 4) * P], po.ap))
                po.release(t)
                state["out", g] = t

            def project_out(b, state):
                while any(("out", g) not in state for g in range(G3)):
                    yield False
                o = state["o"]
                po = yield from psum.take(1)
                for h in range(H3):
                    last = pe.after([state["out", g] for g in range(G3)], po.free).matmul(po.ap[:, 0:D], o.ap[:, h * P:(h + 1) * P], l3_wo[:, h, :],
                                                                                         start=(h == 0), stop=(h == H3 - 1))
                t = pe.done(last)
                o.release(t)
                yield True
                t = dve.done(dve.after(t).scalar_tensor_tensor(X[b], po.ap[:, 0:D], gates[:, 3:4], X[b], ALU.mult, ALU.add))
                po.release(t)
                x_ready[b] = [t]

            main = []
            for b in range(NB):
                state = {}
                main += [unit(b, g, state) for g in range(G3)] + [project_out(b, state)]
            run(interleave([interleave([pair_prologue(i) for i in range(NB // PAIR)], 1),
                            interleave([tile_prologue(b) for b in range(NB)], 1), interleave(main, 6)], 3))

        def l3_ffn():
            W = Arena(sbuf, A_AT, COLS)
            gate = split_cols(W.f32(KD * E3), KD)
            sgu = split_cols(W.f32(KD * 2 * SI3), KD)
            sd = split_cols(W.f32(2 * D), 2)
            iota, base = W.f32(E3), W.f32(E3)
            before_f = W.f32(P)
            before, ones = W.bf16(P), W.bf16(P)
            zeros = W.f32(2 * BANK)
            rl = lane("l3_router_weights_loaded")
            load(rl, gate, chunks_of(A["l3_gateT"]))
            load(rl, iota, A["iota"].broadcast_to([P, E3]))
            load(rl, base, A["slot_base"].broadcast_to([P, E3]))
            load(rl, before_f, A["before"])
            load(rl, sgu, chunks_of(A["l3_sguT"]))
            load(rl, sd[:, 0], A["l3_sdT"][0:P])
            load(rl, sd[0:SI3 - P, 1], A["l3_sdT"][P:SI3])
            t_z = dve.done(dve.api.memset(zeros, 0.0))
            for i in range(NSLOT // 512):
                slot_lane.start(sp, x_slots[i * 512:(i + 1) * 512].rearrange("(p r) n -> p (r n)", p=P), zeros, t_z)
            slot_lane.start(sp, y_slots[NSLOT:NSLOT + P], zeros[:, 0:D], t_z)
            t_bf = dve.done(dve.after(rl.token()).tensor_copy(before, before_f))
            t_on = dve.done(dve.api.memset(ones, 1.0))
            NW = 8
            w_ring = Ring([Buf((split_cols(W.f32(KD * 2 * I3), KD), W.f32(D, I3)), lane(f"expert_weights_loaded_{i}")) for i in range(NW)])
            xn_ring = Ring([Buf(W.f32(D), lane(f"rows_scattered_{i}")) for i in range(4)])
            xt_ring = Ring([Buf(W.f32(D)) for _ in range(2)])
            r_ring = Ring([Buf(W.f32(1300)) for _ in range(2)])
            keep_w = [W.f32(8) for _ in range(NB)]
            keep_i = [W.f32(8).bitcast(U32) for _ in range(NB)]
            cum_f = W.f32(E3)
            sel_bf = [W.bf16(2 * E3) for _ in range(3)]
            sel_ring = Ring([Buf(a) for a in sel_bf])
            sh_ring = Ring([Buf(W.f32(2 * SI3)) for _ in range(2)])
            shT_ring = Ring([Buf(W.f32(D)) for _ in range(2)])
            t_cum = dve.done(dve.api.memset(cum_f, 0.0))
            chain = {"cum": t_cum, "next": 0}
            scattered, t_slot = [], [None] * NB

            def route(b, xT, t_x, xn, t_xn):
                r = yield from r_ring.take()
                at = [0]

                def cut(n):
                    a = r.ap[:, at[0]:at[0] + n]
                    at[0] += n
                    return a
                prob, pick, keep_, slot = cut(E3), cut(E3), cut(E3), cut(E3)
                one = split_cols(cut(K3 * E3), K3)
                prod = split_cols(cut(K3 * E3), K3)
                idx = cut(8)
                idx_u = cut(8).bitcast(U32)
                mx, sm, s6 = cut(1), cut(1), cut(8)
                top = keep_w[b]
                ps = yield from psum.take(1)
                for k in range(KD):
                    last = pe.after(t_x, rl.token(), ps.free).matmul(ps.ap[:, 0:E3], xT[:, k], gate[:, k, :], start=(k == 0), stop=(k == KD - 1))
                t = pe.done(last)
                yield True
                t = dve.done(dve.after(t, r.free).tensor_reduce(mx, ps.ap[:, 0:E3], AXX, ALU.max, negate=True))
                t = act.done(act.after(t).activation(prob, ps.ap[:, 0:E3], ACT.Exp, bias=mx, accum_out=sm))
                ps.release(t)
                yield True
                t = dve.done(dve.after(t).reciprocal(sm, sm))
                t = dve.done(dve.after(t).tensor_scalar(prob, prob, sm, None, ALU.mult))
                t = dve.done(dve.after(t).max(top, prob))
                t = dve.done(dve.after(t).max_index(idx_u, top, prob))
                t = dve.done(dve.after(t).tensor_copy(idx, idx_u))
                t = dve.done(dve.after(t).tensor_tensor(one, iota.unsqueeze(1).broadcast_to([P, K3, E3]),
                                                       idx[:, 0:K3].unsqueeze(2).broadcast_to([P, K3, E3]), ALU.is_equal))
                t_p = dve.done(dve.after(t).tensor_reduce(pick, one.rearrange("p k e -> p e k"), AXX, ALU.add))
                while chain["next"] != b:
                    yield False
                sb = yield from sel_ring.take()
                chain["next"] = b + 1
                t1 = dve.done(dve.after(t_p, sb.free).tensor_copy(sb.ap[:, 0:E3], pick))
                t2 = dve.done(dve.after(chain["cum"]).tensor_copy(sb.ap[:, E3:2 * E3], cum_f))
                chain["cum"] = dve.done(dve.after(t2).tensor_tensor(cum_f, cum_f, pick, ALU.add))
                yield True
                pp = yield from psum.take(1)
                pe.after(t1, t2, t_bf, t_on, pp.free).matmul(pp.ap[:, 0:E3], before, sb.ap[:, 0:E3], start=True, stop=False)
                t = pe.done(pe.api.matmul(pp.ap[:, 0:E3], ones, sb.ap[:, E3:2 * E3], start=False, stop=True))
                sb.release(t)
                yield True
                t1 = dve.done(dve.after(t).tensor_scalar(keep_, pp.ap[:, 0:E3], float(CAP3), None, ALU.is_lt))
                t2 = dve.done(dve.api.tensor_tensor(slot, pp.ap[:, 0:E3], base, ALU.add))
                pp.release(t1, t2)
                t = dve.done(dve.after(t1, t2).tensor_tensor(slot, slot, keep_, ALU.mult))
                t = dve.done(dve.after(t).tensor_tensor(prod, one, slot.unsqueeze(1).broadcast_to([P, K3, E3]), ALU.mult))
                t = dve.done(dve.after(t).tensor_reduce(s6[:, 0:K3], prod, AXX, ALU.add))
                t = dve.done(dve.after(t).tensor_scalar(keep_i[b][:, 0:K3], s6[:, 0:K3], float(NSLOT), None, ALU.add))
                r.release(t)
                t_slot[b] = t
                for k in range(K3):
                    pool.after(t, t_xn, slot_lane.token()).indirect_dma_start(
                        out=x_slots[:, :], out_offset=bass.IndirectOffsetOnAxis(ap=keep_i[b][:, k:k + 1], axis=0),
                        in_=xn.ap, in_offset=None, bounds_check=NSLOT - 1, oob_is_err=False).then_inc(xn.lane.sem, 16)
                    xn.lane.count += 16
                xn.release(xn.lane.token())

            def shared(b, xT, t_x):
                ps = yield from psum.take(1)
                for k in range(KD):
                    last = pe.after(t_x, rl.token(), ps.free).matmul(ps.ap[:, 0:2 * SI3], xT[:, k], sgu[:, k, :], start=(k == 0), stop=(k == KD - 1))
                t_m = pe.done(last)
                yield True
                sh = yield from sh_ring.take()
                th, h = sh.ap[:, 0:SI3], sh.ap[:, SI3:2 * SI3]
                t = act.done(act.after(t_m, sh.free).activation(th, ps.ap[:, 0:SI3], ACT.Tanh, scale=0.5))
                t = dve.done(dve.after(t).scalar_tensor_tensor(th, th, 1.0, ps.ap[:, 0:SI3], ALU.add, ALU.mult))
                t = dve.done(dve.after(t).scalar_tensor_tensor(h, th, 0.5, ps.ap[:, SI3:2 * SI3], ALU.mult, ALU.mult))
                ps.release(t)
                yield True
                pt = yield from psum.take(1)
                t = transposes([(h[:, 0:P], pt.ap[:, 0:P]), (h[:, P:SI3], pt.ap[0:SI3 - P, P:2 * P])], pt, ident, t, pt.free)
                sh.release(t)
                hT = yield from shT_ring.take()
                t1 = act.done(act.after(t, hT.free).activation(hT.ap[:, 0:P], pt.ap[:, 0:P], ACT.Copy))
                t2 = act.done(act.api.activation(hT.ap[0:SI3 - P, P:2 * P], pt.ap[0:SI3 - P, P:2 * P], ACT.Copy))
                pt.release(t1, t2)
                yield True
                po = yield from psum.take(1)
                pe.after(t1, t2, po.free).matmul(po.ap[:, 0:D], hT.ap[:, 0:P], sd[:, 0], start=True, stop=False)
                t = pe.done(pe.api.matmul(po.ap[:, 0:D], hT.ap[0:SI3 - P, P:2 * P], sd[0:SI3 - P, 1], start=False, stop=True))
                hT.release(t)
                yield True
                t = dve.done(dve.after(t, x_ready[b]).scalar_tensor_tensor(X[b], po.ap[:, 0:D], gates[:, 7:8], X[b], ALU.mult, ALU.add))
                po.release(t)
                x_ready[b] = [t]
                return t_m

            def tile(b):
                xn = yield from xn_ring.take()
                t_xn = yield from layer_norm(X[b], xn.ap, x_ready[b], xn.free)
                xt = yield from xt_ring.take()
                ps = yield from psum.take(1)
                t = transposes([(xn.ap[:, k * P:(k + 1) * P], ps.ap[:, k * P:(k + 1) * P]) for k in range(KD)], ps, ident, t_xn, ps.free)
                xT = split_cols(xt.ap, KD)
                t_x = act.done(act.after(t, xt.free).activation(xt.ap, ps.ap[:, 0:D], ACT.Copy))
                ps.release(t_x)
                yield True
                yield from route(b, xT, t_x, xn, [t_xn, t])
                t = yield from shared(b, xT, t_x)
                xt.release(t)
                scattered.append(xn.lane)

            run(interleave([tile(b) for b in range(NB)], 2))
            all_in = [buf.lane.token() for buf in xn_ring.bufs]

            xe_ring = Ring([Buf(W.f32(D), lane(f"slot_rows_loaded_{i}")) for i in range(3)])
            xeT_ring = Ring([Buf(W.f32(D)) for _ in range(2)])
            he_ring = Ring([Buf(W.f32(2 * I3)) for _ in range(2)])
            heT_ring = Ring([Buf(W.f32(P, I3)) for _ in range(2)])
            ye_ring = Ring([Buf(W.f32(D), lane(f"slot_outputs_stored_{i}")) for i in range(3)])

            def pair(n):
                ws = []
                for i in range(2):
                    w = yield from w_ring.take()
                    w.lane.start(sp, w.ap[0], chunks_of(A["l3_gu"][2 * n + i]), *w.free)
                    t_w = w.lane.start(sp, w.ap[1], A["l3_down"][2 * n + i])
                    ws.append((w, t_w))
                xe = yield from xe_ring.take()
                t = xe.lane.start(sp, xe.ap, x_slots[n * P:(n + 1) * P], xe.free, all_in)
                yield True
                ps = yield from psum.take(1)
                t = transposes([(xe.ap[:, k * P:(k + 1) * P], ps.ap[:, k * P:(k + 1) * P]) for k in range(KD)], ps, ident, t, ps.free)
                xe.release(t)
                xT = yield from xeT_ring.take()
                xT3 = split_cols(xT.ap, KD)
                t = act.done(act.after(t, xT.free).activation(xT.ap, ps.ap[:, 0:D], ACT.Copy))
                ps.release(t)
                yield True
                pg = yield from psum.take(1)
                for k in range(KD):
                    for i, (w, t_w) in enumerate(ws):
                        last = pe.after(t, t_w, pg.free).matmul(pg.ap[64 * i:64 * i + 64, 0:2 * I3], xT3[:, k, 64 * i:64 * i + 64], w.ap[0][:, k, :],
                                                                start=(k == 0), stop=(k == KD - 1), tile_position=(0, 64 * i))
                t = pe.done(last)
                xT.release(t)
                yield True
                h = yield from he_ring.take()
                th, hh = h.ap[:, 0:I3], h.ap[:, I3:2 * I3]
                t = act.done(act.after(t, h.free).activation(th, pg.ap[:, 0:I3], ACT.Tanh, scale=0.5))
                t = dve.done(dve.after(t).scalar_tensor_tensor(th, th, 1.0, pg.ap[:, 0:I3], ALU.add, ALU.mult))
                t = dve.done(dve.after(t).scalar_tensor_tensor(hh, th, 0.5, pg.ap[:, I3:2 * I3], ALU.mult, ALU.mult))
                pg.release(t)
                yield True
                pt = yield from psum.take(1)
                t = transposes([(hh, pt.ap[0:I3, 0:P])], pt, ident, t, pt.free)
                h.release(t)
                hT = yield from heT_ring.take()
                t = dve.done(dve.after(t, hT.free).tensor_copy(hT.ap, pt.ap[0:I3, 0:P]))
                pt.release(t)
                yield True
                po = yield from psum.take(1)
                for i, (w, t_w) in enumerate(ws):
                    last = pe.after(t, po.free).matmul(po.ap[64 * i:64 * i + 64, 0:D], hT.ap[:, 64 * i:64 * i + 64], w.ap[1],
                                                       start=True, stop=True, tile_position=(0, 64 * i))
                t = pe.done(last)
                for w, _ in ws:
                    w.release(t)
                hT.release(t)
                yield True
                y = yield from ye_ring.take()
                t = act.done(act.after(t, y.free).activation(y.ap, po.ap[:, 0:D], ACT.Copy))
                po.release(t)
                y.release(y.lane.start(sp, y_slots[n * P:(n + 1) * P], y.ap, t))

            run(interleave([pair(n) for n in range(E3 // 2)], 4))
            all_out = [buf.lane.token() for buf in ye_ring.bufs] + [slot_lane.token()]

            g_ring = Ring([Buf(W.f32(K3 * D), lane(f"rows_gathered_{i}")) for i in range(4)])

            def combine(b):
                g = yield from g_ring.take()
                g3 = split_cols(g.ap, K3)
                for k in range(K3):
                    pool.after(g.free, all_out, t_slot[b]).indirect_dma_start(
                        out=g3[:, k], out_offset=None, in_=y_slots[:, :],
                        in_offset=bass.IndirectOffsetOnAxis(ap=keep_i[b][:, k:k + 1], axis=0)).then_inc(g.lane.sem, 16)
                    g.lane.count += 16
                yield True
                t = dve.done(dve.after(g.lane.token()).tensor_scalar(g3[:, 0], g3[:, 0], keep_w[b][:, 0:1], None, ALU.mult))
                for k in range(1, K3):
                    t = dve.done(dve.after(t).scalar_tensor_tensor(g3[:, 0], g3[:, k], keep_w[b][:, k:k + 1], g3[:, 0], ALU.mult, ALU.add))
                t = dve.done(dve.after(t, x_ready[b]).scalar_tensor_tensor(X[b], g3[:, 0], gates[:, 7:8], X[b], ALU.mult, ALU.add))
                g.release(t)
                x_ready[b] = [t]
            run(interleave([combine(b) for b in range(NB)], 3))

        stages = [l0_attention, l0_ffn, l1_attention, l1_ffn, l2_attention, l2_ffn, l3_attention, l3_ffn]
        for stage in stages[:last_stage]:
            stage()
            barrier()
        out_lane = lane("out_stored")
        for b in range(NB):
            out_lane.start(sp, out[b], X[b], x_ready[b])
        sp.after([l.token() for l in lanes if l.count])


def constants():
    c = {"ident": np.eye(P, dtype=np.float32)}
    inv = (1.0 / np.float32(10000.0) ** (np.arange(0, HD0, 2, dtype=np.float32) / np.float32(HD0))).astype(np.float32)

    def tables(n):
        f = (np.arange(n, dtype=np.float32)[None, :] * inv[:, None]).astype(np.float32)
        return np.cos(f), np.sin(f)
    cos, sin = tables(T0)
    scale = np.float32(1.0 / np.sqrt(HD0))
    cos8 = np.concatenate([cos, cos])
    sin8 = np.concatenate([-sin, sin])
    c["l0_cosq"] = (np.repeat(cos8, H0, 0) * scale).astype(np.float32)
    c["l0_sinq"] = (np.repeat(sin8, H0, 0) * scale).astype(np.float32)
    c["l0_cosk"] = np.repeat(cos8, G0, 0).astype(np.float32)
    c["l0_sink"] = np.repeat(sin8, G0, 0).astype(np.float32)
    sel = np.zeros((3, 32, NF0 * P), np.float32)
    for f in range(HID0):
        sel[:, min(f // F0, E0), f] = 1.0
    c["l0_sel"] = sel.reshape(96, NF0 * P)
    cos, sin = tables(S)
    c["l1_cos"] = np.repeat(cos, H1, 0).astype(np.float32)
    c["l1_sin"] = np.repeat(sin, H1, 0).astype(np.float32)
    c["l1_cosq"], c["l1_sinq"] = c["l1_cos"] * scale, c["l1_sin"] * scale
    c["iota"] = np.arange(E3, dtype=np.float32).reshape(1, E3)
    c["slot_base"] = (np.arange(E3, dtype=np.float32) * CAP3 - NSLOT).reshape(1, E3)
    c["before"] = np.triu(np.ones((P, P), np.float32), 1)
    return c


def layout(i):
    a = {n: i[n] for n in ("x", "ctx_2048", "g_xattn", "g_ffn")}
    half = [(d + HD0 // 2) % HD0 for d in range(HD0)]

    def head_minor(w, heads, hd):
        return w.reshape(heads, hd, -1).transpose(1, 0, 2)
    wq, bq = head_minor(i["L0_xattn_Wq"], H0, HD0), head_minor(i["L0_xattn_bq"], H0, HD0)
    wk, bk = head_minor(i["L0_xattn_Wk"], G0, HD0), head_minor(i["L0_xattn_bk"], G0, HD0)
    a["l0_wqT"], a["l0_wqpT"] = wq.reshape(P, P).T, wq[half].reshape(P, P).T
    a["l0_wkT"], a["l0_wkpT"] = wk.reshape(32, P).T, wk[half].reshape(32, P).T
    a["l0_bq2"] = np.stack([bq.reshape(P), bq[half].reshape(P)], 1)
    a["l0_bk2"] = np.stack([bk.reshape(32), bk[half].reshape(32)], 1)
    a["l0_wvT"] = i["L0_xattn_Wv"].T
    a["l0_bv"] = i["L0_xattn_bv"].reshape(1, 32)
    a["l0_bo"] = i["L0_xattn_bo"].reshape(P, 1)
    a["l0_woT"] = i["L0_xattn_Wo"].T
    e0 = E0 * F0
    a["l0_gateT"] = np.concatenate([i["L0_ffn_gate_w"], i["L0_ffn_shared_gate_w"]]).T
    a["l0_fc1T"] = np.concatenate([i["L0_ffn_expert_fc1"].reshape(e0, D), i["L0_ffn_shared_fc1"]]).T
    a["l0_fc2T"] = np.concatenate([i["L0_ffn_expert_fc2"].reshape(e0, D), i["L0_ffn_shared_fc2"]]).T
    a["l0_projT"] = np.concatenate([i["L0_ffn_expert_proj"].transpose(0, 2, 1).reshape(e0, D), i["L0_ffn_shared_proj"].T])

    def columns_head_minor(w, heads, hd):
        return w.reshape(-1, heads, hd).transpose(0, 2, 1).reshape(-1, heads * hd)
    a["mask1"] = i["mask_Bx1xSxS_fk0"].reshape(NB, S, S)
    a["l1_wq"] = columns_head_minor(i["L1_xattn_Wq"], H1, HD1)
    a["l1_wk"] = columns_head_minor(i["L1_xattn_Wk"], H1, HD1)
    a["l1_wv"], a["l1_wo"] = i["L1_xattn_Wv"], i["L1_xattn_Wo"]
    a["l1_gate"] = i["L1_xattn_gate"].reshape(1, H1)
    a["l1_gu"], a["l1_down"] = i["L1_ffn_gate_up_proj"], i["L1_ffn_down_proj"]
    a["mask2T"] = i["mask_BxS2_ik0"].T
    a["l2_wqT"] = columns_head_minor(i["L2_xattn_Wq"].T, H2, HD2)
    a["l2_wkT"] = columns_head_minor(i["L2_xattn_Wk"].T, H2, HD2)
    a["l2_wvT"], a["l2_woT"] = i["L2_xattn_Wv"].T, i["L2_xattn_Wo"].T
    for n in ("bq", "bk"):
        a["l2_" + n] = columns_head_minor(i["L2_xattn_" + n], H2, HD2).reshape(KD, P).T
    a["l2_rows"] = np.stack([i["L2_xattn_" + n] for n in ("bv", "bo", "ln_gamma", "ln_beta")])
    a["l2_rs"] = i["L2_xattn_residual_scale"].reshape(1, 1)
    a["l2_wgT"], a["l2_wuT"], a["l2_wdT"] = i["L2_ffn_w_gate"].T, i["L2_ffn_w_up"].T, i["L2_ffn_w_down"].T
    for n in ("Wq", "Wk", "Wv", "Wo"):
        a["l3_" + n.lower()] = i["L3_xattn_" + n]
    a["l3_qkw"] = np.stack([i["L3_xattn_q_norm_w"], i["L3_xattn_k_norm_w"]], 1)
    a["l3_gateT"] = i["L3_ffn_gate_w"].T
    a["l3_gu"], a["l3_down"] = i["L3_ffn_gate_up_proj"], i["L3_ffn_down_proj"]
    a["l3_sguT"] = np.concatenate([i["L3_ffn_shared_gate_w"], i["L3_ffn_shared_up_w"]]).T
    a["l3_sdT"] = i["L3_ffn_shared_down_w"].T
    return a


LAST_STAGE = 8


def kernel(**inputs):
    import concourse.bacc as _bacc
    from concourse.bass_utils import run_bass_kernel_spmd as _run

    nc = _bacc.Bacc("TRN2", target_bir_lowering=False, num_devices=1)
    arrays, aps = {}, {}
    host = {**layout({k: np.asarray(v) for k, v in inputs.items()}), **constants()}
    for name, a in host.items():
        a = np.ascontiguousarray(a)
        arrays[f"in_{name}"] = a
        aps[name] = nc.dram_tensor(f"in_{name}", a.shape, mybir.dt.from_np(a.dtype), kind="ExternalInput").ap()
    out = nc.dram_tensor("out_x", (NB, S, D), F32, kind="ExternalOutput").ap()
    program(nc, aps, out, LAST_STAGE)
    return _run(nc, [arrays], core_ids=[0]).results[0]["out_x"]
```

```python
from contextlib import ExitStack

import numpy as np

import concourse.bass as bass
from concourse import mybir

F32 = mybir.dt.float32
BF16 = mybir.dt.bfloat16
U32 = mybir.dt.uint32
I32 = mybir.dt.int32
ALU = mybir.AluOpType
ACT = mybir.ActivationFunctionType
AXX = mybir.AxisListType.X

P = 128
NB = 16
S = 128
D = 256
KD = D // P
BANK = 512
BLK = 4
NBLK = NB // BLK
EPS_LN = 1e-5
LOWEST = -3.38e38
ROUND = 12582912.0
TERMS = ((0, 3, 0), (1, 2, 3), (2, 1, 5))

H0, G0, HD0, T0 = 16, 4, 8, 256
E0, F0, FS0 = 8, 176, 704
HID0 = E0 * F0 + FS0
NF0 = -(-HID0 // P)
H1, HD1 = 32, 8
E1 = 4
H2, HD2 = 16, 16
F2 = 832
NF2 = -(-F2 // P)
H3, G3, HD3 = 16, 4, 128
E3, K3, CAP3, I3, SI3 = 64, 6, 64, 96, 192
NSLOT = E3 * CAP3
EPS_RMS = 1e-6


class Engine:

    def __init__(self, api, sem):
        self.api, self.sem, self.count, self.seen = api, sem, 0, {}

    def after(self, *tokens):
        for t in tokens:
            if isinstance(t, list):
                self.after(*t)
            elif t is not None:
                name, sem, value = t
                if self.seen.get(name, 0) < value:
                    self.api.wait_ge(sem, value)
                    self.seen[name] = value
        return self.api

    def done(self, instruction):
        self.count += 1
        instruction.then_inc(self.sem, 1)
        return self.last()

    def last(self):
        return (id(self), self.sem, self.count)


class Lane:

    def __init__(self, sem):
        self.sem, self.count = sem, 0

    def start(self, engine, out, in_, *waits):
        engine.after(*waits).dma_start(out, in_).then_inc(self.sem, 16)
        self.count += 16
        return self.token()

    def token(self):
        return (id(self), self.sem, self.count)


class Buf:

    def __init__(self, ap, lane=None):
        self.ap, self.lane, self.free, self.held, self.age = ap, lane, [], False, 0

    def release(self, *tokens):
        self.free, self.held = list(tokens), False


class Ring:
    def __init__(self, bufs):
        self.bufs, self.clock = bufs, 0

    def take(self):
        while all(b.held for b in self.bufs):
            yield False
        buf = min((b for b in self.bufs if not b.held), key=lambda b: b.age)
        self.clock += 1
        buf.held, buf.age = True, self.clock
        return buf


class PsumBanks:

    def __init__(self, tensor):
        self.tensor, self.free, self.held = tensor, [[] for _ in range(8)], [False] * 8
        self.age, self.clock = [0] * 8, 0

    def take(self, n):
        while True:
            starts = [i for i in range(0, 8, n) if not any(self.held[i:i + n])]
            if starts:
                break
            yield False
        i = min(starts, key=lambda k: (max(self.age[k:k + n]), k))
        self.clock += 1
        for k in range(i, i + n):
            self.held[k], self.age[k] = True, self.clock
        return Banks(self, i, n)


class Banks:
    def __init__(self, pool, i, n):
        self.pool, self.i, self.n = pool, i, n
        self.ap = pool.tensor[:, i * BANK:(i + n) * BANK]
        self.free = [t for k in range(i, i + n) for t in pool.free[k]]

    def release(self, *tokens):
        for k in range(self.i, self.i + self.n):
            self.pool.held[k], self.pool.free[k] = False, list(tokens)
            self.pool.clock += 1
            self.pool.age[k] = self.pool.clock


def interleave(jobs, depth):
    jobs, active = list(jobs), []
    while jobs or active:
        while jobs and len(active) < depth:
            active.append(jobs.pop(0))
        moved = False
        for job in list(active)[::-1]:
            try:
                moved = (next(job) is not False) or moved
            except StopIteration:
                active.remove(job)
                moved = True
        if not moved:
            yield False
        else:
            yield True


def run(job):
    stuck = 0
    for moved in job:
        stuck = stuck + 1 if moved is False else 0
        if stuck > 200:
            raise RuntimeError("the jobs wait for each other")


class Arena:

    def __init__(self, tensor, lo, hi):
        self.tensor, self.at, self.lo, self.hi = tensor, lo, lo, hi

    def f32(self, cols, rows=P):
        a = self.at
        self.at += cols
        if self.at > self.hi:
            raise RuntimeError(f"arena full: {self.at} > {self.hi}")
        return self.tensor[0:rows, a:a + cols]

    def bf16(self, cols, rows=P):
        return self.f32(-(-cols // 2), rows).bitcast(BF16)[:, 0:cols]

    def reset(self):
        self.at = self.lo


def program(nc, A, out):
    ctx = ExitStack()
    with ctx:
        n_sem = [0]

        def sem(name):
            n_sem[0] += 1
            return ctx.enter_context(nc.semaphore(name))

        pe = Engine(nc.tensor, sem("pe_done"))
        dve = Engine(nc.vector, sem("dve_done"))
        act = Engine(nc.scalar, sem("act_done"))
        pool = Engine(nc.gpsimd, sem("pool_done"))
        sp = Engine(nc.sync, sem("sp_done"))
        engines = [pe, dve, act, pool, sp]
        lanes = []

        def lane(name):
            lanes.append(Lane(sem(name)))
            return lanes[-1]

        COLS = 52800
        sbuf = ctx.enter_context(nc.sbuf_tensor("sbuf", [P, COLS], F32))
        psum = PsumBanks(ctx.enter_context(nc.psum_tensor("psum", [P, 8 * BANK], F32)))

        def dram(name, shape, dtype):
            return nc.dram_tensor(name, shape, dtype, kind="Internal").ap()

        A_AT, B_AT, WORK_AT = 8800, 22900, 34300
        keep = Arena(sbuf, 0, A_AT)
        region_a = Arena(sbuf, A_AT, B_AT)
        region_b = Arena(sbuf, B_AT, WORK_AT)

        x_all = keep.f32(NB * D)
        X = [x_all[:, b * D:(b + 1) * D] for b in range(NB)]
        ctxT = keep.f32(KD * NB * S).rearrange("p (k n) -> p k n", k=KD)
        ident = keep.f32(P)
        ident_bf = keep.bf16(P)
        gates = keep.f32(8)
        half_neg = keep.f32(1)
        ln_cols = [keep.f32(16) for _ in range(6)]
        stat_ring = Ring([Buf(a) for a in ln_cols])

        const_lane = lane("const_loaded")
        x_lanes = [lane(f"x_loaded_{i}") for i in range(NBLK)]
        for name, dst in (("ident", ident),):
            const_lane.start(sp, dst, A[name])
        for name, lo in (("g_xattn", 0), ("g_ffn", 4)):
            const_lane.start(sp, gates[:, lo:lo + 4], A[name].rearrange("(a n) -> a n", a=1).broadcast_to([P, 4]))
        x_ready = []
        for b in range(NB):
            if b == 0:
                x_lanes[0].start(sp, x_all[:, 0:BLK * D].rearrange("p (b d) -> p b d", b=BLK), A["x"][0:BLK].rearrange("b s d -> s b d"))
            x_ready.append([])
        t_bf = dve.done(dve.after(const_lane.token()).tensor_copy(ident_bf, ident))
        t_half = dve.done(dve.api.memset(half_neg, -0.5))
        t_gate = act.done(act.after(const_lane.token()).activation(gates, gates, ACT.Tanh))
        for b in range(BLK):
            x_ready[b] = [x_lanes[0].token()]
        for e in (pe, dve, act, pool):
            e.after(t_bf, t_half, t_gate, const_lane.token())

        def barrier(but=()):
            ends = [e.last() for e in engines if e is not sp] + [l.token() for l in lanes if l.count and l not in but]
            for e in engines:
                e.after([t for t in ends if t[0] != id(e)])
                if e is not sp:
                    e.after(e.last())

        def cleared_stacks(arena, cols, name, n, engine):
            bufs = []
            for i in range(n):
                raw = arena.f32(cols // 2)
                bufs.append(Buf(raw.bitcast(BF16), lane(f"{name}_stack_loaded_{i}")))
                bufs[-1].free = [engine.done(engine.api.memset(raw[0:96], 0.0))]
            return Ring(bufs)

        def rstd(out_col, var_col, eps, scale, *waits):
            n = out_col.shape[-1]
            t = dve.done(dve.after(*waits).tensor_scalar(out_col, var_col, scale, eps, ALU.mult, ALU.add))
            return pool.done(pool.after(t).tensor_tensor(out_col, out_col,
                             half_neg.broadcast_to([P, n]) if n > 1 else half_neg, ALU.pow))

        def layer_norm(src, dst, waits, dst_free, kept=None):
            st = yield from stat_ring.take()
            s = st.ap
            t = dve.done(dve.after(waits, st.free).bn_stats(s[:, 0:6], src))
            t = dve.done(dve.after(t).bn_aggr(s[:, 6:8], s[:, 0:6]))
            t = rstd(s[:, 8:9], s[:, 7:8], EPS_LN, 1.0, t)
            yield True
            t = dve.done(dve.after(t, dst_free).tensor_scalar(dst, src, s[:, 6:7], s[:, 8:9],
                                                             ALU.subtract, ALU.mult))
            if kept is not None:
                t = dve.done(dve.api.tensor_copy(kept, s[:, 6:9:2]))
            st.release(t)
            return t

        def split3(src, dst, tmp, waits, dst_free):
            hi, mid, lo = (dst[:, i] for i in range(3))
            t = act.done(act.after(waits, dst_free).activation(hi, src, ACT.Copy))
            t = pool.done(pool.after(t, dst_free).tensor_tensor(tmp, src, hi, ALU.subtract))
            t = act.done(act.after(t).activation(mid, tmp, ACT.Copy))
            return pool.done(pool.after(t).tensor_tensor(lo, tmp, mid, ALU.subtract))

        def add_rows(dst3, src3, col, on_act, waits, dst_free):
            if not on_act:
                return dve.done(dve.after(waits, dst_free).tensor_tensor(dst3, src3, col.unsqueeze(2).broadcast_to(list(src3.shape)), ALU.add))
            for j in range(src3.shape[1]):
                last = act.after(waits, dst_free).activation(dst3[:, j], src3[:, j], ACT.Identity, bias=col[:, j:j + 1])
            return act.done(last)

        def transposes(blocks, ps, ident_ap, *waits):
            api = pe.after(*waits)
            for src, dst in blocks:
                last = api.transpose(dst, src, ident_ap)
            return pe.done(last)

        def normalise(av, width, head_w, dst, t_av, t_free, ring):
            nblk = width // 32
            tb = yield from ring.take()
            T = tb.ap[:, 0:width]
            R = tb.ap[:, width:width + nblk]
            t = dve.done(dve.after(t_av, tb.free).transpose(T, av.ap[:, 0:width]))
            av.release(t)
            T3 = T.rearrange("p (n r) -> p n r", r=32)
            t = dve.done(dve.after(t).reciprocal(R, T3[:, :, head_w]))
            t = dve.done(dve.after(t).tensor_tensor(
                T3, T3, R.unsqueeze(2).broadcast_to([P, nblk, 32]), ALU.mult))
            t = dve.done(dve.after(t, t_free).transpose(dst, T))
            tb.release(t)
            return t

        def load_stack(st, src, side, hd, *waits):
            for part, n, at in TERMS:
                dst = st.ap[hd * at:hd * (at + n)]
                if side == "q":
                    src_rows = src[part].rearrange("(d h) t -> d (h t)", d=hd).unsqueeze(0).broadcast_to([n, hd, dst.shape[1]])
                else:
                    src_rows = src[0:n].rearrange("i (d h) t -> i d (h t)", d=hd)
                st.lane.start(sp, dst, src_rows, st.free, *waits)
            return st.lane.token()

        def load(ln, dst, src, *waits):
            return ln.start(sp, dst, src, *waits)

        def l0_attention():
            A0 = Arena(sbuf, B_AT, COLS)
            wq = A0.f32(P)
            wqp = A0.f32(P)
            wk = A0.f32(2 * 32)
            wv = A0.f32(32)
            wo = A0.f32(4 * P).rearrange("p (j o) -> p j o", j=4)
            cosq, sinq = A0.f32(T0), A0.f32(T0)
            cosk, sink = A0.f32(T0, 32), A0.f32(T0, 32)
            bq = A0.f32(2)
            bk = A0.f32(2, 32)
            bo = A0.f32(1)
            bv = A0.f32(32)
            wl = lane("l0_attention_weights_loaded")
            t_zero = dve.done(dve.api.memset(wo, 0.0))
            load(wl, wq, A["l0_wqT"])
            load(wl, wqp, A["l0_wqpT"])
            load(wl, wk[:, 0:32], A["l0_wkT"])
            load(wl, wk[:, 32:64], A["l0_wkpT"])
            load(wl, wv, A["l0_wvT"])
            load(wl, cosq, A["l0_cosq"])
            load(wl, sinq, A["l0_sinq"])
            load(wl, cosk, A["l0_cosk"])
            load(wl, sink, A["l0_sink"])
            load(wl, bq, A["l0_bq2"])
            load(wl, bk, A["l0_bk2"])
            load(wl, bo, A["l0_bo"])
            load(wl, bv, A["l0_bv"].broadcast_to([P, 32]))
            for g in range(G0):
                load(wl, wo[32 * g:32 * g + HD0], A["l0_woT"][32 * g:32 * g + 32].rearrange("(j d) o -> d j o", d=HD0), t_zero)
            w_ready = wl.token()
            for i in range(1, NBLK):
                t = load(x_lanes[i], x_all[:, i * BLK * D:(i + 1) * BLK * D].rearrange("p (b d) -> p b d", b=BLK),
                         A["x"][i * BLK:(i + 1) * BLK].rearrange("b s d -> s b d"))
                for b in range(i * BLK, (i + 1) * BLK):
                    x_ready[b] = [t]

            ctx_ring = Ring([Buf(A0.f32(T0), lane(f"ctx_loaded_{i}")) for i in range(3)])
            xn_ring = Ring([Buf(A0.f32(T0)) for _ in range(2)])
            rope_ring = Ring([Buf(A0.f32(4 * T0)) for _ in range(2)])
            part_ring = Ring([Buf(A0.bf16(3 * T0), lane(f"q_parts_stored_{i}")) for i in range(2)])
            kpart_ring = Ring([Buf(A0.bf16(3 * T0, 32), lane(f"k_parts_stored_{i}")) for i in range(2)])
            q_ring = cleared_stacks(A0, H0 * T0, "l0_q", 2, pool)
            k_ring = cleared_stacks(A0, G0 * T0, "l0_k", 2, dve)
            v_ring = [Buf(A0.f32(2 * G0 * 32)) for i in range(2)]
            d_ring = Ring([Buf(A0.f32(4 * T0)) for _ in range(4)])
            e_ring = Ring([Buf(A0.f32(2 * 4 * P)) for _ in range(5)])
            m_ring = Ring([Buf(A0.f32(4)) for _ in range(4)])
            t_ring = Ring([Buf(A0.f32(BANK + 16)) for _ in range(2)])
            attn_ring = Ring([Buf(A0.f32(4 * T0)) for _ in range(2)])
            y_ring = Ring([Buf(A0.f32(T0)) for _ in range(2)])
            L0_ON_ACT = (0,)
            q_dram = dram("l0_q_parts", [NB, 3, P, T0], BF16)
            k_dram = dram("l0_k_parts", [NB, 3, 32, T0], BF16)
            for buf in v_ring:
                v4 = buf.ap.rearrange("p (c g w) -> p c g w", c=2, g=G0)
                t = dve.done(dve.api.memset(buf.ap, 0.0))
                buf.free = [dve.done(dve.after(t).memset(v4[:, :, :, HD0:HD0 + 1], 1.0))]
            v_ring = Ring(v_ring)

            ready = {}

            def unit(b, c, g, state):
                while b not in ready:
                    yield False
                r = ready[b]
                m = yield from m_ring.take()
                d = yield from d_ring.take()
                ps = yield from psum.take(2)
                api = pe.after(r["stacks_loaded"], ps.free)
                q3 = r["q"].ap.rearrange("p (h t) -> p h t", h=H0)
                k3 = r["k"].ap.rearrange("p (g t) -> p g t", g=G0)
                for j in range(4):
                    last = api.matmul(ps.ap[:, j * T0:(j + 1) * T0], q3[0:96, 4 * g + j, c * P:(c + 1) * P],
                                      k3[0:96, g, :], start=True, stop=True)
                t_s = pe.done(last)
                state["units"] += 1
                if state["units"] == 2 * G0:
                    r["q"].release(t_s)
                    r["k"].release(t_s)
                yield True
                s3 = ps.ap.rearrange("p (j t) -> p j t", j=4)
                d3 = d.ap.rearrange("p (j t) -> p j t", j=4)
                t = dve.done(dve.after(t_s, m.free).tensor_reduce(m.ap, s3, AXX, ALU.max, negate=True))
                t = add_rows(d3, s3, m.ap, g in L0_ON_ACT, t, d.free)
                ps.release(t)
                m.release(t)
                yield True
                e = yield from e_ring.take()
                pt = yield from psum.take(2)
                t = transposes([(d3[:, j, kc * P:(kc + 1) * P], pt.ap[:, (kc * 4 + j) * P:(kc * 4 + j + 1) * P])
                                for kc in range(2) for j in range(4)], pt, ident, t, pt.free)
                d.release(t)
                yield True
                t = act.done(act.after(t, e.free).activation(e.ap, pt.ap, ACT.Exp))
                pt.release(t)
                state["E"][c, g] = (e, t)

            def values(b, c, state):
                while any((c, g) not in state["E"] for g in range(G0)):
                    yield False
                if c == 0:
                    state["attn"] = yield from attn_ring.take()
                while "attn" not in state:
                    yield False
                at, v = state["attn"], ready[b]["v"]
                E = [state["E"][c, g] for g in range(G0)]
                av = yield from psum.take(1)
                v4 = v.ap.rearrange("p (c g w) -> p c g w", c=2, g=G0)
                for kc in range(2):
                    for g in range(G0):
                        last = pe.after(ready[b]["v_ready"], av.free, E[g][1]).matmul(
                            av.ap[32 * g:32 * g + 32, :], v4[:, kc, g, :], E[g][0].ap[:, kc * BANK:(kc + 1) * BANK],
                            start=(kc == 0), stop=(kc == 1), tile_position=(0, 32 * g))
                t = pe.done(last)
                for g in range(G0):
                    E[g][0].release(t)
                if c == 1:
                    v.release(t)
                yield True
                dst = at.ap.rearrange("p (c n) -> p c n", c=2)[:, c]
                state["out"][c] = yield from normalise(av, BANK, HD0, dst, t, at.free, t_ring)

            def project_out(b, state):
                while len(state["out"]) < 2:
                    yield False
                at = state["attn"]
                po = yield from psum.take(1)
                a4 = at.ap.rearrange("p (c j n) -> p j c n", c=2, j=4)
                for j in range(4):
                    last = pe.after(state["out"][0], state["out"][1], po.free).matmul(po.ap[:, 0:T0], wo[:, j, :], a4[:, j], start=(j == 0), stop=(j == 3))
                t = pe.done(last)
                at.release(t)
                yield True
                tmp = yield from y_ring.take()
                t = dve.done(dve.after(t, tmp.free).tensor_scalar(tmp.ap, po.ap[:, 0:T0], bo, gates[:, 0:1], ALU.add, ALU.mult))
                po.release(t)
                t = pool.done(pool.after(t).tensor_tensor(X[b], X[b], tmp.ap, ALU.add))
                tmp.release(t)
                x_ready[b] = [t]

            def prologue(b):
                cb = yield from ctx_ring.take()
                t_ctx = load(cb.lane, cb.ap, A["ctx_2048"][b], *cb.free)
                xn = yield from xn_ring.take()
                t_xn = yield from layer_norm(X[b], xn.ap, x_ready[b], xn.free)
                yield True
                pc = yield from psum.take(1)
                t = transposes([(cb.ap[:, k * P:(k + 1) * P], pc.ap[:, k * P:(k + 1) * P]) for k in range(KD)],
                               pc, ident, t_ctx, pc.free)
                t_c = act.done(act.after(t).activation(ctxT[:, :, b * S:(b + 1) * S],
                                                       pc.ap[:, 0:D].rearrange("p (k n) -> p k n", k=KD), ACT.Copy))
                pc.release(t_c)
                pq = yield from psum.take(1)
                pk = yield from psum.take(1)
                pv = yield from psum.take(1)
                api = pe.after(t_xn, w_ready, pq.free)
                api.matmul(pq.ap[:, 0:T0], wq, xn.ap, start=True, stop=True)
                t_q = pe.done(api.matmul(pq.ap[:, T0:2 * T0], wqp, xn.ap, start=True, stop=True))
                xn.release(t_q)
                api = pe.after(t_ctx, pk.free, pv.free)
                api.matmul(pk.ap[0:32, 0:T0], wk[:, 0:32], cb.ap, start=True, stop=True)
                api.matmul(pk.ap[0:32, T0:2 * T0], wk[:, 32:64], cb.ap, start=True, stop=True)
                api.matmul(pv.ap[:, 0:32], cb.ap[:, 0:P], wv, start=True, stop=True)
                t_kv = pe.done(api.matmul(pv.ap[:, 32:64], cb.ap[:, P:2 * P], wv, start=True, stop=True))
                cb.release(t_kv, t)
                yield True
                r = yield from rope_ring.take()
                q_a, q_b, k_a, k_b = (r.ap[:, i * T0:(i + 1) * T0] for i in range(4))
                t1 = dve.done(dve.after(t_q, r.free).scalar_tensor_tensor(q_a, pq.ap[:, 0:T0], bq[:, 0:1], cosq, ALU.add, ALU.mult))
                t2 = dve.done(dve.api.scalar_tensor_tensor(q_b, pq.ap[:, T0:2 * T0], bq[:, 1:2], sinq, ALU.add, ALU.mult))
                pq.release(t2)
                t_qr = dve.done(dve.after(t1, t2).tensor_tensor(q_a, q_a, q_b, ALU.add))
                t1 = dve.done(dve.after(t_kv).scalar_tensor_tensor(k_a[0:32], pk.ap[0:32, 0:T0], bk[:, 0:1], cosk, ALU.add, ALU.mult))
                t2 = dve.done(dve.api.scalar_tensor_tensor(k_b[0:32], pk.ap[0:32, T0:2 * T0], bk[:, 1:2], sink, ALU.add, ALU.mult))
                pk.release(t2)
                t_kr = dve.done(dve.after(t1, t2).tensor_tensor(k_a[0:32], k_a[0:32], k_b[0:32], ALU.add))
                v = yield from v_ring.take()
                v4 = v.ap.rearrange("p (c g w) -> p c g w", c=2, g=G0)
                bv3 = bv.rearrange("p (g w) -> p g w", g=G0)
                for c in range(2):
                    t_v = dve.done(dve.after(v.free).tensor_tensor(
                        v4[:, c, :, 0:HD0], pv.ap[:, 32 * c:32 * c + 32].rearrange("p (g w) -> p g w", g=G0), bv3, ALU.add))
                pv.release(t_v)
                yield True
                qp = yield from part_ring.take()
                kp = yield from kpart_ring.take()
                qp3 = qp.ap.rearrange("p (i t) -> p i t", i=3)
                kp3 = kp.ap.rearrange("p (i t) -> p i t", i=3)
                t_qs = split3(q_a, qp3, q_b, t_qr, qp.free)
                t_ks = split3(k_a[0:32], kp3, k_b[0:32], t_kr, kp.free)
                r.release(t_qs, t_ks)
                t_qw = qp.lane.start(sp, q_dram[b].rearrange("i r t -> r i t"), qp3, t_qs)
                t_kw = kp.lane.start(sp, k_dram[b].rearrange("i r t -> r i t"), kp3, t_ks)
                qp.release(t_qw)
                kp.release(t_kw)
                yield True
                q_st = yield from q_ring.take()
                k_st = yield from k_ring.take()
                load_stack(q_st, q_dram[b], "q", HD0, t_qw)
                load_stack(k_st, k_dram[b], "k", HD0, t_kw)
                if b == 1:
                    load_l0_ffn_weights()
                ready[b] = {"q": q_st, "k": k_st, "v": v, "v_ready": t_v, "stacks_loaded": [q_st.lane.token(), k_st.lane.token()]}

            def batch_jobs(b):
                state = {"units": 0, "E": {}, "out": {}}
                for c in range(2):
                    for g in range(G0):
                        yield unit(b, c, g, state)
                    yield values(b, c, state)
                yield project_out(b, state)

            main = [job for b in range(NB) for job in batch_jobs(b)]
            run(interleave([interleave([prologue(b) for b in range(NB)], 1), interleave(main, 5)], 2))

        def chunks_of(src, k=KD):
            return src.rearrange("(k p) n -> p k n", k=k)

        def split_cols(ap, k):
            return ap.rearrange("p (k n) -> p k n", k=k)

        def norm_transpose(blk, xn_ring, xnT, xnT_free, n=BLK):
            tiles = []
            xn = yield from xn_ring.take()
            for i in range(n):
                b = blk * n + i
                tile = xn.ap[:, i * D:(i + 1) * D]
                t = yield from layer_norm(X[b], tile, x_ready[b], xn.free)
                tiles.append((tile, t))
            yield True
            banks = KD * n * P // BANK
            ps = yield from psum.take(banks)
            p4 = ps.ap.rearrange("p (k b n) -> p k b n", k=KD, b=n)
            t = transposes([(xn_i[:, k * P:(k + 1) * P], p4[:, k, i]) for i, (xn_i, _) in enumerate(tiles) for k in range(KD)],
                           ps, ident, [t for _, t in tiles], ps.free)
            xn.release(t)
            yield True
            t = act.done(act.after(t, xnT_free).activation(xnT, split_cols(ps.ap, KD), ACT.Copy))
            ps.release(t)
            return t

        R0 = region_a
        w_fc1 = split_cols(R0.f32(KD * HID0), KD)
        w_fc2 = split_cols(R0.f32(KD * HID0), KD)
        w_proj = split_cols(R0.f32(NF0 * D), NF0)
        w_gate0 = split_cols(R0.f32(KD * 9), KD)
        sel = R0.bf16(NF0 * P)[0:96]
        l0f_lane = lane("l0_ffn_weights_loaded")

        def load_l0_ffn_weights():
            load(l0f_lane, w_gate0, chunks_of(A["l0_gateT"]))
            load(l0f_lane, w_fc1, chunks_of(A["l0_fc1T"]))
            load(l0f_lane, w_fc2, chunks_of(A["l0_fc2T"]))
            whole = HID0 // P * P
            load(l0f_lane, w_proj[:, 0:HID0 // P], chunks_of(A["l0_projT"][0:whole], HID0 // P))
            load(l0f_lane, w_proj[0:HID0 - whole, NF0 - 1], A["l0_projT"][whole:])

        def l0_ffn():
            W = Arena(sbuf, WORK_AT, COLS)
            sel_f = W.f32(NF0 * P, 96)
            sl = lane("l0_selection_loaded")
            iota8 = W.f32(E0)
            sl.start(sp, iota8, A["iota"][:, 0:E0].broadcast_to([P, E0]))
            t_io = sl.start(sp, sel_f, A["l0_sel"])
            load_l1_weights()
            t_sel = act.done(act.after(t_io).activation(sel, sel_f, ACT.Copy))
            xn_ring = Ring([Buf(W.f32(BLK * D)) for _ in range(1)])
            xt_ring = Ring([Buf(W.f32(KD * BANK)) for _ in range(2)])
            r_ring = Ring([Buf(W.f32(400)) for _ in range(2)])
            cs_ring = [Buf(W.bf16(BLK * 96)) for _ in range(2)]
            for buf in cs_ring:
                buf.free = [dve.done(dve.api.memset(buf.ap, 0.0))]
            cs_ring = Ring(cs_ring)
            ct_ring = Ring([Buf(W.bf16(BANK)[0:96]) for _ in range(2)])
            th_ring = Ring([Buf(W.f32(BANK)) for _ in range(3)])
            h_ring = Ring([Buf(W.f32(BANK)) for _ in range(3)])
            ready = {}

            def router(xT, t_x, out):
                r = yield from r_ring.take()
                cuts, at = {}, 0
                for name, n in (("logit", 9), ("prob", 8), ("top", 8), ("comb", 9), ("eq", 8), ("index", 8), ("mx", 1), ("sum", 1), ("tmp", 9)):
                    cuts[name] = r.ap[:, at:at + BLK * n].rearrange("p (b n) -> p b n", b=BLK)
                    at += BLK * n
                idx_u = r.ap[:, at:at + BLK * 8].bitcast(U32).rearrange("p (b n) -> p b n", b=BLK)
                lg, pr, top, comb, eq, index, mx, sm, tmp = (cuts[n] for n in ("logit", "prob", "top", "comb", "eq", "index", "mx", "sum", "tmp"))
                bc8 = lambda a: a.broadcast_to([P, BLK, E0])
                ps = yield from psum.take(1)
                for i in range(BLK):
                    for k in range(KD):
                        last = pe.after(t_x, l0f_lane.token(), ps.free).matmul(
                            ps.ap[:, 16 * i:16 * i + 9], xT[:, k, i * P:(i + 1) * P], w_gate0[:, k, :],
                            start=(k == 0), stop=(k == KD - 1))
                t = pe.done(last)
                t = dve.done(dve.after(t, r.free).tensor_copy(lg, ps.ap[:, 0:16 * BLK].rearrange("p (b n) -> p b n", b=BLK)[:, :, 0:9]))
                ps.release(t)
                t = dve.done(dve.after(t).tensor_reduce(mx, lg[:, :, 0:8], AXX, ALU.max))
                t = dve.done(dve.after(t).tensor_tensor(pr, lg[:, :, 0:8], bc8(mx), ALU.subtract))
                t = act.done(act.after(t).activation(pr, pr, ACT.Exp))
                t_sg = act.done(act.api.activation(comb[:, :, 8:9], lg[:, :, 8:9], ACT.Tanh, scale=0.5))
                yield True
                t = dve.done(dve.after(t).tensor_reduce(sm, pr, AXX, ALU.add))
                t = dve.done(dve.after(t).reciprocal(sm, sm))
                t = dve.done(dve.after(t).tensor_tensor(pr, pr, bc8(sm), ALU.mult))
                for i in range(BLK):
                    t2 = dve.done(dve.after(t).max(top[:, i], pr[:, i]))
                    t3 = dve.done(dve.after(t2).max_index(idx_u[:, i], top[:, i], pr[:, i]))
                t = dve.done(dve.after(t3).tensor_copy(index, idx_u))
                iob = iota8.unsqueeze(1).broadcast_to([P, BLK, E0])
                for k in range(2):
                    dst = comb[:, :, 0:8] if k == 0 else tmp[:, :, 0:8]
                    t = dve.done(dve.after(t, t_io).tensor_tensor(eq, iob, bc8(index[:, :, k:k + 1]), ALU.is_equal))
                    t = dve.done(dve.after(t, t_sg).tensor_tensor(dst, eq, bc8(top[:, :, k:k + 1]), ALU.mult))
                t = dve.done(dve.after(t).tensor_tensor(comb[:, :, 0:8], comb[:, :, 0:8], tmp[:, :, 0:8], ALU.add))
                t = dve.done(dve.after(t).tensor_scalar(comb[:, :, 8:9], comb[:, :, 8:9], 0.5, 0.5, ALU.mult, ALU.add))
                t = dve.done(dve.after(t).tensor_scalar(comb, comb, 0.5, None, ALU.mult))
                cs = yield from cs_ring.take()
                c4 = cs.ap.rearrange("p (b i w) -> p b i w", b=BLK, i=3)
                t = dve.done(dve.after(t, cs.free).tensor_copy(c4[:, :, 0, 0:9], comb))
                t = dve.done(dve.after(t).tensor_tensor(tmp, comb, c4[:, :, 0, 0:9], ALU.subtract))
                t = dve.done(dve.after(t).tensor_copy(c4[:, :, 1, 0:9], tmp))
                t = dve.done(dve.after(t).tensor_tensor(c4[:, :, 2, 0:9], tmp, c4[:, :, 1, 0:9], ALU.subtract))
                r.release(t)
                yield True
                ps = yield from psum.take(1)
                pb = ps.ap.bitcast(BF16)[0:96, 0:BANK]
                t = transposes([(cs.ap[:, 96 * i:96 * i + 96], pb[:, i * P:(i + 1) * P]) for i in range(BLK)],
                               ps, ident_bf, t, ps.free)
                cs.release(t)
                ct = yield from ct_ring.take()
                t = dve.done(dve.after(t, ct.free).tensor_copy(ct.ap, pb))
                ps.release(t)
                out.append((ct, t))

            def hidden(blk, f, state):
                while blk not in ready:
                    yield False
                xT, t_x, ct, t_ct = ready[blk]
                if f == 0:
                    state["acc"] = yield from psum.take(2)
                while "acc" not in state:
                    yield False
                acc = state["acc"]
                M = min(P, HID0 - f * P)
                ps = yield from psum.take(2)
                gp = yield from psum.take(1)
                fs = slice(f * P, f * P + M)
                for n, w in enumerate((w_fc1, w_fc2)):
                    for k in range(KD):
                        last = pe.after(t_x, l0f_lane.token(), ps.free, gp.free).matmul(
                            ps.ap[0:M, n * BANK:(n + 1) * BANK], w[:, k, fs], split_cols(xT.ap, KD)[:, k, :], start=(k == 0), stop=(k == KD - 1))
                t_h = pe.done(last)
                t_g = pe.done(pe.after(t_ct, t_sel).matmul(gp.ap[0:M], sel[:, fs], ct.ap, start=True, stop=True))
                yield True
                h1, h2 = ps.ap[0:M, 0:BANK], ps.ap[0:M, BANK:2 * BANK]
                th = yield from th_ring.take()
                h = yield from h_ring.take()
                t = act.done(act.after(t_h, th.free).activation(th.ap[0:M], h1, ACT.Tanh, scale=0.5))
                t = dve.done(dve.after(t, h.free).scalar_tensor_tensor(h.ap[0:M], th.ap[0:M], 1.0, h1, ALU.add, ALU.mult))
                th.release(t)
                t = dve.done(dve.after(t).tensor_tensor(h.ap[0:M], h.ap[0:M], h2, ALU.mult))
                ps.release(t)
                t = dve.done(dve.after(t, t_g).tensor_tensor(h.ap[0:M], h.ap[0:M], gp.ap[0:M], ALU.mult))
                gp.release(t)
                yield True
                n = state["chunks"]
                state["chunks"] += 1
                for i in range(BLK):
                    last = pe.after(t, acc.free).matmul(acc.ap[:, i * D:(i + 1) * D], h.ap[0:M, i * P:(i + 1) * P], w_proj[0:M, f, :],
                                                        start=(n == 0 and i % 2 == 0), stop=(n == NF0 - 1), skip_group_check=True)
                t = pe.done(last)
                h.release(t)
                if n == NF0 - 1:
                    xT.release(t)
                    ct.release(t)
                    xs = x_all[:, blk * BLK * D:(blk + 1) * BLK * D]
                    t = dve.done(dve.after(t).scalar_tensor_tensor(xs, acc.ap, gates[:, 4:5], xs, ALU.mult, ALU.add))
                    acc.release(t)
                    for b in range(blk * BLK, (blk + 1) * BLK):
                        x_ready[b] = [t]

            def prologue(blk):
                xt = yield from xt_ring.take()
                xT = split_cols(xt.ap, KD)
                t_x = yield from norm_transpose(blk, xn_ring, xT, xt.free)
                got = []
                yield from router(xT, t_x, got)
                ready[blk] = (xt, t_x) + got[0]

            main = []
            for blk in range(NBLK):
                state = {"chunks": 0}
                main += [hidden(blk, f, state) for f in range(NF0)]
            run(interleave([interleave([prologue(i) for i in range(NBLK)], 1), interleave(main, 3)], 2))

        R1 = region_b
        l1_wq, l1_wk, l1_wv = (split_cols(R1.f32(KD * D), KD) for _ in range(3))
        l1_wo = split_cols(R1.f32(8 * D), 8)
        l1_gu = R1.f32(E1 * KD * 2 * D).rearrange("p (e k n) -> p e k n", e=E1, k=KD)
        l1_down = R1.f32(E1 * KD * D).rearrange("p (e k n) -> p e k n", e=E1, k=KD)
        l1_cos, l1_sin, l1_cosq, l1_sinq = (R1.f32(S) for _ in range(4))
        l1_gate = R1.f32(H1)
        l1_lane = lane("l1_weights_loaded")

        def load_l1_weights():
            t_zero = dve.done(dve.api.memset(l1_wo, 0.0))
            for n, dst in (("l1_wq", l1_wq), ("l1_wk", l1_wk), ("l1_wv", l1_wv)):
                load(l1_lane, dst, chunks_of(A[n]))
            for n, dst in (("l1_cos", l1_cos), ("l1_sin", l1_sin), ("l1_cosq", l1_cosq), ("l1_sinq", l1_sinq)):
                load(l1_lane, dst, A[n])
            load(l1_lane, l1_gate, A["l1_gate"].broadcast_to([P, H1]))
            wo = A["l1_wo"].rearrange("(j q d) o -> q d j o", q=4, d=HD1)
            for q in range(4):
                load(l1_lane, l1_wo[32 * q:32 * q + HD1], wo[q], t_zero)
            for e in range(E1):
                load(l1_lane, l1_gu[:, e], chunks_of(A["l1_gu"][e]))
                load(l1_lane, l1_down[:, e], chunks_of(A["l1_down"][e]))

        def store_parts(parts, dst, blk, t, n=BLK):
            p5 = parts.ap.rearrange("p (i c b n) -> p i c b n", i=3, c=KD, b=n)
            for i in range(n):
                for c in range(KD):
                    tok = parts.lane.start(sp, dst[blk * n + i, :, c * P:(c + 1) * P, :].rearrange("i r t -> r i t"), p5[:, :, c, i, :], t)
            return tok

        def l1_attention():
            W = Arena(sbuf, WORK_AT, COLS)
            V = Arena(sbuf, A_AT, B_AT)
            PAIR = 2
            N = PAIR * S
            l1_gate_t = act.done(act.after(l1_lane.token()).activation(l1_gate, l1_gate, ACT.Tanh))
            xn_ring = Ring([Buf(W.f32(PAIR * D)) for _ in range(1)])
            xt_ring = Ring([Buf(W.f32(KD * N)) for _ in range(2)])
            rope_ring = Ring([Buf(W.f32(2 * KD * N)) for _ in range(1)])
            part_ring = Ring([Buf(W.bf16(3 * KD * N), lane(f"l1_parts_stored_{i}")) for i in range(2)])
            d_ring = Ring([Buf(W.f32(8 * P)) for _ in range(4)])
            e_ring = Ring([Buf(W.f32(8 * P)) for _ in range(4)])
            m_ring = Ring([Buf(W.f32(8)) for _ in range(4)])
            t_ring = Ring([Buf(W.f32(BANK + 16)) for _ in range(2)])
            mask_ring = Ring([Buf(W.f32(S), lane(f"mask_loaded_{i}")) for i in range(2)])
            a_ring = cleared_stacks(V, H1 * S, "l1_a", 2, pool)
            q_ring = cleared_stacks(V, H1 * S, "l1_q", 2, dve)
            k_ring = cleared_stacks(V, H1 * S, "l1_k", 2, pool)
            v_ring = [Buf(V.f32(H1 * 32))] + [Buf(W.f32(H1 * 32)) for _ in range(3)]
            for buf in v_ring:
                t = dve.done(dve.api.memset(buf.ap, 0.0))
                buf.free = [dve.done(dve.after(t).memset(split_cols(buf.ap, H1)[:, :, HD1:HD1 + 1], 1.0))]
            v_ring = Ring(v_ring)
            at_ring = Ring([Buf(W.f32(8 * P)) for _ in range(1)])
            q_dram, k_dram, a_dram = (dram(f"l1_{n}_parts", [NB, 3, D, S], BF16) for n in "qka")
            sent, ready = {}, {}

            def project(w, src, waits, kind, dst, pair):
                ps = yield from psum.take(1)
                for c in range(KD):
                    for k in range(KD):
                        last = pe.after(waits, l1_lane.token(), ps.free).matmul(
                            ps.ap[:, c * N:(c + 1) * N], w[:, k, c * P:(c + 1) * P], src[:, k, :], start=(k == 0), stop=(k == KD - 1))
                t_m = t = pe.done(last)
                yield True
                r = yield from rope_ring.take()
                val, tmp = r.ap[:, 0:KD * N], r.ap[:, KD * N:2 * KD * N]
                if kind == "a":
                    t = act.done(act.after(t, r.free).activation(val, ps.ap, ACT.Copy))
                else:
                    cos, sin = (l1_cosq, l1_sinq) if kind == "q" else (l1_cos, l1_sin)
                    both = lambda a, n: a.unsqueeze(1).broadcast_to([P, n, S])
                    half = [split_cols(ps.ap[:, c * N:(c + 1) * N], PAIR) for c in range(2)]
                    v2 = [val[:, c * N:(c + 1) * N] for c in range(2)]
                    m2 = [tmp[:, c * N:(c + 1) * N] for c in range(2)]
                    dve.done(dve.after(t, r.free).tensor_tensor(split_cols(val, KD * PAIR), split_cols(ps.ap, KD * PAIR), both(cos, KD * PAIR), ALU.mult))
                    for c in range(2):
                        t = dve.done(dve.api.tensor_tensor(split_cols(m2[c], PAIR), half[1 - c], both(sin, PAIR), ALU.mult))
                ps.release(t)
                if kind != "a":
                    t1 = dve.done(dve.after(t).tensor_tensor(v2[0], v2[0], m2[0], ALU.subtract))
                    t = dve.done(dve.after(t1).tensor_tensor(v2[1], v2[1], m2[1], ALU.add))
                yield True
                parts = yield from part_ring.take()
                t = split3(val, parts.ap.rearrange("p (i n) -> p i n", i=3), tmp, t, parts.free)
                r.release(t)
                t = store_parts(parts, dst, pair, t, PAIR)
                parts.release(t)
                yield True
                return t_m, t

            def values_of(src, w, waits, v, kind):
                ps = yield from psum.take(1)
                for k in range(KD):
                    last = pe.after(waits, ps.free).matmul(ps.ap[:, 0:D], src[:, k, :], w[:, k, :], start=(k == 0), stop=(k == KD - 1))
                t = pe.done(last)
                yield True
                dst, got = split_cols(v.ap, H1)[:, :, 0:HD1], split_cols(ps.ap[:, 0:D], H1)
                if kind == "a":
                    t2 = dve.done(dve.after(t, v.free, l1_gate_t).tensor_tensor(dst, got, l1_gate.unsqueeze(2).broadcast_to([P, H1, HD1]), ALU.mult))
                else:
                    t2 = act.done(act.after(t, v.free).activation(dst, got, ACT.Copy))
                ps.release(t2)
                return t, t2

            def pair_prologue(pair):
                cT = ctxT[:, :, pair * N:(pair + 1) * N]
                _, t_a = yield from project(l1_wk, cT, None, "a", a_dram, pair)
                xt = yield from xt_ring.take()
                xT = split_cols(xt.ap, KD)
                t_x = yield from norm_transpose(pair, xn_ring, xT, xt.free, PAIR)
                t_mq, t_q = yield from project(l1_wq, xT, t_x, "q", q_dram, pair)
                t_mk, t_k = yield from project(l1_wk, xT, t_x, "k", k_dram, pair)
                sent[pair] = {"xt": xt, "x": t_x, "projected": [t_mq, t_mk], "q": t_q, "k": t_k, "a": t_a}

            def tile_prologue(b):
                pair, i = divmod(b, PAIR)
                q_st = yield from q_ring.take()
                k_st = yield from k_ring.take()
                a_st = yield from a_ring.take()
                while pair not in sent:
                    yield False
                p = sent[pair]
                t_a = load_stack(a_st, a_dram[b], "k", HD1, p["a"])
                t_q = load_stack(q_st, q_dram[b], "q", HD1, p["q"])
                t_k = load_stack(k_st, k_dram[b], "k", HD1, p["k"])
                vs = yield from v_ring.take()
                va = yield from v_ring.take()
                mk = yield from mask_ring.take()
                t_m = load(mk.lane, mk.ap, A["mask1"][b], *mk.free)
                xT = split_cols(p["xt"].ap, KD)
                tp, t_vs = yield from values_of(xT[:, :, i * P:(i + 1) * P], l1_wv, p["x"], vs, "k")
                if i == PAIR - 1:
                    p["xt"].release(p["projected"], tp)
                _, t_va = yield from values_of(ctxT[:, :, b * S:(b + 1) * S], l1_wv, None, va, "a")
                yield True
                t_m = dve.done(dve.after(t_m).tensor_scalar(mk.ap, mk.ap, LOWEST, None, ALU.max))
                ready[b] = {"q": q_st, "k": k_st, "a": a_st, "vk": (vs, t_vs), "va": (va, t_va), "mask": mk,
                            "loaded": [t_q, t_k, t_a], "mask_ready": t_m}

            def unit(b, s, kind, state):
                while b not in ready:
                    yield False
                r = ready[b]
                m = yield from m_ring.take()
                d = yield from d_ring.take()
                ps = yield from psum.take(2)
                q3, k3 = split_cols(r["q"].ap, H1), split_cols(r[kind].ap, H1)
                s3, d3 = split_cols(ps.ap, 8), split_cols(d.ap, 8)
                for j in range(8):
                    last = pe.after(r["loaded"], ps.free).matmul(s3[:, j], q3[0:96, 8 * s + j, :], k3[0:96, 8 * s + j, :], start=True, stop=True)
                t = pe.done(last)
                state[kind] = state.get(kind, 0) + 1
                if state[kind] == 4:
                    r[kind].release(t)
                if state.get("k", 0) == 4 and state.get("a", 0) == 4:
                    r["q"].release(t)
                yield True
                if kind == "k":
                    t = dve.done(dve.after(t, r["mask_ready"], d.free).tensor_tensor(d3, s3, r["mask"].ap.unsqueeze(1).broadcast_to([P, 8, S]), ALU.add))
                    ps.release(t)
                    state["masked"] = state.get("masked", 0) + 1
                    if state["masked"] == 4:
                        r["mask"].release(t)
                    t = dve.done(dve.after(t, m.free).tensor_reduce(m.ap, d3, AXX, ALU.max, negate=True))
                    t = add_rows(d3, d3, m.ap, False, t, None)
                else:
                    t = dve.done(dve.after(t, m.free).tensor_reduce(m.ap, s3, AXX, ALU.max, negate=True))
                    t = add_rows(d3, s3, m.ap, True, t, d.free)
                    ps.release(t)
                m.release(t)
                yield True
                e = yield from e_ring.take()
                pt = yield from psum.take(2)
                p3 = split_cols(pt.ap, 8)
                t = transposes([(d3[:, j], p3[:, j]) for j in range(8)], pt, ident, t, pt.free)
                d.release(t)
                yield True
                t = act.done(act.after(t, e.free).activation(e.ap, pt.ap, ACT.Exp))
                pt.release(t)
                state["e", kind, s] = (e, t)

            def values(b, s, state):
                while ("e", "k", s) not in state or ("e", "a", s) not in state:
                    yield False
                av = yield from psum.take(1)
                for n, kind in enumerate("ka"):
                    e, t_e = state["e", kind, s]
                    v, t_v = ready[b]["v" + kind]
                    e3, v3 = split_cols(e.ap, 8), split_cols(v.ap, H1)
                    for j in range(2):
                        for q in range(4):
                            last = pe.after(t_e, t_v, av.free).matmul(av.ap[32 * q:32 * q + 32, (2 * n + j) * P:(2 * n + j + 1) * P], v3[:, 8 * s + 4 * j + q, :],
                                                                      e3[:, 4 * j + q, :], start=True, stop=True, tile_position=(0, 32 * q))
                t = pe.done(last)
                state["valued"] = state.get("valued", 0) + 1
                for kind in "ka":
                    state["e", kind, s][0].release(t)
                    if state["valued"] == 4:
                        ready[b]["v" + kind][0].release(t)
                yield True
                if state["valued"] and "attn" not in state and not state.get("taking"):
                    state["taking"] = True
                    state["attn"] = yield from at_ring.take()
                while "attn" not in state:
                    yield False
                at = state["attn"]
                tb = yield from t_ring.take()
                T, R = tb.ap[:, 0:BANK], tb.ap[:, BANK:BANK + 16]
                t = dve.done(dve.after(t, tb.free).transpose(T, av.ap))
                av.release(t)
                T3 = T.rearrange("p (n r) -> p n r", r=32)
                t = dve.done(dve.after(t).reciprocal(R, T3[:, :, HD1]))
                t = dve.done(dve.after(t).tensor_tensor(T3, T3, R.unsqueeze(2).broadcast_to([P, 16, 32]), ALU.mult))
                t = pool.done(pool.after(t).tensor_tensor(T[:, 0:D], T[:, 0:D], T[:, D:2 * D], ALU.add))
                yield True
                t = dve.done(dve.after(t, at.free).transpose(at.ap[:, s * D:(s + 1) * D], T[:, 0:D]))
                tb.release(t)
                state["out", s] = t

            def project_out(b, state):
                while any(("out", s) not in state for s in range(4)):
                    yield False
                at = state["attn"]
                po = yield from psum.take(1)
                a3 = split_cols(at.ap, 8)
                for j in range(8):
                    last = pe.after([state["out", s] for s in range(4)], po.free).matmul(po.ap[:, 0:D], a3[:, j], l1_wo[:, j, :], start=(j == 0), stop=(j == 7))
                t = pe.done(last)
                at.release(t)
                yield True
                t = dve.done(dve.after(t).scalar_tensor_tensor(X[b], po.ap[:, 0:D], gates[:, 1:2], X[b], ALU.mult, ALU.add))
                po.release(t)
                x_ready[b] = [t]

            main = []
            for b in range(NB):
                state = {}
                for s in range(4):
                    main += [unit(b, s, "k", state), unit(b, s, "a", state), values(b, s, state)]
                main.append(project_out(b, state))
            run(interleave([interleave([pair_prologue(i) for i in range(NB // PAIR)], 1),
                            interleave([tile_prologue(b) for b in range(NB)], 1), interleave(main, 6)], 3))

        def l1_ffn():
            load_l2_weights()
            W = Arena(sbuf, WORK_AT, COLS)
            xn_ring = Ring([Buf(W.f32(BLK * D)) for _ in range(2)])
            xT = split_cols(W.f32(KD * NB * S), KD)
            yT = split_cols(W.f32(KD * NB * S), KD)
            th_ring = Ring([Buf(W.f32(BANK)) for _ in range(3)])
            h_ring = Ring([Buf(W.f32(KD * BANK)) for _ in range(2)])
            of_expert = lambda a, k, e: a[:, k, :].rearrange("p (n e) -> p n e", e=E1)[:, :, e]
            t_x = []

            def norm(blk):
                t_x.append((yield from norm_transpose(blk, xn_ring, xT[:, :, blk * BANK:(blk + 1) * BANK], None)))
            run(interleave([norm(i) for i in range(NBLK)], 2))

            def half(e, c, h, h_free, out):
                ps = yield from psum.take(2)
                for n in range(2):
                    for k in range(KD):
                        last = pe.after(t_x, l1_lane.token(), ps.free).matmul(
                            ps.ap[:, n * BANK:(n + 1) * BANK], l1_gu[:, e, k, n * D + c * P:n * D + (c + 1) * P], of_expert(xT, k, e),
                            start=(k == 0), stop=(k == KD - 1))
                t = pe.done(last)
                yield True
                th = yield from th_ring.take()
                t = act.done(act.after(t, th.free).activation(th.ap, ps.ap[:, 0:BANK], ACT.Tanh, scale=0.5))
                t = dve.done(dve.after(t).scalar_tensor_tensor(th.ap, th.ap, 1.0, ps.ap[:, 0:BANK], ALU.add, ALU.mult))
                t = dve.done(dve.after(t, h_free).scalar_tensor_tensor(h[:, c], th.ap, 0.5, ps.ap[:, BANK:2 * BANK], ALU.mult, ALU.mult))
                ps.release(t)
                th.release(t)
                out.append(t)

            done_y = []

            def expert(e):
                h = yield from h_ring.take()
                h2, got = split_cols(h.ap, KD), []
                yield from interleave([half(e, c, h2, h.free, got) for c in range(KD)], 2)
                for c in range(KD):
                    ps = yield from psum.take(1)
                    for k in range(KD):
                        last = pe.after(got, ps.free).matmul(ps.ap, l1_down[:, e, k, c * P:(c + 1) * P], h2[:, k], start=(k == 0), stop=(k == KD - 1))
                    t_m = pe.done(last)
                    t = act.done(act.after(t_m).activation(of_expert(yT, c, e), ps.ap, ACT.Copy))
                    ps.release(t)
                    done_y.append(t)
                h.release(t_m)

            run(interleave([expert(e) for e in range(E1)], 2))

            def back(blk):
                ps = yield from psum.take(2)
                p4 = ps.ap.rearrange("p (b k n) -> p b k n", b=BLK, k=KD)
                t = transposes([(yT[:, k, (blk * BLK + i) * P:(blk * BLK + i + 1) * P], p4[:, i, k]) for i in range(BLK) for k in range(KD)],
                               ps, ident, done_y, ps.free)
                yield True
                xs = x_all[:, blk * BLK * D:(blk + 1) * BLK * D]
                t = dve.done(dve.after(t).scalar_tensor_tensor(xs, ps.ap, gates[:, 5:6], xs, ALU.mult, ALU.add))
                ps.release(t)
                for b in range(blk * BLK, (blk + 1) * BLK):
                    x_ready[b] = [t]
            run(interleave([back(i) for i in range(NBLK)], 2))

        R2 = Arena(sbuf, A_AT, B_AT)
        l2_wq, l2_wk, l2_wv = (split_cols(R2.f32(KD * D), KD) for _ in range(3))
        l2_wo = split_cols(R2.f32(4 * D), 4)
        l2_bq, l2_bk = R2.f32(KD), R2.f32(KD)
        l2_bv, l2_bo, l2_gamma, l2_beta = (R2.f32(D) for _ in range(4))
        l2_rs = R2.f32(1)
        l2_att, l2_attb = R2.f32(NB), R2.f32(NB)
        l2_mask = R2.f32(NB).bitcast(I32)
        l2_raw_at = R2.at
        l2_raw = [split_cols(R2.f32(KD * F2), KD) for _ in range(2)] + [split_cols(R2.f32(NF2 * D), NF2)]
        l2_raw_cols = R2.at - l2_raw_at
        l2_q = [split_cols(R2.bf16(KD * F2), KD) for _ in range(2)] + [split_cols(R2.bf16(NF2 * D), NF2)]
        l2_lane = lane("l2_weights_loaded")

        def load_l2_weights():
            t_zero = dve.done(dve.api.memset(l2_wo, 0.0))
            for n, dst in (("l2_wqT", l2_wq), ("l2_wkT", l2_wk), ("l2_wvT", l2_wv), ("l2_wgT", l2_raw[0]), ("l2_wuT", l2_raw[1])):
                load(l2_lane, dst, chunks_of(A[n]))
            full = F2 // P
            load(l2_lane, l2_raw[2][:, 0:full], chunks_of(A["l2_wdT"][0:full * P], full))
            load(l2_lane, l2_raw[2][0:F2 - full * P, full], A["l2_wdT"][full * P:])
            load(l2_lane, l2_bq, A["l2_bq"])
            load(l2_lane, l2_bk, A["l2_bk"])
            for n, dst in enumerate((l2_bv, l2_bo, l2_gamma, l2_beta)):
                load(l2_lane, dst, A["l2_rows"][n:n + 1].broadcast_to([P, D]))
            load(l2_lane, l2_rs, A["l2_rs"].broadcast_to([P, 1]))
            load(l2_lane, l2_mask, A["mask2T"])
            wo = A["l2_woT"].rearrange("(j q d) o -> q d j o", q=4, d=HD2)
            for q in range(4):
                load(l2_lane, l2_wo[32 * q:32 * q + HD2], wo[q], t_zero)

        def l2_attention(W, finished):
            t = dve.done(dve.after(l2_lane.token()).tensor_scalar(l2_rs, l2_rs, 0.0, 0.3, ALU.max, ALU.min))
            t = dve.done(dve.api.tensor_scalar(l2_att, l2_mask, 0.5, None, ALU.is_gt))
            t_att = dve.done(dve.after(t).tensor_scalar(l2_attb, l2_att, 1.0, 50.0, ALU.subtract, ALU.mult))
            PAIR = 2
            N = PAIR * S
            xn_ring = Ring([Buf(W.f32(PAIR * D)) for _ in range(1)])
            xt_ring = Ring([Buf(W.f32(KD * N)) for _ in range(2)])
            val_ring = Ring([Buf(W.f32(2 * KD * N)) for _ in range(2)])
            part_ring = Ring([Buf(W.bf16(3 * KD * N), lane(f"l2_parts_stored_{i}")) for i in range(2)])
            d_ring = Ring([Buf(W.f32(8 * P)) for _ in range(4)])
            t_ring = Ring([Buf(W.f32(D + 8)) for _ in range(2)])
            q_ring, k_ring = (Ring([Buf(W.bf16(H2 * S), lane(f"l2_{n}_stack_loaded_{i}")) for i in range(2)]) for n in "qk")
            v_ring = [Buf(W.f32(H2 * 32)) for _ in range(2)]
            for buf in v_ring:
                t = dve.done(dve.api.memset(buf.ap, 0.0))
                buf.free = [dve.done(dve.after(t).memset(split_cols(buf.ap, H2)[:, :, HD2:HD2 + 1], 1.0))]
            v_ring = Ring(v_ring)
            at_ring = Ring([Buf(W.f32(4 * P)) for _ in range(2)])
            y_ring = Ring([Buf(W.f32(D + 16)) for _ in range(2)])
            q_dram, k_dram = (dram(f"l2_{n}_parts", [NB, 3, D, S], BF16) for n in "qk")
            sent, ready = {}, {}

            def project(w, bias, scale, src, waits, dst, pair):
                ps = yield from psum.take(1)
                for c in range(KD):
                    for k in range(KD):
                        last = pe.after(waits, l2_lane.token(), ps.free).matmul(
                            ps.ap[:, c * N:(c + 1) * N], w[:, k, c * P:(c + 1) * P], src[:, k, :], start=(k == 0), stop=(k == KD - 1))
                t_m = pe.done(last)
                yield True
                r = yield from val_ring.take()
                val, tmp = r.ap[:, 0:KD * N], r.ap[:, KD * N:2 * KD * N]
                for c in range(KD):
                    t = dve.done(dve.after(t_m, r.free).tensor_scalar(val[:, c * N:(c + 1) * N], ps.ap[:, c * N:(c + 1) * N],
                                                                     bias[:, c:c + 1], scale, ALU.add, ALU.mult))
                ps.release(t)
                yield True
                parts = yield from part_ring.take()
                t = split3(val, parts.ap.rearrange("p (i n) -> p i n", i=3), tmp, t, parts.free)
                r.release(t)
                t = store_parts(parts, dst, pair, t, PAIR)
                parts.release(t)
                yield True
                return t_m, t

            def pair_prologue(pair):
                _, t_k = yield from project(l2_wk, l2_bk, 1.0, ctxT[:, :, pair * N:(pair + 1) * N], None, k_dram, pair)
                xt = yield from xt_ring.take()
                xT = split_cols(xt.ap, KD)
                t_x = yield from norm_transpose(pair, xn_ring, xT, xt.free, PAIR)
                t_m, t_q = yield from project(l2_wq, l2_bq, 0.25, xT, t_x, q_dram, pair)
                xt.release(t_m)
                sent[pair] = (t_q, t_k)

            def tile_prologue(b):
                v = yield from v_ring.take()
                ps = yield from psum.take(1)
                for k in range(KD):
                    last = pe.after(l2_lane.token(), ps.free).matmul(ps.ap[:, 0:D], ctxT[:, k, b * S:(b + 1) * S], l2_wv[:, k, :],
                                                                    start=(k == 0), stop=(k == KD - 1))
                t = pe.done(last)
                yield True
                t_v = dve.done(dve.after(t, v.free).tensor_tensor(split_cols(v.ap, H2)[:, :, 0:HD2], split_cols(ps.ap[:, 0:D], H2),
                                                                 split_cols(l2_bv, H2), ALU.add))
                ps.release(t_v)
                q_st = yield from q_ring.take()
                k_st = yield from k_ring.take()
                while b // PAIR not in sent:
                    yield False
                t_q, t_k = sent[b // PAIR]
                t_k = load_stack(k_st, k_dram[b], "k", HD2, t_k)
                t_q = load_stack(q_st, q_dram[b], "q", HD2, t_q)
                yield True
                ready[b] = {"q": q_st, "k": k_st, "loaded": [t_q, t_k], "v": v, "v_ready": t_v}

            def unit(b, s, state):
                while b not in ready:
                    yield False
                r = ready[b]
                d = yield from d_ring.take()
                ps = yield from psum.take(2)
                q3, k3 = split_cols(r["q"].ap, H2), split_cols(r["k"].ap, H2)
                s3, d3 = split_cols(ps.ap, 8), split_cols(d.ap, 8)
                for j in range(8):
                    last = pe.after(r["loaded"], ps.free).matmul(s3[:, j], k3[0:96, 8 * s + j, :], q3[0:96, 8 * s + j, :], start=True, stop=True)
                t = pe.done(last)
                state["scored"] = state.get("scored", 0) + 1
                if state["scored"] == 2:
                    r["q"].release(t)
                    r["k"].release(t)
                yield True
                t = dve.done(dve.after(t, d.free).tensor_scalar(d.ap, ps.ap, 50.0, -50.0, ALU.min, ALU.max))
                ps.release(t)
                t = act.done(act.after(t, t_att).activation(d.ap, d.ap, ACT.Exp, bias=l2_attb[:, b:b + 1], scale=l2_att[:, b:b + 1]))
                yield True
                av = yield from psum.take(1)
                v3 = split_cols(r["v"].ap, H2)
                for j in range(2):
                    for q in range(4):
                        last = pe.after(t, r["v_ready"], av.free).matmul(av.ap[32 * q:32 * q + 32, j * P:(j + 1) * P], v3[:, 8 * s + 4 * j + q, :],
                                                                d3[:, 4 * j + q, :], start=True, stop=True, tile_position=(0, 32 * q))
                t = pe.done(last)
                d.release(t)
                state["valued"] = state.get("valued", 0) + 1
                if state["valued"] == 2:
                    r["v"].release(t)
                if state["valued"] == 1:
                    state["attn"] = yield from at_ring.take()
                yield True
                while "attn" not in state:
                    yield False
                at = state["attn"]
                state["out", s] = yield from normalise(av, D, HD2, at.ap[:, s * D:(s + 1) * D], t, at.free, t_ring)

            def project_out(b, state):
                while ("out", 0) not in state or ("out", 1) not in state:
                    yield False
                at = state["attn"]
                po = yield from psum.take(1)
                for j in range(4):
                    last = pe.after(state["out", 0], state["out", 1], po.free).matmul(po.ap[:, 0:D], at.ap[:, j * P:(j + 1) * P], l2_wo[:, j, :],
                                                                                      start=(j == 0), stop=(j == 3))
                t = pe.done(last)
                at.release(t)
                yield True
                y = yield from y_ring.take()
                d, s = y.ap[:, 0:D], y.ap[:, D:D + 16]
                t = dve.done(dve.after(t, y.free).tensor_tensor(d, po.ap[:, 0:D], l2_bo, ALU.add))
                po.release(t)
                t = dve.done(dve.after(t).tensor_scalar(d, d, l2_rs, None, ALU.mult))
                t = dve.done(dve.after(t).bn_stats(s[:, 0:6], d))
                t = dve.done(dve.after(t).bn_aggr(s[:, 6:8], s[:, 0:6]))
                t = rstd(s[:, 8:9], s[:, 7:8], EPS_LN, 1.0, t)
                yield True
                t = dve.done(dve.after(t).tensor_scalar(d, d, s[:, 6:7], s[:, 8:9], ALU.subtract, ALU.mult))
                t = pool.done(pool.after(t).tensor_tensor(d, d, l2_gamma, ALU.mult))
                t = pool.done(pool.after(t).tensor_tensor(d, d, l2_beta, ALU.add))
                yield True
                t = dve.done(dve.after(t).scalar_tensor_tensor(X[b], d, gates[:, 2:3], X[b], ALU.mult, ALU.add))
                y.release(t)
                x_ready[b] = [t]
                finished.add(b)

            main = []
            for b in range(NB):
                state = {}
                main += [unit(b, s, state) for s in range(2)] + [project_out(b, state)]
            return [interleave([pair_prologue(i) for i in range(NB // PAIR)], 2),
                    interleave([tile_prologue(b) for b in range(NB)], 1), interleave(main, 5)]

        def l2_ffn(W, finished):
            ones, minus_round = W.f32(P), W.f32(1)
            wsum, wscale = W.f32(16), W.f32(16)
            t_one = dve.done(dve.api.memset(ones, 1.0))
            act.after(dve.done(dve.api.memset(minus_round, -ROUND)))
            t0 = dve.done(dve.api.memset(wsum, 0.0))
            raws = [(l2_raw[0], slice(0, P)), (l2_raw[1], slice(0, P)), (l2_raw[2][:, 0:NF2 - 1], slice(0, P)), (l2_raw[2][:, NF2 - 1], slice(0, F2 % P))]
            t_w = []

            def quantise(t):
                ps = yield from psum.take(1)
                t = pe.done(pe.after(t, t_one, ps.free).matmul(ps.ap[:, 0:4], ones, wsum[:, 0:4], start=True, stop=True))
                yield True
                t = dve.done(dve.after(t).tensor_scalar(wscale[:, 0:4], ps.ap[:, 0:4], 1.0 / (F2 * D), 1e-5, ALU.mult, ALU.max))
                ps.release(t)
                t_sc = dve.done(dve.after(t).reciprocal(wscale[:, 4:8], wscale[:, 0:4]))
                for n in range(3):
                    parts = [(l2_raw[n], l2_q[n])] if n < 2 else [(l2_raw[2][:, 0:NF2 - 1], l2_q[2][:, 0:NF2 - 1]), (l2_raw[2][0:F2 % P, NF2 - 1], l2_q[2][0:F2 % P, NF2 - 1])]
                    for w, q in parts:
                        rows = w.shape[0]
                        t = dve.done(dve.after(t_sc).tensor_scalar(w, w, wscale[0:rows, 4 + n:5 + n], ROUND, ALU.mult, ALU.add))
                        t = dve.done(dve.after(t).tensor_scalar(w, w, ROUND, -1.0, ALU.subtract, ALU.max))
                        t = dve.done(dve.after(t).tensor_scalar(q, w, 1.0, None, ALU.min))
                        t_w.append(t)
                        yield True
                for ring in (xn_ring, th_ring, h_ring, hq_ring, ht_ring):
                    for buf in ring.bufs:
                        buf.free = list(t_w)
                finished.add("weights")

            RAW = Arena(sbuf, l2_raw_at, l2_raw_at + l2_raw_cols)
            xn_ring = Ring([Buf(W.f32(D)), Buf(RAW.f32(D))])
            xq_ring = Ring([Buf(W.bf16(2 * D)) for _ in range(2)])
            s_ring = Ring([Buf(W.f32(16)) for _ in range(3)])
            th_ring = Ring([Buf(RAW.f32(F2)) for _ in range(2)])
            h_ring = Ring([Buf(RAW.f32(F2)) for _ in range(2)])
            hq_ring = Ring([Buf(RAW.bf16(NF2 * P)) for _ in range(2)])
            ht_ring = Ring([Buf(RAW.bf16(NF2 * P)) for _ in range(1)] + [Buf(W.bf16(NF2 * P)) for _ in range(1)])
            HF = F2 // 2

            def sum_weights():
                t = t0
                for n, (w, rows) in enumerate(raws):
                    flat = w[rows] if n == 3 else w[rows].rearrange("p k n -> p (k n)")
                    t = dve.done(dve.after(t, l2_lane.token()).tensor_reduce(wsum[rows, n:n + 1], flat, AXX, ALU.add, apply_absolute_value=True))
                    yield True
                t = dve.done(dve.after(t).tensor_tensor(wsum[:, 2:3], wsum[:, 2:3], wsum[:, 3:4], ALU.add))
                yield from quantise(t)

            def tile(b):
                while b not in finished or "weights" not in finished:
                    yield False
                xn = yield from xn_ring.take()
                s = yield from s_ring.take()
                c = lambda i: s.ap[:, i:i + 1]
                t = yield from layer_norm(X[b], xn.ap, x_ready[b], xn.free)
                yield True
                t = dve.done(dve.after(t, s.free).tensor_reduce(c(0), xn.ap, AXX, ALU.max, apply_absolute_value=True))
                t = dve.done(dve.after(t).tensor_scalar(c(0), c(0), 1e-5, None, ALU.max))
                t = dve.done(dve.after(t).reciprocal(c(1), c(0)))
                t = dve.done(dve.after(t).tensor_scalar(c(1), c(1), 127.0, None, ALU.mult))
                t = dve.done(dve.after(t).tensor_scalar(xn.ap, xn.ap, c(1), ROUND, ALU.mult, ALU.add))
                xq = yield from xq_ring.take()
                xqa, xT = xq.ap[:, 0:D], split_cols(xq.ap[:, D:2 * D], KD)
                t = act.done(act.after(t, xq.free).activation(xqa, xn.ap, ACT.Identity, bias=minus_round))
                xn.release(t)
                t_a = dve.done(dve.api.tensor_scalar(c(2), c(0), wscale[:, 0:1], 1.0 / 127.0, ALU.mult, ALU.mult))
                t_b = dve.done(dve.api.tensor_scalar(c(3), c(0), wscale[:, 1:2], 1.0 / 127.0, ALU.mult, ALU.mult))
                t_c = dve.done(dve.after(t_a).tensor_scalar(c(4), c(2), 0.5, None, ALU.mult))
                t_d = dve.done(dve.after(t_b, t_c).tensor_tensor(c(5), c(4), c(3), ALU.mult))
                yield True
                px = yield from psum.take(1)
                pb = px.ap.bitcast(BF16)[:, 0:D]
                t = transposes([(xqa[:, k * P:(k + 1) * P], pb[:, k * P:(k + 1) * P]) for k in range(KD)], px, ident_bf, t, px.free)
                t = act.done(act.after(t).activation(xT, split_cols(pb, KD), ACT.Copy))
                px.release(t)
                yield True
                pg = yield from psum.take(2)
                pu = yield from psum.take(2)
                for ps, w in ((pg, l2_q[0]), (pu, l2_q[1])):
                    for h in range(2):
                        for k in range(KD):
                            last = pe.after(t, t_w, ps.free).matmul(ps.ap[:, h * BANK:h * BANK + HF], xT[:, k], w[:, k, h * HF:(h + 1) * HF],
                                                                    start=(k == 0), stop=(k == KD - 1))
                t = pe.done(last)
                xq.release(t)
                yield True
                th = yield from th_ring.take()
                hb = yield from h_ring.take()
                g2, u2 = (split_cols(p.ap, 2)[:, :, 0:HF] for p in (pg, pu))
                th2, h2 = split_cols(th.ap, 2), split_cols(hb.ap, 2)
                t = act.done(act.after(t, t_c, th.free).activation(th2, g2, ACT.Tanh, scale=c(4)))
                t = dve.done(dve.after(t, hb.free).scalar_tensor_tensor(h2, th2, 1.0, g2, ALU.add, ALU.mult))
                th.release(t)
                pg.release(t)
                t = dve.done(dve.after(t).tensor_tensor(h2, h2, u2, ALU.mult))
                pu.release(t)
                t = dve.done(dve.after(t).tensor_reduce(c(6), hb.ap, AXX, ALU.max, apply_absolute_value=True))
                t = dve.done(dve.after(t, t_d).tensor_scalar(c(6), c(6), c(5), 1e-5, ALU.mult, ALU.max))
                t = dve.done(dve.after(t).reciprocal(c(7), c(6)))
                t = dve.done(dve.after(t).tensor_scalar(c(7), c(7), c(5), 127.0, ALU.mult, ALU.mult))
                t_o = dve.done(dve.api.tensor_scalar(c(8), c(6), wscale[:, 2:3], 1.0 / 127.0, ALU.mult, ALU.mult))
                t_o = dve.done(dve.after(t_o).tensor_scalar(c(8), c(8), gates[:, 6:7], None, ALU.mult))
                t = dve.done(dve.after(t).tensor_scalar(hb.ap, hb.ap, c(7), ROUND, ALU.mult, ALU.add))
                hq = yield from hq_ring.take()
                yield True
                t = act.done(act.after(t, hq.free).activation(hq.ap[:, 0:F2], hb.ap, ACT.Identity, bias=minus_round))
                hb.release(t)
                yield True
                pt = yield from psum.take(1)
                pb = pt.ap.bitcast(BF16)
                t = transposes([(hq.ap[:, f * P:min(F2, (f + 1) * P)], pb[0:min(P, F2 - f * P), f * P:(f + 1) * P]) for f in range(NF2)],
                               pt, ident_bf, t, pt.free)
                hq.release(t)
                ht = yield from ht_ring.take()
                full = (NF2 - 1) * P
                t1 = act.done(act.after(t, ht.free).activation(ht.ap[:, 0:full], pb[:, 0:full], ACT.Copy))
                t2 = act.done(act.api.activation(ht.ap[0:F2 - full, full:], pb[0:F2 - full, full:full + P], ACT.Copy))
                pt.release(t1, t2)
                yield True
                po = yield from psum.take(1)
                for f in range(NF2):
                    M = min(P, F2 - f * P)
                    last = pe.after(t1, t2, po.free).matmul(po.ap[:, 0:D], ht.ap[0:M, f * P:(f + 1) * P], l2_q[2][0:M, f, :],
                                                            start=(f == 0), stop=(f == NF2 - 1))
                t = pe.done(last)
                ht.release(t)
                yield True
                t = dve.done(dve.after(t, t_o).scalar_tensor_tensor(X[b], po.ap[:, 0:D], c(8), X[b], ALU.mult, ALU.add))
                po.release(t)
                s.release(t)
                x_ready[b] = [t]

            return [sum_weights(), interleave([tile(b) for b in range(NB)], 3)]

        def layer_2():
            load_l3_weights()
            W, finished = Arena(sbuf, WORK_AT, COLS), set()
            ffn = l2_ffn(W, finished)
            run(interleave(l2_attention(W, finished) + ffn, 5))

        R3 = Arena(sbuf, B_AT, WORK_AT)
        l3_wq = split_cols(R3.f32(KD * H3 * HD3), KD)
        l3_wk, l3_wv = (split_cols(R3.f32(KD * G3 * HD3), KD) for _ in range(2))
        l3_wo = split_cols(R3.f32(H3 * D), H3)
        l3_w = R3.f32(4)
        l3_lane = lane("l3_weights_loaded")
        x_slots = dram("l3_slot_inputs", [NSLOT, D], F32)
        y_slots = dram("l3_slot_outputs", [NSLOT + P, D], F32)
        slot_lane = lane("l3_slots_cleared")

        def load_l3_weights():
            load(l3_lane, l3_wq, chunks_of(A["l3_wq"]))
            load(l3_lane, l3_wk, chunks_of(A["l3_wk"]))
            load(l3_lane, l3_wv, chunks_of(A["l3_wv"]))
            load(l3_lane, l3_wo, chunks_of(A["l3_wo"], H3))
            load(l3_lane, l3_w[:, 0:2], A["l3_qkw"])

        def l3_attention(W, V, finished):
            pick = W.f32(32 * G3)
            t_one = dve.done(dve.api.memset(pick, 0.0))
            for g in range(G3):
                t_one = dve.done(dve.after(t_one).memset(pick[:, 33 * g:33 * g + 1], 1.0))
            t_w = dve.done(dve.after(l3_lane.token()).tensor_scalar(l3_w[:, 2:3], l3_w[:, 0:1], l3_w[:, 1:2], float(HD3) ** -0.5, ALU.mult, ALU.mult))
            PAIR = 2
            N = PAIR * S
            xn_ring = Ring([Buf(W.f32(PAIR * D)) for _ in range(1)])
            xt_ring = Ring([Buf(W.f32(KD * N)) for _ in range(2)])
            q_ring = Ring([Buf(V.f32(H3 * N)) for _ in range(2)] + [Buf(W.f32(H3 * N))])
            sq_ring = Ring([Buf(W.f32(2 * BANK)) for _ in range(2)])
            rq_ring = Ring([Buf(W.f32(PAIR * H3)) for _ in range(3)])
            kn_ring = Ring([Buf(V.f32(BANK + 8)) for _ in range(2)])
            kT_ring = Ring([Buf(V.f32(BANK)) for _ in range(3)])
            v_ring = Ring([Buf(V.f32(BANK)) for _ in range(3)])
            e_ring = Ring([Buf(W.f32(BANK)) for _ in range(4)])
            eT_ring = Ring([Buf(W.f32(BANK)) for _ in range(3)])
            m_ring = Ring([Buf(W.f32(8)) for _ in range(5)])
            o_ring = Ring([Buf(W.f32(H3 * P)) for _ in range(2)])
            sent, ready = {}, {}

            def queries(g, xT, t_x, q, q_free, pss, out):
                sq = yield from sq_ring.take()
                ps = yield from psum.take(2)
                for j in range(4):
                    for k in range(KD):
                        last = pe.after(t_x, l3_lane.token(), ps.free).matmul(ps.ap[:, j * N:(j + 1) * N], l3_wq[:, k, (4 * g + j) * P:(4 * g + j + 1) * P], xT[:, k, :],
                                                                             start=(k == 0), stop=(k == KD - 1))
                t = pe.done(last)
                yield True
                t_s = act.done(act.after(t, sq.free).activation(sq.ap, ps.ap, ACT.Square))
                t_q = dve.done(dve.after(t_s, q_free).tensor_copy(q[:, 4 * g * N:(4 * g + 4) * N], ps.ap))
                ps.release(t_q)
                yield True
                n = len(out)
                for j in range(4):
                    last = pe.after(t_s, t_one, pss.free).matmul(pss.ap[32 * j:32 * j + 32, 0:N], pick[:, 32 * g:32 * g + 32], sq.ap[:, j * N:(j + 1) * N],
                                                                 start=(n == 0), stop=(n == G3 - 1), tile_position=(0, 32 * j))
                t_ss = pe.done(last)
                sq.release(t_ss)
                out.append((t, t_q, t_ss))

            def pair_prologue(pair):
                xt = yield from xt_ring.take()
                xT = split_cols(xt.ap, KD)
                t_x = yield from norm_transpose(pair, xn_ring, xT, xt.free, PAIR)
                q = yield from q_ring.take()
                rq = yield from rq_ring.take()
                pss = yield from psum.take(1)
                out = []
                yield from interleave([queries(g, xT, t_x, q.ap, q.free, pss, out) for g in range(G3)], 2)
                xt.release([o[0] for o in out])
                sq = yield from sq_ring.take()
                ss = sq.ap[:, 0:N]
                t = act.done(act.after(out[-1][2], sq.free).activation(ss, pss.ap[:, 0:N], ACT.Copy))
                yield True
                t = transposes([(ss[:, i * P:(i + 1) * P], pss.ap[:, N + i * P:N + (i + 1) * P]) for i in range(PAIR)], pss, ident, t)
                sq.release(t)
                yield True
                for i in range(PAIR):
                    sums = pss.ap[:, N + i * P:N + (i + 1) * P].rearrange("p (j g) -> p g j", j=4)[:, 0:G3]
                    t_r = dve.done(dve.after(t, rq.free).tensor_scalar(rq.ap[:, i * H3:(i + 1) * H3].rearrange("p (g j) -> p g j", g=G3), sums, 1.0 / HD3, EPS_RMS, ALU.mult, ALU.add))
                t = t_r
                pss.release(t)
                t = pool.done(pool.after(t).tensor_tensor(rq.ap, rq.ap, half_neg.broadcast_to([P, PAIR * H3]), ALU.pow))
                sent[pair] = {"q": q, "rq": rq, "q_ready": [o[1] for o in out], "rq_ready": t, "units": 0, "exps": 0}
                yield True

            def tile_prologue(b):
                kn = yield from kn_ring.take()
                ps = yield from psum.take(1)
                for k in range(KD):
                    last = pe.after(l3_lane.token(), ps.free).matmul(ps.ap, ctxT[:, k, b * S:(b + 1) * S], l3_wk[:, k, :], start=(k == 0), stop=(k == KD - 1))
                t_k = pe.done(last)
                yield True
                n, ss = kn.ap[:, 0:BANK], kn.ap[:, BANK:BANK + 4]
                t = act.done(act.after(t_k, kn.free).activation(n, ps.ap, ACT.Square))
                t = dve.done(dve.after(t).tensor_reduce(ss, split_cols(n, G3), AXX, ALU.add))
                t = rstd(ss, ss, EPS_RMS, 1.0 / HD3, t)
                yield True
                t = dve.done(dve.after(t).tensor_tensor(split_cols(n, G3), split_cols(ps.ap, G3), ss.unsqueeze(2).broadcast_to([P, G3, HD3]), ALU.mult))
                ps.release(t)
                yield True
                kT = yield from kT_ring.take()
                pt = yield from psum.take(1)
                t = transposes([(n[:, g * P:(g + 1) * P], pt.ap[:, g * P:(g + 1) * P]) for g in range(G3)], pt, ident, t, pt.free)
                kn.release(t)
                yield True
                t = dve.done(dve.after(t, t_w, kT.free).tensor_scalar(kT.ap, pt.ap, l3_w[:, 2:3], None, ALU.mult))
                pt.release(t)
                v = yield from v_ring.take()
                pv = yield from psum.take(1)
                for k in range(KD):
                    last = pe.after(pv.free).matmul(pv.ap, ctxT[:, k, b * S:(b + 1) * S], l3_wv[:, k, :], start=(k == 0), stop=(k == KD - 1))
                t_m = pe.done(last)
                yield True
                t_v = act.done(act.after(t_m, v.free).activation(v.ap, pv.ap, ACT.Copy))
                pv.release(t_v)
                ready[b] = {"kT": kT, "kT_ready": t, "v": v, "v_ready": t_v}

            def unit(b, g, state):
                pair, i = divmod(b, PAIR)
                while b not in ready or pair not in sent:
                    yield False
                r, p = ready[b], sent[pair]
                q = split_cols(p["q"].ap, H3)
                m = yield from m_ring.take()
                e = yield from e_ring.take()
                ps = yield from psum.take(1)
                for j in range(4):
                    last = pe.after(p["q_ready"], r["kT_ready"], ps.free).matmul(
                        ps.ap[:, j * P:(j + 1) * P], q[:, 4 * g + j, i * P:(i + 1) * P], r["kT"].ap[:, g * P:(g + 1) * P], start=True, stop=True)
                t = pe.done(last)
                p["units"] += 1
                if p["units"] == PAIR * G3:
                    p["q"].release(t)
                state["scored"] = state.get("scored", 0) + 1
                if state["scored"] == G3:
                    r["kT"].release(t)
                yield True
                r4 = p["rq"].ap[:, i * H3 + 4 * g:i * H3 + 4 * g + 4]
                bias, rs = m.ap[:, 0:4], m.ap[:, 4:8]
                t = dve.done(dve.after(t, m.free).tensor_reduce(bias, split_cols(ps.ap, 4), AXX, ALU.max))
                t = dve.done(dve.after(t, p["rq_ready"]).scalar_tensor_tensor(bias, bias, -1.0, r4, ALU.mult, ALU.mult))
                for j in range(4):
                    t = act.done(act.after(t, e.free).activation(e.ap[:, j * P:(j + 1) * P], ps.ap[:, j * P:(j + 1) * P], ACT.Exp,
                                                                bias=bias[:, j:j + 1], scale=r4[:, j:j + 1], accum_out=rs[:, j:j + 1]))
                ps.release(t)
                p["exps"] += 1
                if p["exps"] == PAIR * G3:
                    p["rq"].release(t)
                yield True
                t = dve.done(dve.after(t).reciprocal(rs, rs))
                t = dve.done(dve.after(t).tensor_tensor(split_cols(e.ap, 4), split_cols(e.ap, 4), rs.unsqueeze(2).broadcast_to([P, 4, S]), ALU.mult))
                m.release(t)
                yield True
                eT = yield from eT_ring.take()
                pt = yield from psum.take(1)
                t = transposes([(e.ap[:, j * P:(j + 1) * P], pt.ap[:, j * P:(j + 1) * P]) for j in range(4)], pt, ident, t, pt.free)
                e.release(t)
                yield True
                t = act.done(act.after(t, eT.free).activation(eT.ap, pt.ap, ACT.Copy))
                pt.release(t)
                yield True
                po = yield from psum.take(1)
                t = pe.done(pe.after(t, r["v_ready"], po.free).matmul(po.ap, r["v"].ap[:, g * P:(g + 1) * P], eT.ap, start=True, stop=True))
                eT.release(t)
                state["valued"] = state.get("valued", 0) + 1
                if state["valued"] == G3:
                    r["v"].release(t)
                if state["valued"] == 1:
                    state["o"] = yield from o_ring.take()
                yield True
                while "o" not in state:
                    yield False
                o = state["o"]
                t = dve.done(dve.after(t, o.free).tensor_copy(o.ap[:, 4 * g * P:(4 * g + 4) * P], po.ap))
                po.release(t)
                state["out", g] = t

            def project_out(b, state):
                while any(("out", g) not in state for g in range(G3)):
                    yield False
                o = state["o"]
                po = yield from psum.take(1)
                for h in range(H3):
                    last = pe.after([state["out", g] for g in range(G3)], po.free).matmul(po.ap[:, 0:D], o.ap[:, h * P:(h + 1) * P], l3_wo[:, h, :],
                                                                                         start=(h == 0), stop=(h == H3 - 1))
                t = pe.done(last)
                o.release(t)
                yield True
                t = dve.done(dve.after(t).scalar_tensor_tensor(X[b], po.ap[:, 0:D], gates[:, 3:4], X[b], ALU.mult, ALU.add))
                po.release(t)
                x_ready[b] = [t]
                finished.add(b)

            main = []
            for b in range(NB):
                state = {}
                main += [unit(b, g, state) for g in range(G3)] + [project_out(b, state)]
            return [interleave([pair_prologue(i) for i in range(NB // PAIR)], 2),
                    interleave([tile_prologue(b) for b in range(NB)], 1), interleave(main, 5)]

        def l3_routing(W, V, finished):
            gate = split_cols(W.f32(KD * E3), KD)
            iota, base = W.f32(E3), W.f32(E3)
            before_f = W.f32(P)
            before, ones = W.bf16(P), W.bf16(P)
            zeros = W.f32(D)
            rl = lane("l3_router_weights_loaded")
            load(rl, gate, chunks_of(A["l3_gateT"]))
            load(rl, iota, A["iota"].broadcast_to([P, E3]))
            load(rl, base, A["slot_base"].broadcast_to([P, E3]))
            load(rl, before_f, A["before"])
            t_z = dve.done(dve.api.memset(zeros, 0.0))
            for i in range(NSLOT // 512):
                slot_lane.start(sp, x_slots[i * 512:(i + 1) * 512].rearrange("(p r) n -> p r n", p=P), zeros.unsqueeze(1).broadcast_to([P, 4, D]), t_z)
            slot_lane.start(sp, y_slots[NSLOT:NSLOT + P], zeros, t_z)
            t_bf = dve.done(dve.after(rl.token()).tensor_copy(before, before_f))
            t_on = dve.done(dve.api.memset(ones, 1.0))
            xn_ring = Ring([Buf(W.f32(D), lane(f"rows_scattered_{i}")) for i in range(2)])
            xt_ring = Ring([Buf(W.f32(D)) for _ in range(2)])
            r_ring = Ring([Buf(V.f32(4 * E3 + K3 * E3 + 26)) for _ in range(2)])
            keep_w = [W.f32(8) for _ in range(NB)]
            keep_s = [W.f32(2) for _ in range(NB)]
            keep_i = [W.f32(8).bitcast(U32) for _ in range(NB)]
            cum_f = V.f32(E3)
            sel_bf = [V.bf16(2 * E3) for _ in range(3)]
            sel_ring = Ring([Buf(a) for a in sel_bf])
            t_cum = dve.done(dve.api.memset(cum_f, 0.0))
            chain = {"cum": t_cum, "next": 0}
            t_slot = [None] * NB

            def route(b, xT, t_x, xn, t_xn):
                r = yield from r_ring.take()
                at = [0]

                def cut(n):
                    a = r.ap[:, at[0]:at[0] + n]
                    at[0] += n
                    return a
                prob, pick, keep_, slot = cut(E3), cut(E3), cut(E3), cut(E3)
                one = split_cols(cut(K3 * E3), K3)
                idx = cut(8)
                idx_u = cut(8).bitcast(U32)
                mx, sm, s6 = cut(1), cut(1), cut(8)
                top = keep_w[b]
                ps = yield from psum.take(1)
                for k in range(KD):
                    last = pe.after(t_x, rl.token(), ps.free).matmul(ps.ap[:, 0:E3], xT[:, k], gate[:, k, :], start=(k == 0), stop=(k == KD - 1))
                t = pe.done(last)
                yield True
                t_logits = t
                t = dve.done(dve.after(t, r.free).tensor_reduce(mx, ps.ap[:, 0:E3], AXX, ALU.max, negate=True))
                t = act.done(act.after(t).activation(prob, ps.ap[:, 0:E3], ACT.Exp, bias=mx, accum_out=sm))
                ps.release(t)
                yield True
                t = dve.done(dve.after(t).reciprocal(sm, sm))
                t = dve.done(dve.after(t).tensor_scalar(prob, prob, sm, None, ALU.mult))
                t = dve.done(dve.after(t).max(top, prob))
                t = dve.done(dve.after(t).max_index(idx_u, top, prob))
                t = dve.done(dve.after(t).tensor_copy(idx, idx_u))
                t = dve.done(dve.after(t).tensor_tensor(one, iota.unsqueeze(1).broadcast_to([P, K3, E3]),
                                                       idx[:, 0:K3].unsqueeze(2).broadcast_to([P, K3, E3]), ALU.is_equal))
                t_p = dve.done(dve.after(t).tensor_reduce(pick, one.rearrange("p k e -> p e k"), AXX, ALU.add))
                while chain["next"] != b:
                    yield False
                sb = yield from sel_ring.take()
                chain["next"] = b + 1
                t1 = dve.done(dve.after(t_p, sb.free).tensor_copy(sb.ap[:, 0:E3], pick))
                t2 = dve.done(dve.after(chain["cum"]).tensor_copy(sb.ap[:, E3:2 * E3], cum_f))
                chain["cum"] = dve.done(dve.after(t2).tensor_tensor(cum_f, cum_f, pick, ALU.add))
                yield True
                pp = yield from psum.take(1)
                pe.after(t1, t2, t_bf, t_on, pp.free).matmul(pp.ap[:, 0:E3], before, sb.ap[:, 0:E3], start=True, stop=False)
                t = pe.done(pe.api.matmul(pp.ap[:, 0:E3], ones, sb.ap[:, E3:2 * E3], start=False, stop=True))
                sb.release(t)
                yield True
                t1 = dve.done(dve.after(t).tensor_scalar(keep_, pp.ap[:, 0:E3], float(CAP3), None, ALU.is_lt))
                t2 = dve.done(dve.api.tensor_tensor(slot, pp.ap[:, 0:E3], base, ALU.add))
                pp.release(t1, t2)
                t = dve.done(dve.after(t1, t2).tensor_tensor(slot, slot, keep_, ALU.mult))
                t = dve.done(dve.after(t).tensor_tensor(one, one, slot.unsqueeze(1).broadcast_to([P, K3, E3]), ALU.mult))
                t = dve.done(dve.after(t).tensor_reduce(s6[:, 0:K3], one, AXX, ALU.add))
                t = dve.done(dve.after(t).tensor_scalar(keep_i[b][:, 0:K3], s6[:, 0:K3], float(NSLOT), None, ALU.add))
                r.release(t)
                t_slot[b] = t
                for k in range(K3):
                    pool.after(t, t_xn, slot_lane.token()).indirect_dma_start(
                        out=x_slots[:, :], out_offset=bass.IndirectOffsetOnAxis(ap=keep_i[b][:, k:k + 1], axis=0),
                        in_=xn.ap, in_offset=None, bounds_check=NSLOT - 1, oob_is_err=False).then_inc(xn.lane.sem, 16)
                    xn.lane.count += 16
                xn.release(xn.lane.token())
                return t_logits

            def tile(b):
                while b not in finished:
                    yield False
                xn = yield from xn_ring.take()
                t_xn = yield from layer_norm(X[b], xn.ap, x_ready[b], xn.free, keep_s[b])
                xt = yield from xt_ring.take()
                ps = yield from psum.take(1)
                t = transposes([(xn.ap[:, k * P:(k + 1) * P], ps.ap[:, k * P:(k + 1) * P]) for k in range(KD)], ps, ident, t_xn, ps.free)
                xT = split_cols(xt.ap, KD)
                t_x = act.done(act.after(t, xt.free).activation(xt.ap, ps.ap[:, 0:D], ACT.Copy))
                ps.release(t_x)
                yield True
                xt.release((yield from route(b, xT, t_x, xn, [t_xn, t])))

            return [interleave([tile(b) for b in range(NB)], 3)], [buf.lane for buf in xn_ring.bufs], keep_s, keep_w, keep_i, t_slot

        def l3_weights(W, finished):
            w_ring = Ring([Buf((W.f32(2 * KD * 2 * I3).rearrange("p (e k n) -> p e k n", e=2, k=KD), split_cols(W.f32(2 * D, I3), 2)),
                               lane(f"expert_weights_loaded_{i}")) for i in range(20)])
            weights = {}

            def load_weights(n):
                w = yield from w_ring.take()
                w.lane.start(sp, w.ap[0], A["l3_gu_pairs"][n], *w.free)
                weights[n] = (w, w.lane.start(sp, w.ap[1], A["l3_down_pairs"][n], *w.free))

            def prefetch():
                while len(finished) < NB:
                    yield False
                for buf in w_ring.bufs:
                    buf.free = [pe.last(), dve.last(), act.last(), pool.last()]
                for n in range(len(w_ring.bufs)):
                    yield from load_weights(n)
            return w_ring, weights, load_weights, prefetch

        def l3_experts(W, w_ring, weights, load_weights, routed_lanes, keep_s, keep_w, keep_i, t_slot):
            all_in = [l.token() for l in routed_lanes] + [slot_lane.token()]
            sgu = split_cols(W.f32(KD * 2 * SI3), KD)
            sd = split_cols(W.f32(2 * D), 2)
            sl = lane("shared_expert_weights_loaded")
            sxn_ring, sxt_ring, shT_ring = (Ring([Buf(W.f32(D)) for _ in range(2)]) for _ in range(3))
            sh_ring = Ring([Buf(W.f32(SI3)) for _ in range(2)])
            shared_done = set()

            def shared(b):
                s = keep_s[b]
                xn = yield from sxn_ring.take()
                t_x = dve.done(dve.after(x_ready[b], xn.free).tensor_scalar(xn.ap, X[b], s[:, 0:1], s[:, 1:2], ALU.subtract, ALU.mult))
                yield True
                xt = yield from sxt_ring.take()
                ps = yield from psum.take(1)
                t = transposes([(xn.ap[:, k * P:(k + 1) * P], ps.ap[:, k * P:(k + 1) * P]) for k in range(KD)], ps, ident, t_x, ps.free)
                xn.release(t)
                yield True
                xT = split_cols(xt.ap, KD)
                t_x = act.done(act.after(t, xt.free).activation(xt.ap, ps.ap[:, 0:D], ACT.Copy))
                ps.release(t_x)
                yield True
                ps = yield from psum.take(1)
                for k in range(KD):
                    last = pe.after(t_x, sl.token(), ps.free).matmul(ps.ap[:, 0:2 * SI3], xT[:, k], sgu[:, k, :], start=(k == 0), stop=(k == KD - 1))
                t_m = pe.done(last)
                xt.release(t_m)
                yield True
                sh = yield from sh_ring.take()
                h = sh.ap[:, 0:SI3]
                t = act.done(act.after(t_m, sh.free).activation(h, ps.ap[:, 0:SI3], ACT.Tanh, scale=0.5))
                t = dve.done(dve.after(t).scalar_tensor_tensor(h, h, 1.0, ps.ap[:, 0:SI3], ALU.add, ALU.mult))
                t = dve.done(dve.after(t).scalar_tensor_tensor(h, h, 0.5, ps.ap[:, SI3:2 * SI3], ALU.mult, ALU.mult))
                ps.release(t)
                yield True
                pt = yield from psum.take(1)
                t = transposes([(h[:, 0:P], pt.ap[:, 0:P]), (h[:, P:SI3], pt.ap[0:SI3 - P, P:2 * P])], pt, ident, t, pt.free)
                sh.release(t)
                hT = yield from shT_ring.take()
                t1 = act.done(act.after(t, hT.free).activation(hT.ap[:, 0:P], pt.ap[:, 0:P], ACT.Copy))
                t2 = act.done(act.api.activation(hT.ap[0:SI3 - P, P:2 * P], pt.ap[0:SI3 - P, P:2 * P], ACT.Copy))
                pt.release(t1, t2)
                yield True
                po = yield from psum.take(1)
                pe.after(t1, t2, po.free).matmul(po.ap[:, 0:D], hT.ap[:, 0:P], sd[:, 0], start=True, stop=False)
                t = pe.done(pe.api.matmul(po.ap[:, 0:D], hT.ap[0:SI3 - P, P:2 * P], sd[0:SI3 - P, 1], start=False, stop=True))
                hT.release(t)
                yield True
                t = dve.done(dve.after(t, x_ready[b]).scalar_tensor_tensor(X[b], po.ap[:, 0:D], gates[:, 7:8], X[b], ALU.mult, ALU.add))
                po.release(t)
                x_ready[b] = [t]
                shared_done.add(b)

            xe_ring = Ring([Buf(W.f32(D), lane(f"slot_rows_loaded_{i}")) for i in range(6)])
            xeT_ring = Ring([Buf(W.f32(D)) for _ in range(4)])
            he_ring = Ring([Buf(W.f32(2 * I3)) for _ in range(4)])
            heT_ring = Ring([Buf(W.f32(P, I3)) for _ in range(4)])
            ye_ring = Ring([Buf(W.f32(D), lane(f"slot_outputs_stored_{i}")) for i in range(6)])

            def pair(n):
                while n not in weights:
                    yield False
                w, t_w = weights[n]
                xe = yield from xe_ring.take()
                t = xe.lane.start(act, xe.ap, x_slots[n * P:(n + 1) * P], xe.free, all_in)
                yield True
                ps = yield from psum.take(1)
                t = transposes([(xe.ap[:, k * P:(k + 1) * P], ps.ap[:, k * P:(k + 1) * P]) for k in range(KD)], ps, ident, t, ps.free)
                xe.release(t)
                xT = yield from xeT_ring.take()
                xT3 = split_cols(xT.ap, KD)
                t = act.done(act.after(t, xT.free).activation(xT.ap, ps.ap[:, 0:D], ACT.Copy))
                ps.release(t)
                yield True
                pg = yield from psum.take(1)
                for k in range(KD):
                    for i in range(2):
                        last = pe.after(t, t_w, pg.free).matmul(pg.ap[64 * i:64 * i + 64, 0:2 * I3], xT3[:, k, 64 * i:64 * i + 64], w.ap[0][:, i, k, :],
                                                                start=(k == 0), stop=(k == KD - 1), tile_position=(0, 64 * i))
                t = pe.done(last)
                xT.release(t)
                yield True
                h = yield from he_ring.take()
                th, hh = h.ap[:, 0:I3], h.ap[:, I3:2 * I3]
                t = act.done(act.after(t, h.free).activation(th, pg.ap[:, 0:I3], ACT.Tanh, scale=0.5))
                t = dve.done(dve.after(t).scalar_tensor_tensor(th, th, 1.0, pg.ap[:, 0:I3], ALU.add, ALU.mult))
                t = dve.done(dve.after(t).scalar_tensor_tensor(hh, th, 0.5, pg.ap[:, I3:2 * I3], ALU.mult, ALU.mult))
                pg.release(t)
                yield True
                pt = yield from psum.take(1)
                t = transposes([(hh, pt.ap[0:I3, 0:P])], pt, ident, t, pt.free)
                h.release(t)
                hT = yield from heT_ring.take()
                t = dve.done(dve.after(t, hT.free).tensor_copy(hT.ap, pt.ap[0:I3, 0:P]))
                pt.release(t)
                yield True
                po = yield from psum.take(1)
                for i in range(2):
                    last = pe.after(t, po.free).matmul(po.ap[64 * i:64 * i + 64, 0:D], hT.ap[:, 64 * i:64 * i + 64], w.ap[1][:, i, :],
                                                       start=True, stop=True, tile_position=(0, 64 * i))
                t = pe.done(last)
                w.release(t)
                hT.release(t)
                yield True
                y = yield from ye_ring.take()
                t = act.done(act.after(t, y.free).activation(y.ap, po.ap[:, 0:D], ACT.Copy))
                po.release(t)
                y.release(y.lane.start(sp, y_slots[n * P:(n + 1) * P], y.ap, t))

            run(interleave([interleave([load_weights(n) for n in range(len(w_ring.bufs), E3 // 2)], 1), interleave([pair(n) for n in range(E3 // 2)], 6)], 2))
            all_out = [buf.lane.token() for buf in ye_ring.bufs] + [slot_lane.token()]

            g_ring = Ring([Buf(W.f32(K3 * D), lane(f"rows_gathered_{i}")) for i in range(3)])

            def combine(b):
                while b not in shared_done:
                    yield False
                g = yield from g_ring.take()
                g3 = split_cols(g.ap, K3)
                for k in range(K3):
                    pool.after(g.free, all_out, t_slot[b]).indirect_dma_start(
                        out=g3[:, k], out_offset=None, in_=y_slots[:, :],
                        in_offset=bass.IndirectOffsetOnAxis(ap=keep_i[b][:, k:k + 1], axis=0)).then_inc(g.lane.sem, 16)
                    g.lane.count += 16
                yield True
                t = dve.done(dve.after(g.lane.token()).tensor_scalar(g3[:, 0], g3[:, 0], keep_w[b][:, 0:1], None, ALU.mult))
                for k in range(1, K3):
                    t = dve.done(dve.after(t).scalar_tensor_tensor(g3[:, 0], g3[:, k], keep_w[b][:, k:k + 1], g3[:, 0], ALU.mult, ALU.add))
                t = dve.done(dve.after(t, x_ready[b]).scalar_tensor_tensor(X[b], g3[:, 0], gates[:, 7:8], X[b], ALU.mult, ALU.add))
                g.release(t)
                out_lane.start(sp, out[b], X[b], t)

            load(sl, sgu, chunks_of(A["l3_sguT"]))
            load(sl, sd[:, 0], A["l3_sdT"][0:P])
            load(sl, sd[0:SI3 - P, 1], A["l3_sdT"][P:SI3])
            run(interleave([interleave([shared(b) for b in range(NB)], 2), interleave([combine(b) for b in range(NB)], 4)], 2))

        def layer_3():
            W, V, finished = Arena(sbuf, WORK_AT, COLS), Arena(sbuf, A_AT, B_AT), set()
            streams = l3_attention(W, V, finished)
            attention_end = W.at
            routing, routed_lanes, keep_s, keep_w, keep_i, t_slot = l3_routing(W, V, finished)
            w_ring, weights, load_weights, prefetch = l3_weights(Arena(sbuf, B_AT, attention_end), finished)
            run(interleave(streams + routing + [prefetch()], 5))
            barrier(but=[buf.lane for buf in w_ring.bufs])
            l3_experts(Arena(sbuf, A_AT, B_AT), w_ring, weights, load_weights, routed_lanes, keep_s, keep_w, keep_i, t_slot)

        out_lane = lane("out_stored")
        stages = [l0_attention, l0_ffn, l1_attention, l1_ffn, layer_2, layer_3]
        for stage in stages:
            stage()
            if stage is not layer_3:
                barrier()
        sp.after([l.token() for l in lanes if l.count])


def constants():
    c = {"ident": np.eye(P, dtype=np.float32)}
    inv = (1.0 / np.float32(10000.0) ** (np.arange(0, HD0, 2, dtype=np.float32) / np.float32(HD0))).astype(np.float32)

    def tables(n):
        f = (np.arange(n, dtype=np.float32)[None, :] * inv[:, None]).astype(np.float32)
        return np.cos(f), np.sin(f)
    cos, sin = tables(T0)
    scale = np.float32(1.0 / np.sqrt(HD0))
    cos8 = np.concatenate([cos, cos])
    sin8 = np.concatenate([-sin, sin])
    c["l0_cosq"] = (np.repeat(cos8, H0, 0) * scale).astype(np.float32)
    c["l0_sinq"] = (np.repeat(sin8, H0, 0) * scale).astype(np.float32)
    c["l0_cosk"] = np.repeat(cos8, G0, 0).astype(np.float32)
    c["l0_sink"] = np.repeat(sin8, G0, 0).astype(np.float32)
    sel = np.zeros((3, 32, NF0 * P), np.float32)
    for f in range(HID0):
        sel[:, min(f // F0, E0), f] = 1.0
    c["l0_sel"] = sel.reshape(96, NF0 * P)
    cos, sin = tables(S)
    c["l1_cos"] = np.repeat(cos, H1, 0).astype(np.float32)
    c["l1_sin"] = np.repeat(sin, H1, 0).astype(np.float32)
    c["l1_cosq"], c["l1_sinq"] = c["l1_cos"] * scale, c["l1_sin"] * scale
    c["iota"] = np.arange(E3, dtype=np.float32).reshape(1, E3)
    c["slot_base"] = (np.arange(E3, dtype=np.float32) * CAP3 - NSLOT).reshape(1, E3)
    c["before"] = np.triu(np.ones((P, P), np.float32), 1)
    return c


def layout(i):
    a = {n: i[n] for n in ("x", "ctx_2048", "g_xattn", "g_ffn")}
    half = [(d + HD0 // 2) % HD0 for d in range(HD0)]

    def head_minor(w, heads, hd):
        return w.reshape(heads, hd, -1).transpose(1, 0, 2)
    wq, bq = head_minor(i["L0_xattn_Wq"], H0, HD0), head_minor(i["L0_xattn_bq"], H0, HD0)
    wk, bk = head_minor(i["L0_xattn_Wk"], G0, HD0), head_minor(i["L0_xattn_bk"], G0, HD0)
    a["l0_wqT"], a["l0_wqpT"] = wq.reshape(P, P).T, wq[half].reshape(P, P).T
    a["l0_wkT"], a["l0_wkpT"] = wk.reshape(32, P).T, wk[half].reshape(32, P).T
    a["l0_bq2"] = np.stack([bq.reshape(P), bq[half].reshape(P)], 1)
    a["l0_bk2"] = np.stack([bk.reshape(32), bk[half].reshape(32)], 1)
    a["l0_wvT"] = i["L0_xattn_Wv"].T
    a["l0_bv"] = i["L0_xattn_bv"].reshape(1, 32)
    a["l0_bo"] = i["L0_xattn_bo"].reshape(P, 1)
    a["l0_woT"] = i["L0_xattn_Wo"].T
    e0 = E0 * F0
    a["l0_gateT"] = np.concatenate([i["L0_ffn_gate_w"], i["L0_ffn_shared_gate_w"]]).T
    a["l0_fc1T"] = np.concatenate([i["L0_ffn_expert_fc1"].reshape(e0, D), i["L0_ffn_shared_fc1"]]).T
    a["l0_fc2T"] = np.concatenate([i["L0_ffn_expert_fc2"].reshape(e0, D), i["L0_ffn_shared_fc2"]]).T
    a["l0_projT"] = np.concatenate([i["L0_ffn_expert_proj"].transpose(0, 2, 1).reshape(e0, D), i["L0_ffn_shared_proj"].T])

    def columns_head_minor(w, heads, hd):
        return w.reshape(-1, heads, hd).transpose(0, 2, 1).reshape(-1, heads * hd)
    a["mask1"] = i["mask_Bx1xSxS_fk0"].reshape(NB, S, S)
    a["l1_wq"] = columns_head_minor(i["L1_xattn_Wq"], H1, HD1)
    a["l1_wk"] = columns_head_minor(i["L1_xattn_Wk"], H1, HD1)
    a["l1_wv"], a["l1_wo"] = i["L1_xattn_Wv"], i["L1_xattn_Wo"]
    a["l1_gate"] = i["L1_xattn_gate"].reshape(1, H1)
    a["l1_gu"], a["l1_down"] = i["L1_ffn_gate_up_proj"], i["L1_ffn_down_proj"]
    a["mask2T"] = i["mask_BxS2_ik0"].T
    a["l2_wqT"] = columns_head_minor(i["L2_xattn_Wq"].T, H2, HD2)
    a["l2_wkT"] = columns_head_minor(i["L2_xattn_Wk"].T, H2, HD2)
    a["l2_wvT"], a["l2_woT"] = i["L2_xattn_Wv"].T, i["L2_xattn_Wo"].T
    for n in ("bq", "bk"):
        a["l2_" + n] = columns_head_minor(i["L2_xattn_" + n], H2, HD2).reshape(KD, P).T
    a["l2_rows"] = np.stack([i["L2_xattn_" + n] for n in ("bv", "bo", "ln_gamma", "ln_beta")])
    a["l2_rs"] = i["L2_xattn_residual_scale"].reshape(1, 1)
    a["l2_wgT"], a["l2_wuT"], a["l2_wdT"] = i["L2_ffn_w_gate"].T, i["L2_ffn_w_up"].T, i["L2_ffn_w_down"].T
    for n in ("Wq", "Wk", "Wv", "Wo"):
        a["l3_" + n.lower()] = i["L3_xattn_" + n]
    a["l3_qkw"] = np.stack([i["L3_xattn_q_norm_w"], i["L3_xattn_k_norm_w"]], 1)
    a["l3_gateT"] = i["L3_ffn_gate_w"].T
    a["l3_gu_pairs"] = i["L3_ffn_gate_up_proj"].reshape(E3 // 2, 2, KD, P, 2 * I3).transpose(0, 3, 1, 2, 4)
    a["l3_down_pairs"] = i["L3_ffn_down_proj"].reshape(E3 // 2, 2, I3, D).transpose(0, 2, 1, 3)
    a["l3_sguT"] = np.concatenate([i["L3_ffn_shared_gate_w"], i["L3_ffn_shared_up_w"]]).T
    a["l3_sdT"] = i["L3_ffn_shared_down_w"].T
    return a


def kernel(**inputs):
    import concourse.bacc as _bacc
    from concourse.bass_utils import run_bass_kernel_spmd as _run

    nc = _bacc.Bacc("TRN2", target_bir_lowering=False, num_devices=1)
    arrays, aps = {}, {}
    host = {**layout({k: np.asarray(v) for k, v in inputs.items()}), **constants()}
    for name, a in host.items():
        a = np.ascontiguousarray(a)
        arrays[f"in_{name}"] = a
        aps[name] = nc.dram_tensor(f"in_{name}", a.shape, mybir.dt.from_np(a.dtype), kind="ExternalInput").ap()
    out = nc.dram_tensor("out_x", (NB, S, D), F32, kind="ExternalOutput").ap()
    program(nc, aps, out)
    return _run(nc, [arrays], core_ids=[0]).results[0]["out_x"]
```
